# Optimizing a Trainium2 kernel written in Bass

```python
import numpy as np
import jax
import jax.numpy as jnp

def _softmax(x, axis=-1):
    return jax.nn.softmax(x, axis=axis)

def _gelu(x):
    return jax.nn.gelu(x, approximate=True)

def _silu(x):
    return jax.nn.silu(x)

def _sigmoid(x):
    return jax.nn.sigmoid(x)

def _layernorm(x, axis=-1, eps=1e-05):
    m = jnp.mean(x, axis=axis, keepdims=True)
    v = jnp.var(x, axis=axis, keepdims=True)
    return (x - m) / jnp.sqrt(v + eps)

def _scatter_add(tgt, idx, src, axis=0):
    return tgt.at[idx].add(src)

def _segment_sum(src, seg, n):
    return jax.ops.segment_sum(src, seg, n)
kernel_name = 'mk_lm_tower_d1_tok_ids768_r4_bd8a55'

def setup_inputs(seed: int=0):
    np.random.seed(seed)
    _w = jnp.asarray

    def _rec_inputs():
        import jax
        import jax.numpy as jnp
        _rk = jax.random.key(seed)
        x = jax.random.randint(jax.random.fold_in(_rk, 1), (16, 128), 0, 31999, jnp.int32)
        itok_BS_0_15 = jax.random.randint(jax.random.fold_in(_rk, 21), (16, 128), 0, 16, jnp.int32)
        itok_BS_0_3 = jax.random.randint(jax.random.fold_in(_rk, 22), (16, 128), 0, 4, jnp.int32)
        itok_BS_0_9999 = jax.random.randint(jax.random.fold_in(_rk, 23), (16, 128), 0, 2500, jnp.int32)
        itok_BS_0_2047 = jax.random.randint(jax.random.fold_in(_rk, 24), (16, 128), 0, 512, jnp.int32)
        fside_BS_age_tau = 49.5725 + 28.8366 * jax.random.normal(jax.random.fold_in(_rk, 25), (16, 128), jnp.float32)
        fside_BS_delays_tau = 49.8282 + 28.8637 * jax.random.normal(jax.random.fold_in(_rk, 26), (16, 128), jnp.float32)
        return (x, itok_BS_0_15, itok_BS_0_3, itok_BS_0_9999, itok_BS_0_2047, fside_BS_age_tau, fside_BS_delays_tau)
    x, itok_BS_0_15, itok_BS_0_3, itok_BS_0_9999, itok_BS_0_2047, fside_BS_age_tau, fside_BS_delays_tau = _rec_inputs()

    def _L0_tok_setup():
        import jax, jax.numpy as jnp
        import numpy as np
        B, S, H = (8, 512, 192)
        VOCAB, MODAL_V, SEG_V, NPI_V, MAX_POS = (8000, 16, 4, 2500, 512)
        LN_EPS = 1e-12

        def _sinusoidal_table(max_pos, hidden):
            pos = np.arange(max_pos, dtype=np.float32)[:, None]
            idx = np.arange(hidden, dtype=np.float32)[None, :]
            angle = pos / np.power(10000.0, 2.0 * idx / hidden)
            tab = np.where(np.arange(hidden)[None, :] % 2 == 0, np.sin(angle), np.cos(angle))
            return jnp.asarray(tab, dtype=jnp.float32)

        def _time2vec(tau, w, b, w0, b0):
            t = tau[..., None]
            v1 = jnp.sin(t * w[0] + b)
            v2 = t * w0[0] + b0
            return jnp.concatenate([v1, v2], axis=-1)

        def _layer_norm(x, gamma, beta, eps):
            mu = jnp.mean(x, axis=-1, keepdims=True)
            var = jnp.mean(jnp.square(x - mu), axis=-1, keepdims=True)
            return (x - mu) * jax.lax.rsqrt(var + eps) * gamma + beta
        key = jax.random.key(seed)
        ks = jax.random.split(key, 16)
        inp = {'word_ids': jax.random.randint(ks[0], (B, S), 0, VOCAB), 'modalities_ids': jax.random.randint(ks[1], (B, S), 0, MODAL_V), 'seg_ids': jax.random.randint(ks[2], (B, S), 0, SEG_V), 'npi_ids': jax.random.randint(ks[3], (B, S), 0, NPI_V), 'posi_ids': jnp.sort(jax.random.randint(ks[4], (B, S), 0, MAX_POS), axis=-1), 'age_tau': jax.random.uniform(ks[5], (B, S), dtype=jnp.float32) * 100.0, 'delays_tau': jax.random.uniform(ks[6], (B, S), dtype=jnp.float32) * 100.0, 'word_table': jax.random.normal(ks[7], (VOCAB, H), dtype=jnp.float32) * 0.02, 'modalities_table': jax.random.normal(ks[8], (MODAL_V, H), dtype=jnp.float32) * 0.02, 'seg_table': jax.random.normal(ks[9], (SEG_V, H), dtype=jnp.float32) * 0.02, 'npi_table': jax.random.normal(ks[10], (NPI_V, H), dtype=jnp.float32) * 0.02, 'posi_table': _sinusoidal_table(MAX_POS, H), 'age_w': jax.random.normal(ks[11], (1, H - 1), dtype=jnp.float32), 'age_b': jax.random.normal(ks[12], (H - 1,), dtype=jnp.float32), 'age_w0': jax.random.normal(ks[13], (1, 1), dtype=jnp.float32), 'age_b0': jax.random.normal(ks[14], (1,), dtype=jnp.float32), 'delay_w': jax.random.normal(ks[15], (1, H - 1), dtype=jnp.float32), 'delay_b': jax.random.normal(jax.random.fold_in(key, 100), (H - 1,), dtype=jnp.float32), 'delay_w0': jax.random.normal(jax.random.fold_in(key, 101), (1, 1), dtype=jnp.float32), 'delay_b0': jax.random.normal(jax.random.fold_in(key, 102), (1,), dtype=jnp.float32), 'ln_gamma': jnp.ones((H,), dtype=jnp.float32), 'ln_beta': jnp.zeros((H,), dtype=jnp.float32)}
        return inp
    _L0_tok_all = _L0_tok_setup()
    _L0_tok_in = {k: v for k, v in _L0_tok_all.items() if k in ('word_table', 'modalities_table', 'seg_table', 'npi_table', 'posi_table', 'age_w', 'age_b', 'age_w0', 'age_b0', 'delay_w', 'delay_b', 'delay_w0', 'delay_b0', 'ln_gamma', 'ln_beta')}
    del _L0_tok_all

    def _L0_attn_setup():
        import jax, jax.numpy as jnp
        import numpy as np
        import math
        DIM = 192
        NUM_HEADS = 12
        HEAD_DIM = DIM // NUM_HEADS
        EPS = 1e-06

        def rms_norm(x, w):
            xf = x.astype(jnp.float32)
            var = jnp.mean(xf * xf, axis=-1, keepdims=True)
            return (xf * jax.lax.rsqrt(var + EPS) * w).astype(x.dtype)
        key = jax.random.key(seed)
        ks = jax.random.split(key, 6)
        B, N, C = (4, 512, DIM)
        return {'x': jax.random.normal(ks[0], (B, N, C), dtype=jnp.float32), 'qkv_w': jax.random.normal(ks[1], (3 * C, C), dtype=jnp.float32) * C ** (-0.5), 'qkv_b': jax.random.normal(ks[2], (3 * C,), dtype=jnp.float32) * 0.02, 'proj_w': jax.random.normal(ks[3], (C, C), dtype=jnp.float32) * C ** (-0.5), 'proj_b': jax.random.normal(ks[4], (C,), dtype=jnp.float32) * 0.02, 'q_norm_w': jnp.ones((HEAD_DIM,), dtype=jnp.float32), 'k_norm_w': jnp.ones((HEAD_DIM,), dtype=jnp.float32)}
    _L0_attn_all = _L0_attn_setup()
    _L0_attn_in = {k: v for k, v in _L0_attn_all.items() if k in ('qkv_w', 'qkv_b', 'proj_w', 'proj_b', 'q_norm_w', 'k_norm_w')}
    del _L0_attn_all

    def _L0_ffn_setup():
        import jax, jax.numpy as jnp
        import numpy as np
        B, S, D, F, E = (8, 512, 192, 768, 16)
        CAP = 64
        EPS = 1e-06

        def _switch_moe_block(x, ln_w, w_router, wi, wo):
            var = jnp.mean(jnp.square(x.astype(jnp.float32)), axis=-1, keepdims=True)
            normed = (x * jax.lax.rsqrt(var + EPS)).astype(x.dtype) * ln_w
            logits = jnp.einsum('bsd,de->bse', normed.astype(jnp.float32), w_router.astype(jnp.float32))
            probs = jax.nn.softmax(logits, axis=-1)
            expert_idx = jnp.argmax(probs, axis=-1)
            onehot = jax.nn.one_hot(expert_idx, E, dtype=jnp.float32)
            priority = jnp.cumsum(onehot, axis=1)
            keep = onehot * (priority <= CAP)
            pos = (priority - 1.0).astype(jnp.int32)
            dispatch = keep[..., None] * jax.nn.one_hot(pos, CAP, dtype=jnp.float32)
            expert_in = jnp.einsum('bsec,bsd->becd', dispatch, normed)
            h = jax.nn.relu(jnp.einsum('becd,edf->becf', expert_in, wi))
            expert_out = jnp.einsum('becf,efd->becd', h, wo)
            combined = jnp.einsum('bsec,becd->bsd', dispatch, expert_out)
            routed = jnp.sum(dispatch, axis=(2, 3)) > 0
            next_states = jnp.where(routed[..., None], combined.astype(x.dtype), normed)
            router_prob = jnp.max(probs, axis=-1, keepdims=True).astype(x.dtype)
            return x + router_prob * next_states
        key = jax.random.key(seed)
        k_x, k_r, k_wi, k_wo = jax.random.split(key, 4)
        x = jax.random.normal(k_x, (B, S, D), dtype=jnp.float32)
        ln_w = jnp.ones((D,), dtype=jnp.float32)
        w_router = jax.random.normal(k_r, (D, E), dtype=jnp.float32) * 0.02
        wi = jax.random.normal(k_wi, (E, D, F), dtype=jnp.float32) * D ** (-0.5)
        wo = jax.random.normal(k_wo, (E, F, D), dtype=jnp.float32) * F ** (-0.5)
        return {'x': x, 'ln_w': ln_w, 'w_router': w_router, 'wi': wi, 'wo': wo}
    _L0_ffn_all = _L0_ffn_setup()
    _L0_ffn_in = {k: v for k, v in _L0_ffn_all.items() if k in ('ln_w', 'w_router', 'wi', 'wo')}
    del _L0_ffn_all
    return {'x': x, 'itok_BS_0_15': itok_BS_0_15, 'itok_BS_0_3': itok_BS_0_3, 'itok_BS_0_9999': itok_BS_0_9999, 'itok_BS_0_2047': itok_BS_0_2047, 'fside_BS_age_tau': fside_BS_age_tau, 'fside_BS_delays_tau': fside_BS_delays_tau, 'L0_tok_word_table': _L0_tok_in['word_table'], 'L0_tok_modalities_table': _L0_tok_in['modalities_table'], 'L0_tok_seg_table': _L0_tok_in['seg_table'], 'L0_tok_npi_table': _L0_tok_in['npi_table'], 'L0_tok_posi_table': _L0_tok_in['posi_table'], 'L0_tok_age_w': _L0_tok_in['age_w'], 'L0_tok_age_b': _L0_tok_in['age_b'], 'L0_tok_age_w0': _L0_tok_in['age_w0'], 'L0_tok_age_b0': _L0_tok_in['age_b0'], 'L0_tok_delay_w': _L0_tok_in['delay_w'], 'L0_tok_delay_b': _L0_tok_in['delay_b'], 'L0_tok_delay_w0': _L0_tok_in['delay_w0'], 'L0_tok_delay_b0': _L0_tok_in['delay_b0'], 'L0_tok_ln_gamma': _L0_tok_in['ln_gamma'], 'L0_tok_ln_beta': _L0_tok_in['ln_beta'], 'L0_attn_qkv_w': _L0_attn_in['qkv_w'], 'L0_attn_qkv_b': _L0_attn_in['qkv_b'], 'L0_attn_proj_w': _L0_attn_in['proj_w'], 'L0_attn_proj_b': _L0_attn_in['proj_b'], 'L0_attn_q_norm_w': _L0_attn_in['q_norm_w'], 'L0_attn_k_norm_w': _L0_attn_in['k_norm_w'], 'L0_ffn_ln_w': _L0_ffn_in['ln_w'], 'L0_ffn_w_router': _L0_ffn_in['w_router'], 'L0_ffn_wi': _L0_ffn_in['wi'], 'L0_ffn_wo': _L0_ffn_in['wo']}

def reference(x, itok_BS_0_15, itok_BS_0_3, itok_BS_0_9999, itok_BS_0_2047, fside_BS_age_tau, fside_BS_delays_tau, L0_tok_word_table, L0_tok_modalities_table, L0_tok_seg_table, L0_tok_npi_table, L0_tok_posi_table, L0_tok_age_w, L0_tok_age_b, L0_tok_age_w0, L0_tok_age_b0, L0_tok_delay_w, L0_tok_delay_b, L0_tok_delay_w0, L0_tok_delay_b0, L0_tok_ln_gamma, L0_tok_ln_beta, L0_attn_qkv_w, L0_attn_qkv_b, L0_attn_proj_w, L0_attn_proj_b, L0_attn_q_norm_w, L0_attn_k_norm_w, L0_ffn_ln_w, L0_ffn_w_router, L0_ffn_wi, L0_ffn_wo):
    import jax
    import jax.numpy as jnp

    def _L0_tok_ref(word_ids, modalities_ids, seg_ids, npi_ids, posi_ids, age_tau, delays_tau, word_table, modalities_table, seg_table, npi_table, posi_table, age_w, age_b, age_w0, age_b0, delay_w, delay_b, delay_w0, delay_b0, ln_gamma, ln_beta):
        import jax, jax.numpy as jnp
        import numpy as np
        B, S, H = (8, 512, 192)
        VOCAB, MODAL_V, SEG_V, NPI_V, MAX_POS = (8000, 16, 4, 2500, 512)
        LN_EPS = 1e-12

        def _sinusoidal_table(max_pos, hidden):
            pos = np.arange(max_pos, dtype=np.float32)[:, None]
            idx = np.arange(hidden, dtype=np.float32)[None, :]
            angle = pos / np.power(10000.0, 2.0 * idx / hidden)
            tab = np.where(np.arange(hidden)[None, :] % 2 == 0, np.sin(angle), np.cos(angle))
            return jnp.asarray(tab, dtype=jnp.float32)

        def _time2vec(tau, w, b, w0, b0):
            t = tau[..., None]
            v1 = jnp.sin(t * w[0] + b)
            v2 = t * w0[0] + b0
            return jnp.concatenate([v1, v2], axis=-1)

        def _layer_norm(x, gamma, beta, eps):
            mu = jnp.mean(x, axis=-1, keepdims=True)
            var = jnp.mean(jnp.square(x - mu), axis=-1, keepdims=True)
            return (x - mu) * jax.lax.rsqrt(var + eps) * gamma + beta
        word_e = word_table[word_ids]
        seg_e = seg_table[seg_ids]
        modal_e = modalities_table[modalities_ids]
        npi_e = npi_table[npi_ids]
        posi_e = posi_table[posi_ids]
        age_e = _time2vec(age_tau, age_w, age_b, age_w0, age_b0)
        delay_e = _time2vec(delays_tau, delay_w, delay_b, delay_w0, delay_b0)
        emb = word_e + seg_e + posi_e + modal_e + delay_e + age_e + npi_e
        emb = _layer_norm(emb, ln_gamma, ln_beta, LN_EPS)
        return emb

    def _L0_attn_ref(x, qkv_w, qkv_b, proj_w, proj_b, q_norm_w, k_norm_w):
        import jax, jax.numpy as jnp
        import numpy as np
        import math
        DIM = 192
        NUM_HEADS = 12
        HEAD_DIM = DIM // NUM_HEADS
        EPS = 1e-06

        def rms_norm(x, w):
            xf = x.astype(jnp.float32)
            var = jnp.mean(xf * xf, axis=-1, keepdims=True)
            return (xf * jax.lax.rsqrt(var + EPS) * w).astype(x.dtype)
        B, N, C = x.shape
        H, D = (NUM_HEADS, C // NUM_HEADS)
        qkv = x @ qkv_w.T + qkv_b
        qkv = qkv.reshape(B, N, 3, H, D).transpose(2, 0, 3, 1, 4)
        q, k, v = (qkv[0], qkv[1], qkv[2])
        q = rms_norm(q, q_norm_w)
        k = rms_norm(k, k_norm_w)
        scale = 1.0 / math.sqrt(D)
        w = jnp.einsum('bhnd,bhmd->bhnm', q.astype(jnp.float32), k.astype(jnp.float32)) * scale
        w = jax.nn.softmax(w, axis=-1).astype(v.dtype)
        out = jnp.einsum('bhnm,bhmd->bhnd', w, v)
        out = out.transpose(0, 2, 1, 3).reshape(B, N, C)
        return out @ proj_w.T + proj_b

    def _L0_ffn_ref(x, ln_w, w_router, wi, wo):
        import jax, jax.numpy as jnp
        import numpy as np
        B, S, D, F, E = (8, 512, 192, 768, 16)
        CAP = 64
        EPS = 1e-06

        def _switch_moe_block(x, ln_w, w_router, wi, wo):
            var = jnp.mean(jnp.square(x.astype(jnp.float32)), axis=-1, keepdims=True)
            normed = (x * jax.lax.rsqrt(var + EPS)).astype(x.dtype) * ln_w
            logits = jnp.einsum('bsd,de->bse', normed.astype(jnp.float32), w_router.astype(jnp.float32))
            probs = jax.nn.softmax(logits, axis=-1)
            expert_idx = jnp.argmax(probs, axis=-1)
            onehot = jax.nn.one_hot(expert_idx, E, dtype=jnp.float32)
            priority = jnp.cumsum(onehot, axis=1)
            keep = onehot * (priority <= CAP)
            pos = (priority - 1.0).astype(jnp.int32)
            dispatch = keep[..., None] * jax.nn.one_hot(pos, CAP, dtype=jnp.float32)
            expert_in = jnp.einsum('bsec,bsd->becd', dispatch, normed)
            h = jax.nn.relu(jnp.einsum('becd,edf->becf', expert_in, wi))
            expert_out = jnp.einsum('becf,efd->becd', h, wo)
            combined = jnp.einsum('bsec,becd->bsd', dispatch, expert_out)
            routed = jnp.sum(dispatch, axis=(2, 3)) > 0
            next_states = jnp.where(routed[..., None], combined.astype(x.dtype), normed)
            router_prob = jnp.max(probs, axis=-1, keepdims=True).astype(x.dtype)
            return x + router_prob * next_states
        return _switch_moe_block(x, ln_w, w_router, wi, wo)
    h = _L0_tok_ref(x, itok_BS_0_15, itok_BS_0_3, itok_BS_0_9999, itok_BS_0_2047, fside_BS_age_tau, fside_BS_delays_tau, L0_tok_word_table, L0_tok_modalities_table, L0_tok_seg_table, L0_tok_npi_table, L0_tok_posi_table, L0_tok_age_w, L0_tok_age_b, L0_tok_age_w0, L0_tok_age_b0, L0_tok_delay_w, L0_tok_delay_b, L0_tok_delay_w0, L0_tok_delay_b0, L0_tok_ln_gamma, L0_tok_ln_beta)
    h = h + _L0_attn_ref(_layernorm(h, axis=-1), L0_attn_qkv_w, L0_attn_qkv_b, L0_attn_proj_w, L0_attn_proj_b, L0_attn_q_norm_w, L0_attn_k_norm_w)
    h = h + _L0_ffn_ref(_layernorm(h, axis=-1), L0_ffn_ln_w, L0_ffn_w_router, L0_ffn_wi, L0_ffn_wo)
    return h

_drawn_inputs = setup_inputs


def setup_inputs(seed=0):
    import zlib

    import numpy as np

    out = dict(_drawn_inputs(seed))
    spreads = {'L0_tok_ln_gamma': (1.0, 0.2),
     'L0_tok_ln_beta': (0.0, 0.1),
     'L0_attn_q_norm_w': (1.0, 0.2),
     'L0_attn_k_norm_w': (1.0, 0.2),
     'L0_ffn_ln_w': (1.0, 0.6)}
    factors = {'L0_tok_word_table': 5.379,
     'L0_tok_modalities_table': 6.189,
     'L0_tok_seg_table': 5.947,
     'L0_tok_npi_table': 6.277,
     'L0_attn_qkv_b': 3.155,
     'L0_attn_proj_b': 3.389,
     'L0_ffn_wi': 2.671}
    for name, (base, spread) in spreads.items():
        noise = np.random.default_rng([zlib.crc32(name.encode()), seed]).standard_normal(out[name].shape)
        drawn = base * np.exp(spread * noise) if base else spread * noise
        out[name] = jnp.asarray(drawn.astype(out[name].dtype))
    for name, factor in factors.items():
        out[name] = (out[name] * factor).astype(out[name].dtype)
    return out
```

```python
from contextlib import ExitStack

import concourse.bass as bass
from concourse import mybir

F32 = mybir.dt.float32
BF16 = mybir.dt.bfloat16
I32 = mybir.dt.int32
U32 = mybir.dt.uint32
ALU = mybir.AluOpType
ACT = mybir.ActivationFunctionType
AX = mybir.AxisListType.X

P = 128
NSEQ = 16
D = 192
HALF = D // 2
HEADS = 12
HD = D // HEADS
GROUPS = 3
CHUNKS = HEADS // GROUPS
HPAD = 32
NE = 16
CAP = 64
FF = 768
FC = FF // P
SLOTS = NSEQ * CAP
SPLIT = SLOTS // P
NLISTS = NE * SPLIT
WCOL = 2 * FF + FC * D
GW = GROUPS * HPAD
MODAL_V, SEG_V, WORD_V, NPI_V, POS_V = 16, 4, 8000, 2500, 512
T2V = D - 1
NPAIR = NSEQ // 2
NBLK = (NSEQ * P - NE) // P + NE
ROW = 2 * D + 1
BIG = float(1 << 20)
ROUND = 12582912.0
TWO_PI = 6.283185307179586
TWO_PI_HI = 6.28125
TWO_PI_LO = TWO_PI - TWO_PI_HI
PI_BELOW = 3.1415925
LN_EPS, NORM_EPS, RMS_EPS = 1e-12, 1e-5, 1e-6
ARENA_FIRST = 11


def tower_kernel(nc, t, out):
    assert NBLK == 31
    ctx = ExitStack()
    with ctx:
        def sb(name, shape, dt=F32):
            return ctx.enter_context(nc.sbuf_tensor(name, shape, dt))

        sems = {}

        def sem(name):
            if name not in sems:
                sems[name] = ctx.enter_context(nc.semaphore("s_" + name))
            return sems[name]

        weights = sb("weights", [P, NE * WCOL])
        w_by_expert = weights[:, :].rearrange("p (e c) -> p e c", e=NE)
        shared = sb("shared", [P, 4800])

        def carver(ap, start, end):
            at = [start]

            def carve(cols):
                a = at[0]
                at[0] += cols
                assert at[0] <= end, (at[0], end)
                return ap[:, a:a + cols]

            return carve

        arena = carver(weights, ARENA_FIRST * WCOL, NE * WCOL)
        share_a = carver(shared, 0, 4800)
        share_b = carver(shared, 0, 4800)

        h_all = arena(NSEQ * D)
        terms = [arena(6 * D) for _ in range(2)]
        turns = [arena(2 * D) for _ in range(2)]
        xn = [arena(D) for _ in range(2)]
        xT = [arena(2 * P) for _ in range(2)]
        qk_pad = [arena(2 * HEADS * HPAD) for _ in range(2)]
        v_aug = [arena(HEADS * (HD + 1)) for _ in range(2)]
        kT = [arena(CHUNKS * P) for _ in range(2)]
        qT = [arena(CHUNKS * P) for _ in range(2)]
        kT16 = [arena(CHUNKS * P // 2).bitcast(BF16) for _ in range(2)]
        qT16 = [arena(CHUNKS * P // 2).bitcast(BF16) for _ in range(2)]
        squares = [arena(2 * D) for _ in range(2)]
        o_sb = [squares[u][:, D:2 * D] for u in range(2)]
        oT = [arena(2 * P) for _ in range(2)]
        nT = xT
        probsT = [share_a(HEADS * P) for _ in range(2)]
        row = [share_a(ROW) for _ in range(2)]
        h1 = [share_a(D) for _ in range(2)]
        x2 = [share_a(D) for _ in range(2)]

        grow = [share_b(ROW) for _ in range(2)]
        gT = [share_b(2 * P) for _ in range(2)]
        hid = [share_b(FF) for _ in range(2)]
        hidT = [share_b(FC * P) for _ in range(2)]
        res = [share_b(D) for _ in range(2)]

        ident = sb("ident", [P, P])
        identb = sb("identb", [P, 2, P], BF16)
        wqkv = sb("wqkv", [HALF + 1, 2, 3 * D])
        wproj = sb("wproj", [HALF + 1, 2, D])
        wrout = sb("wrout", [HALF, 2, NE])
        gamma_bc = sb("gamma_bc", [P, D])
        beta_bc = sb("beta_bc", [P, D])
        lnw_bc = sb("lnw_bc", [P, D])
        t2v_w = sb("t2v_w", [P, 2, D])
        t2v_b = sb("t2v_b", [P, 2, D])
        tau = sb("tau", [P, 2, NSEQ])
        ids = sb("ids", [P, NSEQ, 4], I32)
        rawid = sb("rawid", [P, 5, NSEQ], I32)
        wrapped = sb("wrapped", [P, 5, NSEQ])
        qk_scale = sb("qk_scale", [P, 2])
        mhalf = sb("mhalf", [P, 2 * HEADS])
        expert_iota = sb("expert_iota", [P, NE])
        token_iota = sb("token_iota", [P, NSEQ])
        small = [sb(f"small{u}", [P, 160]) for u in range(2)]
        idx4 = [sb(f"idx4{u}", [P, 4], I32) for u in range(2)]
        slot_i = [sb(f"slot_i{u}", [P, 1], I32) for u in range(2)]
        top_i = [sb(f"top_i{u}", [P, 8], U32) for u in range(2)]
        onehot16 = [sb(f"onehot16{u}", [P, NE], BF16) for u in range(2)]
        total = sb("total", [P, NE])
        tokens = sb("tokens", [P, NLISTS])
        tok_col = [sb(f"tok_col{u}", [P, 1]) for u in range(2)]
        list_edge = sb("list_edge", [P, SPLIT])
        pair_table = shared
        plan = sb("plan", [P, 400])
        blk_idx = sb("blk_idx", [P, NBLK])
        blk_pen = sb("blk_pen", [P, NBLK])
        blk_col = sb("blk_col", [P, NBLK], I32)
        blk_list = sb("blk_list", [P, NBLK], I32)
        gidx = [sb(f"gidx{u}", [P, 1], I32) for u in range(2)]
        oidx = [sb(f"oidx{u}", [P, 1], I32) for u in range(2)]

        psum = [ctx.enter_context(nc.psum_tensor(f"psum{u}", [P, 4, 512], F32)) for u in range(2)]
        psum_s = [psum[u][:, 0:3, :] for u in range(2)]
        psum_m = [psum[u][:, 3, :] for u in range(2)]

        def cols(tile, start, n):
            return tile[:, start:start + n]

        STATS, MV, RSTD1, MV2, RSTD2, MV3, RSTD3, SSQ, RSTDN = 0, 8, 10, 12, 14, 16, 18, 20, 22
        SSQK, RQK, RSUM, TOP, NEGTOP, EXPS, ZSUM, ONEH, SCR = 24, 48, 72, 84, 92, 93, 109, 110, 126
        TOPF, PRIO, BASE, KEEP, DEST, SPLITNO = 144, 145, 146, 147, 148, 149

        pair_dram = nc.dram_tensor("pair_rows", [MODAL_V * SEG_V, D], F32).ap()
        rows = nc.dram_tensor("token_rows", [NSEQ * P, ROW], F32).ap()
        lists = nc.dram_tensor("expert_lists", [P * NLISTS, 1], F32).ap()

        def freed(eng, semaphore, value):
            if not isinstance(value, int) or value > 0:
                eng.wait_ge(semaphore, value)

        def pairs(eng, body, last):
            body(0)
            with eng.Fori(1, last) as i:
                body(i)

        N_CONST = 19
        Y0 = 256

        block = ctx.enter_context(nc.Block())

        @block.sync
        def _(sp):
            def const(dst, src):
                sp.dma_start(dst, src).then_inc(sem("const"), 16)

            const(pair_table[0:MODAL_V * SEG_V, 0:D], t["modal_table"].unsqueeze(1).broadcast_to([MODAL_V, SEG_V, D]))
            for m in range(MODAL_V):
                sp.dma_start(pair_table[m * SEG_V:(m + 1) * SEG_V, D:2 * D], t["seg_table"]).then_inc(sem("seg"), 16)
            const(rawid[:, :, :], t["ids"].rearrange("k p n -> p k n"))
            const(tau[:, :, :], t["taus"].rearrange("k p n -> p k n"))
            for k, a in enumerate(("age", "delay")):
                for tile, x, x0 in ((t2v_w, "_w", "_w0"), (t2v_b, "_b", "_b0")):
                    const(tile[:, k, 0:T2V], t[a + x].partition_broadcast(P))
                    const(tile[:, k, T2V:D], t[a + x0].partition_broadcast(P))
            const(gamma_bc[:, :], t["ln_gamma"].partition_broadcast(P))
            const(beta_bc[:, :], t["ln_beta"].partition_broadcast(P))
            const(lnw_bc[:, :], t["ln_w"].partition_broadcast(P))
            sp.wait_ge(sem("memset"), 3)
            const(wqkv[0:HALF, :, :], t["qkv_wT"].rearrange("(k p) f -> p k f", p=HALF))
            const(wqkv[HALF:HALF + 1, 1, :], t["qkv_b"].unsqueeze(0))
            const(wproj[0:HALF, :, :], t["proj_wT"].rearrange("(k p) f -> p k f", p=HALF))
            const(wproj[HALF:HALF + 1, 1, :], t["proj_b"].unsqueeze(0))
            const(wrout[:, :, :], t["w_router"].rearrange("(k p) f -> p k f", p=HALF))
            for g in range(P // HPAD):
                for j, name in enumerate(("q_norm_w", "k_norm_w")):
                    sp.dma_start(qk_scale[g * HPAD:g * HPAD + HD, j:j + 1], t[name].unsqueeze(1)).then_inc(sem("qkw"), 16)

            sp.wait_ge(sem("zeroed"), 1)
            sp.dma_start(lists.rearrange("(p q) o -> p (q o)", p=P), tokens[:, :]).then_inc(sem("lists0"), 16)
            sp.wait_ge(sem("pair_sum"), 1)
            sp.dma_start(pair_dram, pair_table[0:MODAL_V * SEG_V, 0:D]).then_inc(sem("pair_stored"), 16)

            def load_expert(e):
                sp.dma_start(w_by_expert[0:HALF, e, 0:2 * FF].rearrange("p (k f) -> p k f", k=2),
                             t["wi"][e].rearrange("(k p) f -> p k f", p=HALF)).then_inc(sem("weights"), 16)
                sp.dma_start(w_by_expert[:, e, 2 * FF:WCOL].rearrange("p (k f) -> p k f", k=FC),
                             t["wo"][e].rearrange("(k p) f -> p k f", p=P)).then_inc(sem("weights"), 16)

            for e in range(ARENA_FIRST):
                load_expert(e)

            def attn(i):
                for u in range(2):
                    n = 2 * i + u
                    sp.wait_ge(sem("out0"), n + 1)
                    sp.dma_start(out[bass.ds(n * P, P), :], x2[u]).then_inc(sem("out_plain"), 16)
                    sp.dma_start(rows[bass.ds(n * P, P), :], row[u]).then_inc(sem("out_plain"), 16)

            pairs(sp, attn, NPAIR)
            sp.wait_ge(sem("out_plain"), 32 * NSEQ)
            sp.wait_ge(sem("listed"), 16 * NSEQ)
            sp.dma_start(tokens[:, :], lists.rearrange("(p q) o -> p (q o)", p=P)).then_inc(sem("tokens"), 16)
            for e in range(ARENA_FIRST, NE):
                load_expert(e)
            sp.wait_ge(sem("scattered0"), 16 * ((NBLK + 1) // 2))
            sp.wait_ge(sem("scattered1"), 16 * (NBLK // 2))

        @block.gpsimd
        def _(pool):
            turn = {name: pool.alloc_register("turn_" + name) for name in ("idx4", "dest", "gidx", "res")}
            for name, first in (("idx4", 5), ("dest", 3), ("gidx", 3), ("res", 3)):
                pool.reg_mov(turn[name], first)

            def arrived(name, value):
                if isinstance(value, int):
                    pool.wait_ge(sem(name), value)
                else:
                    pool.wait_ge(sem(name), turn[name])
                    pool.reg_add(turn[name], turn[name], 1)

            nc.gpsimd.memset(ident[:, :], 0.0).then_inc(sem("g"), 1)
            nc.gpsimd.memset(identb[:, :, :], 1.0).then_inc(sem("g"), 1)
            pool.wait_ge(sem("g"), 2)
            nc.gpsimd.affine_select(out=ident[:, :], in_=ident[:, :], compare_op=ALU.not_equal, fill=1.0,
                                    base=0, pattern=[[-1, P]], channel_multiplier=1).then_inc(sem("ident"), 1)
            nc.gpsimd.affine_select(out=identb[:, 0, :], in_=identb[:, 0, :], compare_op=ALU.is_ge, fill=0.0,
                                    base=0, pattern=[[1, P]], channel_multiplier=-1).then_inc(sem("ident"), 1)
            nc.gpsimd.memset(mhalf[:, :], -0.5).then_inc(sem("g"), 1)
            nc.gpsimd.iota(expert_iota[:, :], [[1, NE]], base=0, channel_multiplier=0,
                           allow_small_or_imprecise_dtypes=True).then_inc(sem("ident"), 1)
            nc.gpsimd.iota(token_iota[:, :], [[P, NSEQ]], base=0, channel_multiplier=1,
                           allow_small_or_imprecise_dtypes=True).then_inc(sem("ident"), 1)
            nc.gpsimd.iota(list_edge[:, :], [[P, SPLIT]], base=P, channel_multiplier=0,
                           allow_small_or_imprecise_dtypes=True).then_inc(sem("ident"), 1)
            nc.gpsimd.iota(blk_idx[:, :], [[1, NBLK]], base=0, channel_multiplier=0,
                           allow_small_or_imprecise_dtypes=True).then_inc(sem("ident"), 1)
            pool.wait_ge(sem("pair_stored"), 16)
            pool.wait_ge(sem("lists0"), 16)

            def gathers(i):
                for u in range(2):
                    n = 2 * i + u
                    freed(pool, sem("summed"), 2 * i)
                    nc.gpsimd.tensor_copy(idx4[u][:, :], ids[:, bass.ds(n, 1), :].rearrange("p a k -> p (a k)")).then_inc(sem("idx4"), 1)
                    arrived("idx4", n + 1)
                    for k, (table, rows) in enumerate(((t["word_table"], WORD_V), (t["npi_table"], NPI_V),
                                                       (t["posi_table"], POS_V), (pair_dram, MODAL_V * SEG_V))):
                        nc.gpsimd.indirect_dma_start(
                            out=terms[u][:, k * D:(k + 1) * D], out_offset=None, in_=table,
                            in_offset=bass.IndirectOffsetOnAxis(ap=idx4[u][:, k:k + 1], axis=0),
                        ).then_inc(sem(f"gathered{u}"), 16)

            def power(i, src, made, done, width=1):
                for u in range(2):
                    pool.wait_ge(sem(made), 2 * i + u + 1)
                    s = small[u]
                    nc.gpsimd.tensor_tensor(cols(s, src[1], width), cols(s, src[0], width),
                                            mhalf[:, 0:width], ALU.pow).then_inc(sem(done), 1)

            def tok(i):
                gathers(i)
                power(i, (MV + 1, RSTD1), "var1", "rstd1")

            def attn(i):
                power(i, (MV2 + 1, RSTD2), "var2", "rstd2")
                power(i, (SSQK, RQK), "ssqk", "rqk", 2 * HEADS)
                power(i, (MV3 + 1, RSTD3), "var3", "rstd3")
                power(i, (SSQ, RSTDN), "ssq_e", "rstdn")
                for u in range(2):
                    n = 2 * i + u
                    arrived("dest", n + 1)
                    nc.gpsimd.indirect_dma_start(
                        out=lists, out_offset=bass.IndirectOffsetOnAxis(ap=slot_i[u][:, :], axis=0),
                        in_=tok_col[u][:, :], in_offset=None, bounds_check=NE * SLOTS - 1, oob_is_err=False,
                    ).then_inc(sem("listed"), 16)

            pool.wait_ge(sem("g"), 3)
            pool.wait_ge(sem("ids"), 2)
            def attn_then_tok(i):
                attn(i)
                tok(i + 1)

            tok(0)
            pairs(pool, attn_then_tok, NPAIR - 1)
            attn(NPAIR - 1)

            pool.wait_ge(sem("listed"), 16 * NSEQ)
            pool.wait_ge(sem("out_plain"), 32 * NSEQ)

            def blocks(i, us):
                for u in us:
                    j = 2 * i + u
                    arrived("gidx", j + 1)
                    nc.gpsimd.indirect_dma_start(
                        out=grow[u], out_offset=None, in_=rows,
                        in_offset=bass.IndirectOffsetOnAxis(ap=gidx[u][:, :], axis=0),
                    ).then_inc(sem(f"rows{u}"), 16)
                for u in us:
                    j = 2 * i + u
                    arrived("res", j + 1)
                    nc.gpsimd.indirect_dma_start(
                        out=out, out_offset=bass.IndirectOffsetOnAxis(ap=oidx[u][:, :], axis=0),
                        in_=res[u], in_offset=None, bounds_check=NSEQ * P - 1, oob_is_err=False,
                    ).then_inc(sem(f"scattered{u}"), 16)

            pairs(pool, lambda i: blocks(i, (0, 1)), NBLK // 2)
            blocks(NBLK // 2, (0,))

        @block.scalar
        def _(act):
            def tok(i):
                for u in range(2):
                    n = 2 * i + u
                    r = turns[u].rearrange("p (k d) -> p k d", k=2)
                    a = terms[u][:, 4 * D:6 * D].rearrange("p (k d) -> p k d", k=2)
                    act.wait_ge(sem("reduced"), n + 1)
                    nc.scalar.activation(a[:, :, 0:T2V], r[:, :, 0:T2V], ACT.Sin).then_inc(sem("sin"), 1)

            def attn(i):
                for u in range(2):
                    n = 2 * i + u
                    act.wait_ge(sem("p_xT"), n + 1)
                    nc.scalar.copy(xT[u][0:HALF, :], psum_m[u][0:HALF, 0:2 * P]).then_inc(sem("xT"), 1)
                for u in range(2):
                    n = 2 * i + u
                    act.wait_ge(sem("p_qkv"), n + 1)
                    nc.scalar.activation(squares[u], psum_s[u][:, 0, 0:2 * D], ACT.Square).then_inc(sem("sq"), 1)
                    nc.scalar.copy(v_aug[u].rearrange("p (h d) -> p h d", d=HD + 1)[:, :, 0:HD],
                                   psum_s[u][:, 1, 0:D].rearrange("p (h d) -> p h d", d=HD)).then_inc(sem("v"), 1)
                for u in range(2):
                    n = 2 * i + u
                    act.wait_ge(sem("p_kT"), n + 1)
                    nc.scalar.copy(kT[u][0:GW, :], psum_s[u][0:GW, 2, :]).then_inc(sem("kT"), 1)
                    nc.scalar.copy(kT16[u][0:GW, :], psum_s[u][0:GW, 2, :]).then_inc(sem("kT16"), 1)
                    act.wait_ge(sem("p_qT0"), n + 1)
                    nc.scalar.activation(qT16[u][0:GW, :], psum_m[u][0:GW, :], ACT.Copy, scale=qk_scale[0:GW, 0:1]).then_inc(sem("qT16"), 1)
                for u in range(2):
                    n = 2 * i + u
                    act.wait_ge(sem("p_qT1"), n + 1)
                    nc.scalar.activation(qT[u][0:GW, :], psum_m[u][0:GW, :], ACT.Copy, scale=qk_scale[0:GW, 0:1]).then_inc(sem("qT"), 1)
                for u in range(2):
                    n = 2 * i + u
                    act.wait_ge(sem("p_sT"), n + 1)
                    nc.scalar.activation(probsT[u], psum_s[u][:, :, :].rearrange("p b c -> p (b c)"), ACT.Exp).then_inc(sem("probs"), 1)
                for u in range(2):
                    n = 2 * i + u
                    act.wait_ge(sem("p_oT"), n + 1)
                    nc.scalar.copy(oT[u][0:HALF, :], psum_m[u][0:HALF, 2 * P:4 * P]).then_inc(sem("oT"), 1)
                for u in range(2):
                    n = 2 * i + u
                    act.wait_ge(sem("x2"), n + 1)
                    nc.scalar.activation(squares[u][:, 0:D], x2[u], ACT.Square,
                                         accum_out=cols(small[u], SSQ + 1, 1)).then_inc(sem("ssq"), 1)
                for u in range(2):
                    n = 2 * i + u
                    act.wait_ge(sem("p_nT"), n + 1)
                    nc.scalar.copy(nT[u][0:HALF, :], psum_m[u][0:HALF, 0:2 * P]).then_inc(sem("nT"), 1)
                for u in range(2):
                    n = 2 * i + u
                    act.wait_ge(sem("negtop"), n + 1)
                    act.wait_ge(sem("topi"), n + 1)
                    nc.scalar.activation(cols(small[u], EXPS, NE), psum_s[u][:, 1, 0:NE], ACT.Exp,
                                         bias=cols(small[u], NEGTOP, 1), accum_out=cols(small[u], ZSUM, 1)).then_inc(sem("zsum"), 1)

            act.wait_ge(sem("const"), 16 * N_CONST)
            act.wait_ge(sem("qk_part"), 4)
            def attn_then_tok(i):
                attn(i)
                tok(i + 1)

            tok(0)
            pairs(act, attn_then_tok, NPAIR - 1)
            attn(NPAIR - 1)

            def blocks(i, us):
                for u in us:
                    act.wait_ge(sem("b_gT"), 2 * i + u + 1)
                    nc.scalar.copy(gT[u][0:HALF, :].rearrange("p (k c) -> p k c", k=2),
                                   psum[u][0:HALF, 0:2, FF // 2:512]).then_inc(sem("gT"), 1)
                for u in us:
                    act.wait_ge(sem("b_hid"), 2 * i + u + 1)
                    nc.scalar.activation(hid[u].rearrange("p (k f) -> p k f", k=2), psum_s[u][:, 0:2, 0:FF // 2],
                                         ACT.Relu).then_inc(sem("hid"), 1)

            pairs(act, lambda i: blocks(i, (0, 1)), NBLK // 2)
            blocks(NBLK // 2, (0,))

        @block.vector
        def _(dve):
            V = nc.vector

            for u in range(2):
                V.memset(qk_pad[u], 0.0).then_inc(sem("pad0"), 1)
                for tile in (xT[u], oT[u]):
                    V.memset(tile[HALF:HALF + 1, :], 1.0).then_inc(sem("ones"), 1)
                V.memset(v_aug[u].rearrange("p (h d) -> p h d", d=HD + 1)[:, :, HD:HD + 1], 1.0).then_inc(sem("ones"), 1)
            V.memset(tokens[:, :], 0.0).then_inc(sem("zeroed"), 1)
            V.memset(total[:, :], 0.0).then_inc(sem("total"), 1)
            V.memset(qk_scale[:, :], -1.0).then_inc(sem("memset"), 1)
            V.memset(wqkv[HALF:HALF + 1, 0, :], 0.0).then_inc(sem("memset"), 1)
            V.memset(wproj[HALF:HALF + 1, 0, :], 0.0).then_inc(sem("memset"), 1)
            dve.wait_ge(sem("pad0"), 2)
            for u in range(2):
                kp = qk_pad[u].rearrange("p (h d) -> p h d", d=HPAD)
                V.memset(kp[:, HEADS:2 * HEADS, HD:HD + 1], 1.0).then_inc(sem("pad1"), 1)
            dve.wait_ge(sem("const"), 16 * N_CONST)
            dve.wait_ge(sem("seg"), 16 * MODAL_V)
            pt = pair_table[0:MODAL_V * SEG_V, :]
            V.tensor_tensor(pt[:, 0:D], pt[:, 0:D], pt[:, D:2 * D], ALU.add).then_inc(sem("pair_sum"), 1)
            for k, rows in enumerate((WORD_V, NPI_V, POS_V, MODAL_V, SEG_V)):
                V.tensor_scalar(wrapped[:, k, :], rawid[:, k, :], 0.0, float(rows), ALU.is_lt, ALU.mult).then_inc(sem("wrap"), 1)
                dve.wait_ge(sem("wrap"), 3 * k + 1)
                V.tensor_tensor(wrapped[:, k, :], wrapped[:, k, :], rawid[:, k, :], ALU.add).then_inc(sem("wrap"), 1)
                dve.wait_ge(sem("wrap"), 3 * k + 2)
                V.tensor_scalar(wrapped[:, k, :], wrapped[:, k, :], 0.0, float(rows - 1), ALU.max, ALU.min).then_inc(sem("wrap"), 1)
            dve.wait_ge(sem("wrap"), 15)
            V.tensor_copy(ids[:, :, 0:3], wrapped[:, 0:3, :].rearrange("p k n -> p n k")).then_inc(sem("ids"), 1)
            V.scalar_tensor_tensor(ids[:, :, 3], wrapped[:, 3, :], float(SEG_V), wrapped[:, 4, :], ALU.mult, ALU.add).then_inc(sem("ids"), 1)
            dve.wait_ge(sem("qkw"), 16 * 8)
            for g in range(P // HPAD):
                a = qk_scale[g * HPAD:g * HPAD + HD, :]
                V.scalar_tensor_tensor(a[:, 0:1], a[:, 0:1], HD ** -0.5, a[:, 1:2], ALU.mult, ALU.mult).then_inc(sem("qk_part"), 1)
            dve.wait_ge(sem("qk_part"), 4)
            dve.wait_ge(sem("ident"), 6)

            def tok(i):
                for u in range(2):
                    n = 2 * i + u
                    a = terms[u][:, 4 * D:6 * D].rearrange("p (k d) -> p k d", k=2)
                    r = turns[u].rearrange("p (k d) -> p k d", k=2)
                    freed(dve, sem("summed"), 2 * i)
                    for k in range(2):
                        V.scalar_tensor_tensor(a[:, k, :], t2v_w[:, k, :], tau[:, k, bass.ds(n, 1)], t2v_b[:, k, :],
                                               ALU.mult, ALU.add).then_inc(sem("arg"), 1)
                    dve.wait_ge(sem("arg"), 2 * n + 2)
                    V.tensor_scalar(r, a, 1.0 / TWO_PI, ROUND, ALU.mult, ALU.add).then_inc(sem("turn0"), 1)
                    dve.wait_ge(sem("turn0"), n + 1)
                    V.tensor_scalar(r, r, ROUND, None, ALU.subtract).then_inc(sem("turn1"), 1)
                    dve.wait_ge(sem("turn1"), n + 1)
                    x = a[:, :, 0:T2V]
                    V.scalar_tensor_tensor(x, r[:, :, 0:T2V], -TWO_PI_HI, x, ALU.mult, ALU.add).then_inc(sem("turn2"), 1)
                    dve.wait_ge(sem("turn2"), n + 1)
                    V.scalar_tensor_tensor(r[:, :, 0:T2V], r[:, :, 0:T2V], -TWO_PI_LO, x, ALU.mult, ALU.add).then_inc(sem("turn3"), 1)
                    dve.wait_ge(sem("turn3"), n + 1)
                    V.tensor_scalar(r[:, :, 0:T2V], r[:, :, 0:T2V], PI_BELOW, -PI_BELOW, ALU.min, ALU.max).then_inc(sem("reduced"), 1)
                for u in range(2):
                    n = 2 * i + u
                    s = small[u]
                    h = h_all[:, bass.ds(n * D, D)]
                    dve.wait_ge(sem("sin"), n + 1)
                    dve.wait_ge(sem(f"gathered{u}"), 64 * (i + 1))
                    V.tensor_reduce(h, terms[u].rearrange("p (k d) -> p d k", k=6), AX, ALU.add).then_inc(sem("summed"), 1)
                    dve.wait_ge(sem("ident"), 6)
                    dve.wait_ge(sem("summed"), n + 1)
                    V.bn_stats(cols(s, STATS, 6), h).then_inc(sem("stats1"), 1)
                    dve.wait_ge(sem("ident"), 6)
                    dve.wait_ge(sem("stats1"), n + 1)
                    V.bn_aggr(cols(s, MV, 2), cols(s, STATS, 6)).then_inc(sem("mv1"), 1)
                    dve.wait_ge(sem("mv1"), n + 1)
                    V.tensor_scalar(cols(s, MV + 1, 1), cols(s, MV + 1, 1), LN_EPS, None, ALU.add).then_inc(sem("var1"), 1)
                for u in range(2):
                    n = 2 * i + u
                    s = small[u]
                    h = h_all[:, bass.ds(n * D, D)]
                    dve.wait_ge(sem("rstd1"), n + 1)
                    V.tensor_scalar(h, h, cols(s, MV, 1), cols(s, RSTD1, 1), ALU.subtract, ALU.mult).then_inc(sem("ln1a"), 1)
                    dve.wait_ge(sem("ln1a"), n + 1)
                    V.tensor_tensor(h, h, gamma_bc[:, :], ALU.mult).then_inc(sem("ln1b"), 1)
                    dve.wait_ge(sem("ln1b"), n + 1)
                    V.tensor_tensor(h, h, beta_bc[:, :], ALU.add).then_inc(sem("h"), 1)
                    dve.wait_ge(sem("ident"), 6)
                    dve.wait_ge(sem("h"), n + 1)
                    V.bn_stats(cols(s, STATS, 6), h).then_inc(sem("stats2"), 1)
                    dve.wait_ge(sem("ident"), 6)
                    dve.wait_ge(sem("stats2"), n + 1)
                    V.bn_aggr(cols(s, MV2, 2), cols(s, STATS, 6)).then_inc(sem("mv2"), 1)
                    dve.wait_ge(sem("mv2"), n + 1)
                    V.tensor_scalar(cols(s, MV2 + 1, 1), cols(s, MV2 + 1, 1), NORM_EPS, None, ALU.add).then_inc(sem("var2"), 1)

            def attn(i):
                for u in range(2):
                    n = 2 * i + u
                    dve.wait_ge(sem("rstd2"), n + 1)
                    freed(dve, sem("p_xT"), 2 * i)
                    V.tensor_scalar(xn[u], h_all[:, bass.ds(n * D, D)], cols(small[u], MV2, 1), cols(small[u], RSTD2, 1),
                                    ALU.subtract, ALU.mult).then_inc(sem("xn"), 1)
                for u in range(2):
                    n = 2 * i + u
                    s = small[u]
                    dve.wait_ge(sem("sq"), n + 1)
                    V.tensor_reduce(cols(s, SSQK, 2 * HEADS), squares[u].rearrange("p (h d) -> p h d", d=HD), AX,
                                    ALU.add).then_inc(sem("ssqk0"), 1)
                    dve.wait_ge(sem("ssqk0"), n + 1)
                    V.tensor_scalar(cols(s, SSQK, 2 * HEADS), cols(s, SSQK, 2 * HEADS), 1.0 / HD, RMS_EPS,
                                    ALU.mult, ALU.add).then_inc(sem("ssqk"), 1)
                for u in range(2):
                    n = 2 * i + u
                    dve.wait_ge(sem("rqk"), n + 1)
                    freed(dve, sem("p_qT1"), 2 * i)
                    V.tensor_tensor(qk_pad[u].rearrange("p (h d) -> p h d", d=HPAD)[:, :, 0:HD],
                                    psum_s[u][:, 0, 0:2 * D].rearrange("p (h d) -> p h d", d=HD),
                                    cols(small[u], RQK, 2 * HEADS).unsqueeze(2).broadcast_to([P, 2 * HEADS, HD]),
                                    ALU.mult).then_inc(sem("qk"), 1)
                for u in range(2):
                    n = 2 * i + u
                    dve.wait_ge(sem("p_guard"), n + 1)
                    V.tensor_reduce(qk_pad[u][:, 0:CHUNKS * GW].rearrange("p (c g d) -> p g c d", c=CHUNKS, d=HPAD)[:, :, :, HD],
                                    psum_s[u].rearrange("p g (c m) -> p g c m", m=P), AX,
                                    ALU.max).then_inc(sem("guard"), 1)
                for u in range(2):
                    n = 2 * i + u
                    s = small[u]
                    pv = psum_m[u][:, 0:HEADS * (HD + 1)].rearrange("p (h d) -> p h d", d=HD + 1)
                    dve.wait_ge(sem("p_pv"), n + 1)
                    V.reciprocal(cols(s, RSUM, HEADS), pv[:, :, HD]).then_inc(sem("rsum"), 1)
                    dve.wait_ge(sem("rsum"), n + 1)
                    V.tensor_tensor(o_sb[u].rearrange("p (h d) -> p h d", d=HD), pv[:, :, 0:HD],
                                    cols(s, RSUM, HEADS).unsqueeze(2).broadcast_to([P, HEADS, HD]),
                                    ALU.mult).then_inc(sem("o"), 1)
                for u in range(2):
                    n = 2 * i + u
                    s = small[u]
                    dve.wait_ge(sem("p_y"), n + 1)
                    V.tensor_tensor(h1[u], psum_s[u][:, 0, 0:D], h_all[:, bass.ds(n * D, D)], ALU.add).then_inc(sem("h1"), 1)
                    dve.wait_ge(sem("ident"), 6)
                    dve.wait_ge(sem("h1"), n + 1)
                    V.bn_stats(cols(s, STATS, 6), h1[u]).then_inc(sem("stats3"), 1)
                    dve.wait_ge(sem("ident"), 6)
                    dve.wait_ge(sem("stats3"), n + 1)
                    V.bn_aggr(cols(s, MV3, 2), cols(s, STATS, 6)).then_inc(sem("mv3"), 1)
                    dve.wait_ge(sem("mv3"), n + 1)
                    V.tensor_scalar(cols(s, MV3 + 1, 1), cols(s, MV3 + 1, 1), NORM_EPS, None, ALU.add).then_inc(sem("var3"), 1)
                for u in range(2):
                    n = 2 * i + u
                    s = small[u]
                    dve.wait_ge(sem("rstd3"), n + 1)
                    freed(dve, sem("out_plain"), 64 * i)
                    freed(dve, sem("listed"), 32 * i)
                    V.tensor_scalar(x2[u], h1[u], cols(s, MV3, 1), cols(s, RSTD3, 1), ALU.subtract, ALU.mult).then_inc(sem("x2"), 1)
                    dve.wait_ge(sem("x2"), n + 1)
                    V.tensor_tensor(row[u][:, D:2 * D], x2[u], h1[u], ALU.add).then_inc(sem("base"), 1)
                for u in range(2):
                    n = 2 * i + u
                    s = small[u]
                    dve.wait_ge(sem("ssq"), n + 1)
                    V.tensor_scalar(cols(s, SSQ, 1), cols(s, SSQ + 1, 1), 1.0 / D, RMS_EPS, ALU.mult, ALU.add).then_inc(sem("ssq_e"), 1)
                for u in range(2):
                    n = 2 * i + u
                    dve.wait_ge(sem("rstdn"), n + 1)
                    V.scalar_tensor_tensor(row[u][:, 0:D], x2[u], cols(small[u], RSTDN, 1), lnw_bc[:, :],
                                           ALU.mult, ALU.mult).then_inc(sem("normed"), 1)
                for u in range(2):
                    n = 2 * i + u
                    s = small[u]
                    logits = psum_s[u][:, 1, 0:NE]
                    dve.wait_ge(sem("ident"), 6)
                    dve.wait_ge(sem("p_logit"), n + 1)
                    V.max(cols(s, TOP, 8), logits).then_inc(sem("top"), 1)
                    dve.wait_ge(sem("top"), n + 1)
                    V.tensor_scalar(cols(s, NEGTOP, 1), cols(s, TOP, 1), -1.0, None, ALU.mult).then_inc(sem("negtop"), 1)
                    V.max_index(top_i[u][:, :], cols(s, TOP, 8), logits).then_inc(sem("topi"), 1)
                    dve.wait_ge(sem("topi"), n + 1)
                    V.tensor_copy(cols(s, TOPF, 1), top_i[u][:, 0:1]).then_inc(sem("topf"), 1)
                    dve.wait_ge(sem("topf"), n + 1)
                    V.tensor_scalar(cols(s, ONEH, NE), expert_iota[:, :], cols(s, TOPF, 1), None, ALU.is_equal).then_inc(sem("oneh"), 1)
                    dve.wait_ge(sem("oneh"), n + 1)
                    V.tensor_copy(onehot16[u][:, :], cols(s, ONEH, NE)).then_inc(sem("oneh16"), 1)
                for u in range(2):
                    n = 2 * i + u
                    s = small[u]
                    dve.wait_ge(sem("zsum"), n + 1)
                    V.reciprocal(row[u][:, 2 * D:2 * D + 1], cols(s, ZSUM, 1)).then_inc(sem("rp"), 1)
                    V.tensor_copy(tok_col[u][:, :], token_iota[:, bass.ds(n, 1)]).then_inc(sem("tokcol"), 1)
                    dve.wait_ge(sem("rp"), n + 1)
                    V.scalar_tensor_tensor(x2[u], row[u][:, 0:D], row[u][:, 2 * D:2 * D + 1], row[u][:, D:2 * D],
                                           ALU.mult, ALU.add).then_inc(sem("out0"), 1)
                    dve.wait_ge(sem("p_prio"), n + 1)
                    V.scalar_tensor_tensor(cols(s, SCR, NE), psum_s[u][:, 1, NE:2 * NE], 1.0, cols(s, ONEH, NE), ALU.mult, ALU.mult,
                                           accum_out=cols(s, PRIO, 1)).then_inc(sem("prio"), 1)
                    dve.wait_ge(sem("total"), n + 1)
                    V.scalar_tensor_tensor(cols(s, EXPS, NE), total[:, :], 1.0, cols(s, ONEH, NE), ALU.mult, ALU.mult,
                                           accum_out=cols(s, BASE, 1)).then_inc(sem("basep"), 1)
                    V.scalar_tensor_tensor(total[:, :], psum_s[u][:, 1, 2 * NE:3 * NE], float(CAP), total[:, :],
                                           ALU.min, ALU.add).then_inc(sem("total"), 1)
                    dve.wait_ge(sem("prio"), n + 1)
                    V.tensor_scalar(cols(s, KEEP, 1), cols(s, PRIO, 1), float(CAP), BIG, ALU.is_gt, ALU.mult).then_inc(sem("keep"), 1)
                    dve.wait_ge(sem("basep"), n + 1)
                    V.tensor_tensor(cols(s, BASE, 1), cols(s, BASE, 1), cols(s, PRIO, 1), ALU.add).then_inc(sem("dest0"), 1)
                    dve.wait_ge(sem("dest0"), n + 1)
                    V.tensor_scalar(cols(s, SCR, SPLIT), list_edge[:, :], cols(s, BASE, 1), None, ALU.is_lt, ALU.add,
                                    accum_out=cols(s, SPLITNO, 1)).then_inc(sem("dest1"), 1)
                    dve.wait_ge(sem("keep"), n + 1)
                    V.scalar_tensor_tensor(cols(s, DEST, 1), cols(s, BASE, 1), float(NLISTS), cols(s, KEEP, 1), ALU.mult, ALU.add).then_inc(sem("dest2"), 1)
                    dve.wait_ge(sem("dest2"), n + 1)
                    dve.wait_ge(sem("dest1"), n + 1)
                    V.scalar_tensor_tensor(cols(s, DEST, 1), cols(s, SPLITNO, 1), 1.0 - P * NLISTS, cols(s, DEST, 1), ALU.mult, ALU.add).then_inc(sem("dest3"), 1)
                    dve.wait_ge(sem("dest3"), n + 1)
                    V.scalar_tensor_tensor(cols(s, DEST, 1), cols(s, TOPF, 1), float(SPLIT), cols(s, DEST, 1), ALU.mult, ALU.add).then_inc(sem("dest4"), 1)
                    dve.wait_ge(sem("dest4"), n + 1)
                    dve.wait_ge(sem("tokcol"), n + 1)
                    V.tensor_scalar(slot_i[u][:, :], cols(s, DEST, 1), float(NLISTS), None, ALU.subtract).then_inc(sem("dest"), 1)

            def attn_then_tok(i):
                attn(i)
                tok(i + 1)

            tok(0)
            pairs(dve, attn_then_tok, NPAIR - 1)
            attn(NPAIR - 1)

            steps = [0]

            def planned(ins):
                steps[0] += 1
                ins.then_inc(sem("plan"), 1)
                dve.wait_ge(sem("plan"), steps[0])

            dve.wait_ge(sem("total"), NSEQ + 1)
            dve.wait_ge(sem("out_plain"), 32 * NSEQ)
            dve.wait_ge(sem("listed"), 16 * NSEQ)
            big = shared[:, 0:NBLK * NE].rearrange("p (j e) -> p j e", e=NE)
            big2 = shared[:, 512:512 + NBLK * NE].rearrange("p (j e) -> p j e", e=NE)
            nb, cum, ones, excl = (cols(plan, a, NE) for a in (16, 32, 48, 64))
            jrow, ej, within, length, q0, q1 = (cols(plan, 112 + 32 * a, NBLK) for a in range(6))
            nblk = cols(plan, 304, 1)
            k8 = shared[:, 0:8 * NE].rearrange("p (e k) -> p e k", k=8)
            planned(V.memset(ones, 1.0))
            for k in range(NSEQ * CAP // P):
                planned(V.tensor_scalar(k8[:, :, k], total[:, :], float(k * P), None, ALU.is_gt))
            planned(V.tensor_reduce(nb, k8, AX, ALU.add))
            planned(V.tensor_tensor_scan(cum, ones, nb, 0.0, ALU.mult, ALU.add))
            planned(V.tensor_tensor(excl, cum, nb, ALU.subtract))
            planned(V.tensor_scalar(nblk, cum[:, NE - 1:NE], 1.0, None, ALU.subtract))
            planned(V.tensor_scalar(jrow, blk_idx[:, :], nblk, None, ALU.min))

            def over(v):
                return v.unsqueeze(1).broadcast_to([P, NBLK, NE])

            planned(V.tensor_tensor(big, over(cum), jrow.unsqueeze(2).broadcast_to([P, NBLK, NE]), ALU.is_le))
            planned(V.tensor_reduce(ej, big, AX, ALU.add))
            planned(V.tensor_scalar(blk_col[:, :], ej, float(WCOL), None, ALU.mult))
            V.tensor_copy(plan[:, 399:400], ones[:, 0:1]).then_inc(sem("blk_col"), 1)
            planned(V.tensor_tensor(big, over(expert_iota[:, :]), ej.unsqueeze(2).broadcast_to([P, NBLK, NE]), ALU.is_equal))
            planned(V.tensor_tensor(big2, big, over(excl), ALU.mult))
            planned(V.tensor_reduce(within, big2, AX, ALU.add))
            planned(V.tensor_tensor(big2, big, over(total[:, :]), ALU.mult))
            planned(V.tensor_reduce(length, big2, AX, ALU.add))
            planned(V.tensor_tensor(within, jrow, within, ALU.subtract))
            planned(V.scalar_tensor_tensor(blk_list[:, :], ej, float(SPLIT), within, ALU.mult, ALU.add))
            planned(V.tensor_scalar(within, within, float(P), token_iota[:, 0:1], ALU.mult, ALU.add))
            planned(V.tensor_tensor(q0, within, length, ALU.is_ge))
            planned(V.tensor_tensor(q1, blk_idx[:, :], jrow, ALU.is_gt))
            planned(V.tensor_tensor(q0, q0, q1, ALU.add))
            planned(V.tensor_scalar(blk_pen[:, :], q0, BIG, None, ALU.mult))
            dve.wait_ge(sem("tokens"), 16)

            def blocks(i, us):
                for u in us:
                    j = 2 * i + u
                    at = dve.value_load(blk_list[0:1, bass.ds(j, 1)], min_val=0, max_val=NLISTS - 1)
                    freed(dve, sem(f"rows{u}"), 16 * i)
                    V.tensor_copy(gidx[u][:, :], tokens[:, bass.ds(at, 1)]).then_inc(sem("gidx"), 1)
                    freed(dve, sem(f"scattered{u}"), 16 * i)
                    V.tensor_tensor(oidx[u][:, :], tokens[:, bass.ds(at, 1)], blk_pen[:, bass.ds(j, 1)], ALU.add).then_inc(sem("oidx"), 1)
                for u in us:
                    j = 2 * i + u
                    dve.wait_ge(sem("b_hT"), j + 1)
                    V.tensor_copy(hidT[u], psum[u][:, 2:4, :].rearrange("p b c -> p (b c)")[:, 0:FC * P]).then_inc(sem("hidT"), 1)
                for u in us:
                    j = 2 * i + u
                    dve.wait_ge(sem("b_y"), j + 1)
                    dve.wait_ge(sem("oidx"), j + 1)
                    V.scalar_tensor_tensor(res[u], psum[u][:, 3, Y0:Y0 + D], grow[u][:, 2 * D:2 * D + 1], grow[u][:, D:2 * D],
                                           ALU.mult, ALU.add).then_inc(sem("res"), 1)

            pairs(dve, lambda i: blocks(i, (0, 1)), NBLK // 2)
            blocks(NBLK // 2, (0,))

        @block.tensor
        def _(pe):
            T = nc.tensor

            def halves(dst, src, done):
                T.transpose(dst(0), src[:, 0:HALF], ident[:, :])
                T.transpose(dst(1), src[:, HALF:D], ident[:, :]).then_inc(sem(done), 1)

            def over_d(dst, xt, w, start, width, bias):
                k1 = HALF + 1 if bias else HALF
                T.matmul(dst, xt[0:HALF, 0:P], w[0:HALF, 0, start:start + width], start=True, stop=False)
                return T.matmul(dst, xt[0:k1, P:2 * P], w[0:k1, 1, start:start + width], start=False, stop=True)

            def k_pad(u):
                return qk_pad[u][:, HEADS * HPAD:]

            def attn(i):
                for u in range(2):
                    n = 2 * i + u
                    pe.wait_ge(sem("xn"), n + 1)
                    freed(pe, sem("nT"), 2 * i)
                    halves(lambda k: psum_m[u][0:HALF, k * P:(k + 1) * P], xn[u], "p_xT")
                for u in range(2):
                    n = 2 * i + u
                    pe.wait_ge(sem("xT"), n + 1)
                    pe.wait_ge(sem("total"), 2 * i + 1)
                    freed(pe, sem("zsum"), 2 * i)
                    freed(pe, sem("h1"), 2 * i)
                    over_d(psum_s[u][:, 0, 0:2 * D], xT[u], wqkv, 0, 2 * D, True)
                    over_d(psum_s[u][:, 1, 0:D], xT[u], wqkv, 2 * D, D, True).then_inc(sem("p_qkv"), 1)
                for u in range(2):
                    n = 2 * i + u
                    pe.wait_ge(sem("qk"), n + 1)
                    for c in range(CHUNKS):
                        last = T.transpose(psum_s[u][0:GW, 2, c * P:(c + 1) * P], k_pad(u)[:, c * GW:(c + 1) * GW], ident[:, :])
                    last.then_inc(sem("p_kT"), 1)
                    for c in range(CHUNKS):
                        last = T.transpose(psum_m[u][0:GW, c * P:(c + 1) * P], qk_pad[u][:, c * GW:(c + 1) * GW], ident[:, :])
                    last.then_inc(sem("p_qT0"), 1)
                for u in range(2):
                    n = 2 * i + u
                    pe.wait_ge(sem("v"), n + 1)
                    pe.wait_ge(sem("kT16"), n + 1)
                    pe.wait_ge(sem("qT16"), n + 1)
                    for h in range(HEADS):
                        c, g = divmod(h, GROUPS)
                        rows = slice(g * HPAD, g * HPAD + HD)
                        last = T.matmul(psum_s[u][:, g, c * P:(c + 1) * P], qT16[u][rows, c * P:(c + 1) * P],
                                        kT16[u][rows, c * P:(c + 1) * P], start=True, stop=True)
                    last.then_inc(sem("p_guard"), 1)
                for u in range(2):
                    n = 2 * i + u
                    pe.wait_ge(sem("guard"), n + 1)
                    for c in range(CHUNKS):
                        last = T.transpose(psum_m[u][0:GW, c * P:(c + 1) * P], qk_pad[u][:, c * GW:(c + 1) * GW], ident[:, :])
                    last.then_inc(sem("p_qT1"), 1)
                for u in range(2):
                    n = 2 * i + u
                    pe.wait_ge(sem("qT"), n + 1)
                    for h in range(HEADS):
                        c, g = divmod(h, GROUPS)
                        rows = slice(g * HPAD, g * HPAD + HD + 1)
                        last = T.matmul(psum_s[u][:, g, c * P:(c + 1) * P], kT[u][rows, c * P:(c + 1) * P],
                                        qT[u][rows, c * P:(c + 1) * P], start=True, stop=True)
                    last.then_inc(sem("p_sT"), 1)
                for u in range(2):
                    n = 2 * i + u
                    pe.wait_ge(sem("probs"), n + 1)
                    for h in range(HEADS):
                        c, g = divmod(h, GROUPS)
                        at = (g * CHUNKS + c) * P
                        last = T.matmul(psum_m[u][:, h * (HD + 1):(h + 1) * (HD + 1)], probsT[u][:, at:at + P],
                                        v_aug[u][:, h * (HD + 1):(h + 1) * (HD + 1)], start=True, stop=True)
                    last.then_inc(sem("p_pv"), 1)
                for u in range(2):
                    n = 2 * i + u
                    pe.wait_ge(sem("o"), n + 1)
                    halves(lambda k: psum_m[u][0:HALF, (2 + k) * P:(3 + k) * P], o_sb[u], "p_oT")
                for u in range(2):
                    n = 2 * i + u
                    pe.wait_ge(sem("oT"), n + 1)
                    over_d(psum_s[u][:, 0, 0:D], oT[u], wproj, 0, D, True).then_inc(sem("p_y"), 1)
                for u in range(2):
                    n = 2 * i + u
                    pe.wait_ge(sem("normed"), n + 1)
                    halves(lambda k: psum_m[u][0:HALF, k * P:(k + 1) * P], row[u], "p_nT")
                for u in range(2):
                    n = 2 * i + u
                    pe.wait_ge(sem("nT"), n + 1)
                    over_d(psum_s[u][:, 1, 0:NE], nT[u], wrout, 0, NE, False).then_inc(sem("p_logit"), 1)
                for u in range(2):
                    n = 2 * i + u
                    pe.wait_ge(sem("oneh16"), n + 1)
                    pe.wait_ge(sem("zsum"), n + 1)
                    T.matmul(psum_s[u][:, 1, NE:2 * NE], identb[:, 0, :], onehot16[u][:, :], start=True, stop=True)
                    T.matmul(psum_s[u][:, 1, 2 * NE:3 * NE], identb[:, 1, :], onehot16[u][:, :], start=True, stop=True).then_inc(sem("p_prio"), 1)

            pe.wait_ge(sem("ident"), 6)
            pe.wait_ge(sem("ones"), 6)
            pe.wait_ge(sem("pad1"), 2)
            pe.wait_ge(sem("const"), 16 * N_CONST)
            pairs(pe, attn, NPAIR)

            pe.wait_ge(sem("weights"), 32 * NE)
            pe.wait_ge(sem("blk_col"), 1)

            def blocks(i, us):
                for u in us:
                    pe.wait_ge(sem(f"rows{u}"), 16 * (i + 1))
                    freed(pe, sem("gT"), 2 * i)
                    halves(lambda k: psum[u][0:HALF, k, FF // 2:512], grow[u], "b_gT")
                at = [pe.value_load(blk_col[0:1, bass.ds(2 * i + u, 1)], min_val=0, max_val=(NE - 1) * WCOL) for u in us]
                for u in us:
                    pe.wait_ge(sem("gT"), 2 * i + u + 1)
                    freed(pe, sem("hid"), 2 * i)
                    for half in range(2):
                        for k in range(2):
                            last = T.matmul(psum[u][:, half, 0:FF // 2], gT[u][0:HALF, k * P:(k + 1) * P],
                                            weights[0:HALF, bass.ds(at[u] + k * FF + half * (FF // 2), FF // 2)],
                                            start=k == 0, stop=k == 1)
                    last.then_inc(sem("b_hid"), 1)
                for u in us:
                    pe.wait_ge(sem("hid"), 2 * i + u + 1)
                    freed(pe, sem("res"), 2 * i)
                    for c in range(FC):
                        last = T.transpose(psum[u][:, 2 + c // 4, (c % 4) * P:(c % 4 + 1) * P], hid[u][:, c * P:(c + 1) * P], ident[:, :])
                    last.then_inc(sem("b_hT"), 1)
                for u in us:
                    pe.wait_ge(sem("hidT"), 2 * i + u + 1)
                    for c in range(FC):
                        last = T.matmul(psum[u][:, 3, Y0:Y0 + D], hidT[u][:, c * P:(c + 1) * P],
                                        weights[:, bass.ds(at[u] + 2 * FF + c * D, D)], start=c == 0, stop=c == FC - 1)
                    last.then_inc(sem("b_y"), 1)

            pairs(pe, lambda i: blocks(i, (0, 1)), NBLK // 2)
            blocks(NBLK // 2, (0,))


def kernel(**inputs):
    import numpy as np
    import concourse.bacc as bacc
    from concourse.bass_utils import run_bass_kernel_spmd

    a = {k: np.asarray(v) for k, v in inputs.items()}
    tok = "L0_tok_"
    ids = [a["x"], a["itok_BS_0_9999"], a["itok_BS_0_2047"], a["itok_BS_0_15"], a["itok_BS_0_3"]]
    arrays = {
        "ids": np.stack([x.T for x in ids]),
        "taus": np.stack([a["fside_BS_age_tau"].T, a["fside_BS_delays_tau"].T]),
        "word_table": a[tok + "word_table"],
        "npi_table": a[tok + "npi_table"],
        "posi_table": a[tok + "posi_table"],
        "modal_table": a[tok + "modalities_table"],
        "seg_table": a[tok + "seg_table"],
        "ln_gamma": a[tok + "ln_gamma"],
        "ln_beta": a[tok + "ln_beta"],
        "qkv_wT": a["L0_attn_qkv_w"].T,
        "qkv_b": a["L0_attn_qkv_b"],
        "proj_wT": a["L0_attn_proj_w"].T,
        "proj_b": a["L0_attn_proj_b"],
        "q_norm_w": a["L0_attn_q_norm_w"],
        "k_norm_w": a["L0_attn_k_norm_w"],
        "ln_w": a["L0_ffn_ln_w"],
        "w_router": a["L0_ffn_w_router"],
        "wi": a["L0_ffn_wi"],
        "wo": a["L0_ffn_wo"],
    }
    for k in ("age", "delay"):
        arrays |= {k + x: a[tok + k + x].reshape(-1) for x in ("_w", "_b", "_w0", "_b0")}
    arrays = {"in_" + k: np.ascontiguousarray(v) for k, v in arrays.items()}

    nc = bacc.Bacc("TRN2", target_bir_lowering=False, num_devices=1)
    t = {k[3:]: nc.dram_tensor(k, v.shape, mybir.dt.from_np(v.dtype), kind="ExternalInput").ap()
         for k, v in arrays.items()}
    out = nc.dram_tensor("tower_out", [NSEQ * P, D], F32, kind="ExternalOutput").ap()
    tower_kernel(nc, t, out)
    r = run_bass_kernel_spmd(nc, [arrays], core_ids=[0])
    return r.results[0]["tower_out"].reshape(NSEQ, P, D)
```

```python
from contextlib import ExitStack

import concourse.bass as bass
from concourse import mybir

F32 = mybir.dt.float32
BF16 = mybir.dt.bfloat16
I32 = mybir.dt.int32
U32 = mybir.dt.uint32
ALU = mybir.AluOpType
ACT = mybir.ActivationFunctionType
AX = mybir.AxisListType.X

P = 128
NSEQ = 16
D = 192
HALF = D // 2
HEADS = 12
HD = D // HEADS
GROUPS = 3
CHUNKS = HEADS // GROUPS
HPAD = 32
NE = 16
CAP = 64
FF = 768
FC = FF // P
SLOTS = NSEQ * CAP
SPLIT = SLOTS // P
NLISTS = NE * SPLIT
WCOL = 2 * FF + FC * D
GW = GROUPS * HPAD
MODAL_V, SEG_V, WORD_V, NPI_V, POS_V = 16, 4, 8000, 2500, 512
T2V = D - 1
NPAIR = NSEQ // 2
NBLK = (NSEQ * P - NE) // P + NE
ROW = 2 * D + 1
BIG = float(1 << 20)
RSQRT_BITS = 1597463007.0
ROUND = 12582912.0
TWO_PI = 6.283185307179586
TWO_PI_HI = 6.28125
TWO_PI_LO = TWO_PI - TWO_PI_HI
PI_BELOW = 3.1415925
LN_EPS, NORM_EPS, RMS_EPS = 1e-12, 1e-5, 1e-6
SHARED = 5512
ARENA_FIRST = 11


def tower_kernel(nc, t, out):
    assert NBLK == 31
    ctx = ExitStack()
    with ctx:
        def sb(name, shape, dt=F32):
            return ctx.enter_context(nc.sbuf_tensor(name, shape, dt))

        sems = {}

        def sem(name):
            if name not in sems:
                sems[name] = ctx.enter_context(nc.semaphore("s_" + name))
            return sems[name]

        weights = sb("weights", [P, NE * WCOL])
        w_by_expert = weights[:, :].rearrange("p (e c) -> p e c", e=NE)
        shared = sb("shared", [P, SHARED])

        def carver(ap, start, end):
            at = [start]

            def carve(cols):
                a = at[0]
                at[0] += cols
                assert at[0] <= end, (at[0], end)
                return ap[:, a:a + cols]

            return carve

        arena = carver(weights, ARENA_FIRST * WCOL, NE * WCOL)
        share_a = carver(shared, 0, SHARED)
        share_b = carver(shared, 0, SHARED)

        h_all = arena(NSEQ * D)
        terms = [arena(6 * D) for _ in range(2)]
        turns = [arena(2 * D) for _ in range(2)]
        xn = [arena(D) for _ in range(2)]
        xT = [arena(2 * P) for _ in range(2)]
        qk_pad = [arena(2 * HEADS * HPAD) for _ in range(2)]
        v_aug = [arena(HEADS * (HD + 1)) for _ in range(2)]
        kT = [arena(CHUNKS * P) for _ in range(2)]
        qT = [arena(CHUNKS * P) for _ in range(2)]
        kT16 = [arena(CHUNKS * P // 2).bitcast(BF16) for _ in range(2)]
        qT16 = [arena(CHUNKS * P // 2).bitcast(BF16) for _ in range(2)]
        squares = [arena(2 * D) for _ in range(2)]
        oT = [arena(2 * P) for _ in range(2)]
        nT = oT
        probsT = [share_a(HEADS * P) for _ in range(2)]
        row = [share_a(ROW) for _ in range(2)]
        h1 = [share_a(D) for _ in range(2)]
        x2 = [share_a(D) for _ in range(2)]
        o_sb = [share_a(D) for _ in range(2)]

        grow = [share_b(ROW) for _ in range(4)]
        gT = [share_b(2 * P) for _ in range(2)]
        hid = [share_b(FF) for _ in range(2)]
        hidT = [share_b(FC * P) for _ in range(2)]
        res = [share_b(D) for _ in range(2)]

        ident = sb("ident", [P, P])
        identb = sb("identb", [P, 2, P], BF16)
        wqkv = sb("wqkv", [HALF + 1, 2, 3 * D])
        wproj = sb("wproj", [HALF + 1, 2, D])
        wrout = sb("wrout", [HALF, 2, NE])
        gamma_bc = sb("gamma_bc", [P, D])
        beta_bc = sb("beta_bc", [P, D])
        lnw_bc = sb("lnw_bc", [P, D])
        t2v_w = sb("t2v_w", [P, 2, D])
        t2v_b = sb("t2v_b", [P, 2, D])
        tau = sb("tau", [P, 2, NSEQ])
        ids = sb("ids", [P, NSEQ, 4], I32)
        pair_table = shared[0:MODAL_V * SEG_V, 0:2 * D]
        rawid = shared[:, 2 * D:2 * D + 5 * NSEQ].bitcast(I32).rearrange("p (k n) -> p k n", k=5)
        wrapped = shared[:, 2 * D + 5 * NSEQ:2 * D + 10 * NSEQ].rearrange("p (k n) -> p k n", k=5)
        qk_scale = sb("qk_scale", [P, 2])
        mhalf = sb("mhalf", [P, 1])
        expert_iota = sb("expert_iota", [P, NE])
        token_iota = sb("token_iota", [P, NSEQ])
        small = [sb(f"small{u}", [P, 160]) for u in range(2)]
        ms_qk = sb("ms_qk", [P, 2, 2 * HEADS])
        rs_qk = sb("rs_qk", [P, 2, 2 * HEADS])
        nr_qk = sb("nr_qk", [P, 2, 2 * HEADS])
        idx4 = [sb(f"idx4{u}", [P, 4], I32) for u in range(2)]
        slot_i = [sb(f"slot_i{u}", [P, 1], I32) for u in range(2)]
        top_i = [sb(f"top_i{u}", [P, 8], U32) for u in range(2)]
        onehot16 = [sb(f"onehot16{u}", [P, NE], BF16) for u in range(2)]
        total = sb("total", [P, NE])
        tokens = sb("tokens", [P, NLISTS])
        tok_col = [sb(f"tok_col{u}", [P, 1]) for u in range(2)]
        list_edge = sb("list_edge", [P, SPLIT])
        plan = shared[:, 1024:1424]
        blk_idx = sb("blk_idx", [P, NBLK])
        blk_pen = sb("blk_pen", [P, NBLK])
        blk_col = sb("blk_col", [P, NBLK], I32)
        blk_list = sb("blk_list", [P, NBLK], I32)
        gidx = [sb(f"gidx{k}", [P, 1], I32) for k in range(4)]
        oidx = [sb(f"oidx{u}", [P, 1], I32) for u in range(2)]

        psum = [ctx.enter_context(nc.psum_tensor(f"psum{u}", [P, 4, 512], F32)) for u in range(2)]
        psum_s = [psum[u][:, 0:3, :] for u in range(2)]
        psum_m = [psum[u][:, 3, :] for u in range(2)]

        def cols(tile, start, n):
            return tile[:, start:start + n]

        STATS, MV, RSTD1, MV2, RSTD2, MV3, RSTD3, SSQ, RSTDN = 0, 8, 10, 12, 14, 16, 18, 20, 22
        NMR1, NMR2, NMR3, STATS3, RSUM, TOP, NEGTOP, EXPS, ZSUM, ONEH, SCR = 24, 25, 26, 28, 72, 84, 92, 93, 109, 110, 126
        TOPF, PRIO, BASE, KEEP, DEST, SPLITNO = 144, 145, 146, 147, 148, 149

        pair_dram = nc.dram_tensor("pair_rows", [MODAL_V * SEG_V, D], F32).ap()
        rows = nc.dram_tensor("token_rows", [NSEQ * P, ROW], F32).ap()
        lists = nc.dram_tensor("expert_lists", [P * NLISTS, 1], F32).ap()

        def freed(eng, semaphore, value):
            if not isinstance(value, int) or value > 0:
                eng.wait_ge(semaphore, value)

        def seqs(i):
            return [(u, 2 * i + u) for u in range(2)]

        def phase_b(eng, blocks):
            both = (0, 1)
            blocks(0, 0, both, both)
            blocks(1, 2, both, both)
            with eng.Fori(1, NBLK // 4 - 1) as d:
                blocks(2 * d, 0, both, both)
                blocks(2 * d + 1, 2, both, both)
            blocks(NBLK // 2 - 3, 0, both, both)
            blocks(NBLK // 2 - 2, 2, both, (0,))
            blocks(NBLK // 2 - 1, 0, both, ())
            blocks(NBLK // 2, 2, (0,), ())

        def next_blocks(q):
            if isinstance(q, int) and q >= NBLK // 2 - 1:
                return (0,) if q == NBLK // 2 - 1 else ()
            return (0, 1)

        def phase_a(eng, tok, front, back, route):
            tok(0)
            front(0)
            tok(1)
            back(0, True, True, False)
            with eng.Fori(1, NPAIR - 2) as i:
                back(i, True, True, True)
            back(NPAIR - 2, True, False, True)
            back(NPAIR - 1, False, False, True)
            route(NPAIR - 1)

        EARLY = 4
        N_CONST = 19
        LG = 0
        Y0 = 256

        block = ctx.enter_context(nc.Block())

        @block.sync
        def _(sp):
            def const(dst, src):
                sp.dma_start(dst, src).then_inc(sem("const"), 16)

            const(pair_table[:, 0:D], t["modal_table"].unsqueeze(1).broadcast_to([MODAL_V, SEG_V, D]))
            for m in range(MODAL_V):
                sp.dma_start(pair_table[m * SEG_V:(m + 1) * SEG_V, D:2 * D], t["seg_table"]).then_inc(sem("seg"), 16)
            const(rawid[:, :, :], t["ids"].rearrange("k p n -> p k n"))
            const(tau[:, :, :], t["taus"].rearrange("k p n -> p k n"))
            for k, a in enumerate(("age", "delay")):
                for tile, x, x0 in ((t2v_w, "_w", "_w0"), (t2v_b, "_b", "_b0")):
                    const(tile[:, k, 0:T2V], t[a + x].partition_broadcast(P))
                    const(tile[:, k, T2V:D], t[a + x0].partition_broadcast(P))
            const(gamma_bc[:, :], t["ln_gamma"].partition_broadcast(P))
            const(beta_bc[:, :], t["ln_beta"].partition_broadcast(P))
            const(lnw_bc[:, :], t["ln_w"].partition_broadcast(P))
            sp.wait_ge(sem("memset"), 3)
            const(wqkv[0:HALF, :, :], t["qkv_wT"].rearrange("(k p) f -> p k f", p=HALF))
            const(wqkv[HALF:HALF + 1, 1, :], t["qkv_b"].unsqueeze(0))
            const(wproj[0:HALF, :, :], t["proj_wT"].rearrange("(k p) f -> p k f", p=HALF))
            const(wproj[HALF:HALF + 1, 1, :], t["proj_b"].unsqueeze(0))
            const(wrout[:, :, :], t["w_router"].rearrange("(k p) f -> p k f", p=HALF))
            for g in range(P // HPAD):
                for j, name in enumerate(("q_norm_w", "k_norm_w")):
                    sp.dma_start(qk_scale[g * HPAD:g * HPAD + HD, j:j + 1], t[name].unsqueeze(1)).then_inc(sem("qkw"), 16)

            sp.wait_ge(sem("zeroed"), 1)
            sp.dma_start(lists.rearrange("(p q) o -> p (q o)", p=P), tokens[:, :]).then_inc(sem("lists0"), 16)
            sp.wait_ge(sem("pair_sum"), 1)
            sp.dma_start(pair_dram, pair_table[:, 0:D]).then_inc(sem("pair_stored"), 16)

            def load_expert(e):
                sp.dma_start(w_by_expert[0:HALF, e, 0:2 * FF].rearrange("p (k f) -> p k f", k=2),
                             t["wi"][e].rearrange("(k p) f -> p k f", p=HALF)).then_inc(sem("weights"), 16)
                sp.dma_start(w_by_expert[:, e, 2 * FF:WCOL].rearrange("p (k f) -> p k f", k=FC),
                             t["wo"][e].rearrange("(k p) f -> p k f", p=P)).then_inc(sem("weights"), 16)

            def load_expert_at(e):
                at = e * WCOL
                sp.dma_start(weights[0:HALF, bass.ds(at, 2 * FF)].rearrange("p (k f) -> p k f", k=2),
                             t["wi"][bass.ds(e, 1), :, :].rearrange("o (k p) f -> p (o k) f", p=HALF)).then_inc(sem("weights"), 16)
                sp.dma_start(weights[:, bass.ds(at + 2 * FF, FC * D)].rearrange("p (k f) -> p k f", k=FC),
                             t["wo"][bass.ds(e, 1), :, :].rearrange("o (k p) f -> p (o k) f", p=P)).then_inc(sem("weights"), 16)

            def store_and_load(i, experts):
                for u, n in seqs(i):
                    sp.wait_ge(sem("out0"), n + 1)
                    sp.dma_start(out[bass.ds(n * P, P), :], x2[u]).then_inc(sem("out_plain"), 16)
                    sp.dma_start(rows[bass.ds(n * P, P), :], row[u]).then_inc(sem("out_plain"), 16)
                for e in experts:
                    load_expert_at(e)

            sp.wait_ge(sem("xn"), 2)
            for e in range(EARLY):
                load_expert_at(e)
            with sp.Fori(0, ARENA_FIRST - EARLY) as i:
                store_and_load(i, [i + EARLY])
            for i in range(ARENA_FIRST - EARLY, NPAIR):
                store_and_load(i, [])
            sp.wait_ge(sem("out_plain"), 32 * NSEQ)
            sp.wait_ge(sem("listed"), 16 * NSEQ)
            sp.dma_start(tokens[:, :], lists.rearrange("(p q) o -> p (q o)", p=P)).then_inc(sem("tokens"), 16)
            for e in range(ARENA_FIRST, NE):
                load_expert(e)
            sp.wait_ge(sem("scattered0"), 16 * ((NBLK + 1) // 2))
            sp.wait_ge(sem("scattered1"), 16 * (NBLK // 2))

        @block.gpsimd
        def _(pool):
            turn = {name: pool.alloc_register("turn_" + name) for name in ("idx4", "rp", "dest", "gidx", "res")}
            for name, first in (("idx4", 7), ("rp", 1), ("dest", 1), ("gidx", 9), ("res", 5)):
                pool.reg_mov(turn[name], first)

            def arrived(name, value):
                if isinstance(value, int):
                    pool.wait_ge(sem(name), value)
                else:
                    pool.wait_ge(sem(name), turn[name])
                    pool.reg_add(turn[name], turn[name], 1)

            nc.gpsimd.memset(ident[:, :], 0.0).then_inc(sem("g"), 1)
            nc.gpsimd.memset(identb[:, :, :], 1.0).then_inc(sem("g"), 1)
            pool.wait_ge(sem("g"), 2)
            nc.gpsimd.affine_select(out=ident[:, :], in_=ident[:, :], compare_op=ALU.not_equal, fill=1.0,
                                    base=0, pattern=[[-1, P]], channel_multiplier=1).then_inc(sem("ident"), 1)
            nc.gpsimd.affine_select(out=identb[:, 0, :], in_=identb[:, 0, :], compare_op=ALU.is_ge, fill=0.0,
                                    base=0, pattern=[[1, P]], channel_multiplier=-1).then_inc(sem("ident"), 1)
            nc.gpsimd.memset(mhalf[:, :], -0.5).then_inc(sem("g"), 1)
            nc.gpsimd.iota(expert_iota[:, :], [[1, NE]], base=0, channel_multiplier=0,
                           allow_small_or_imprecise_dtypes=True).then_inc(sem("ident"), 1)
            nc.gpsimd.iota(token_iota[:, :], [[P, NSEQ]], base=0, channel_multiplier=1,
                           allow_small_or_imprecise_dtypes=True).then_inc(sem("ident"), 1)
            nc.gpsimd.iota(list_edge[:, :], [[P, SPLIT]], base=P, channel_multiplier=0,
                           allow_small_or_imprecise_dtypes=True).then_inc(sem("ident"), 1)
            nc.gpsimd.iota(blk_idx[:, :], [[1, NBLK]], base=0, channel_multiplier=0,
                           allow_small_or_imprecise_dtypes=True).then_inc(sem("ident"), 1)
            pool.wait_ge(sem("pair_stored"), 16)
            pool.wait_ge(sem("lists0"), 16)

            G = nc.gpsimd

            def gather_tables(i, u):
                n = 2 * i + u
                freed(pool, sem("summed"), 2 * i)
                G.tensor_copy(idx4[u][:, :], ids[:, bass.ds(n, 1), :].rearrange("p a k -> p (a k)")).then_inc(sem("idx4"), 1)
                arrived("idx4", n + 1)
                for k, table in enumerate((t["word_table"], t["npi_table"], t["posi_table"], pair_dram)):
                    G.indirect_dma_start(
                        out=terms[u][:, k * D:(k + 1) * D], out_offset=None, in_=table,
                        in_offset=bass.IndirectOffsetOnAxis(ap=idx4[u][:, k:k + 1], axis=0),
                    ).then_inc(sem(f"gathered{u}"), 16)

            def power(i, src, made, done):
                for u, n in seqs(i):
                    pool.wait_ge(sem(made), n + 1)
                    G.tensor_tensor(cols(small[u], src[1], 1), cols(small[u], src[0], 1), mhalf[:, :], ALU.pow).then_inc(sem(done), 1)

            def embed(i):
                power(i, (MV + 1, RSTD1), "var1", "rstd1")
                for u, n in seqs(i):
                    h = h_all[:, bass.ds(n * D, D)]
                    pool.wait_ge(sem("ident"), 6)
                    pool.wait_ge(sem("ln1a"), n + 1)
                    G.tensor_tensor(h, h, gamma_bc[:, :], ALU.mult).then_inc(sem("ln1b"), 1)
                for u, n in seqs(i):
                    h = h_all[:, bass.ds(n * D, D)]
                    pool.wait_ge(sem("ident"), 6)
                    pool.wait_ge(sem("ln1b"), n + 1)
                    G.tensor_tensor(h, h, beta_bc[:, :], ALU.add).then_inc(sem("h"), 1)
                power(i, (MV2 + 1, RSTD2), "var2", "rstd2")

            def enlist(i, u):
                n = 2 * i + u
                arrived("rp", n + 1)
                G.tensor_scalar(x2[u], row[u][:, 0:D], row[u][:, 2 * D:2 * D + 1], None, ALU.mult).then_inc(sem("rp_n"), 1)
                pool.wait_ge(sem("rp_n"), n + 1)
                G.tensor_tensor(x2[u], x2[u], row[u][:, D:2 * D], ALU.add).then_inc(sem("out0"), 1)
                arrived("dest", n + 1)
                G.indirect_dma_start(
                    out=lists, out_offset=bass.IndirectOffsetOnAxis(ap=slot_i[u][:, :], axis=0),
                    in_=tok_col[u][:, :], in_offset=None, bounds_check=P * NLISTS - 1, oob_is_err=False,
                ).then_inc(sem("listed"), 16)

            def tok(i):
                gather_tables(i, 0)
                gather_tables(i, 1)
                embed(i)

            def route(i):
                for u in range(2):
                    enlist(i, u)

            def back(i, with_front, with_tok, with_route):
                if with_tok:
                    gather_tables(i + 2, 0)
                if with_route:
                    enlist(i - 1, 0)
                    enlist(i - 1, 1)
                if with_tok:
                    gather_tables(i + 2, 1)
                power(i, (MV3 + 1, RSTD3), "var3", "rstd3")
                for u, n in seqs(i):
                    pool.wait_ge(sem("x2"), n + 1)
                    G.tensor_tensor(row[u][:, D:2 * D], x2[u], h1[u], ALU.add).then_inc(sem("base"), 1)
                power(i, (SSQ, RSTDN), "ssq_e", "rstdn")
                if with_tok:
                    embed(i + 2)

            pool.wait_ge(sem("g"), 3)
            pool.wait_ge(sem("ids"), 2)
            pool.wait_ge(sem("const"), 16 * N_CONST)
            phase_a(pool, tok, lambda i: None, back, route)

            pool.wait_ge(sem("listed"), 16 * NSEQ)
            pool.wait_ge(sem("out_plain"), 32 * NSEQ)

            def gather_rows(q, k0, us):
                for u in us:
                    arrived("gidx", 2 * q + u + 1)
                    G.indirect_dma_start(
                        out=grow[k0 + u], out_offset=None, in_=rows,
                        in_offset=bass.IndirectOffsetOnAxis(ap=gidx[k0 + u][:, :], axis=0),
                    ).then_inc(sem(f"rows{k0 + u}"), 16)

            def blocks(q, k0, us, ahead):
                for u in us:
                    arrived("res", 2 * q + u + 1)
                    G.indirect_dma_start(
                        out=out, out_offset=bass.IndirectOffsetOnAxis(ap=oidx[u][:, :], axis=0),
                        in_=res[u], in_offset=None, bounds_check=NSEQ * P - 1, oob_is_err=False,
                    ).then_inc(sem(f"scattered{u}"), 16)
                gather_rows(q + 2, k0, ahead)

            gather_rows(0, 0, (0, 1))
            gather_rows(1, 2, (0, 1))
            phase_b(pool, blocks)

        @block.scalar
        def _(act):
            S = nc.scalar

            def normalize(dst, src, u, rstd, nmr):
                return S.activation(dst, src, ACT.Identity, scale=cols(small[u], rstd, 1), bias=cols(small[u], nmr, 1))

            def sines(i):
                for u, n in seqs(i):
                    r = turns[u].rearrange("p (k d) -> p k d", k=2)
                    a = terms[u][:, 4 * D:6 * D].rearrange("p (k d) -> p k d", k=2)
                    act.wait_ge(sem("reduced"), n + 1)
                    S.activation(a[:, :, 0:T2V], r[:, :, 0:T2V], ACT.Sin).then_inc(sem("sin"), 1)

            def ln1(i):
                for u, n in seqs(i):
                    h = h_all[:, bass.ds(n * D, D)]
                    act.wait_ge(sem("nmr1"), n + 1)
                    normalize(h, h, u, RSTD1, NMR1).then_inc(sem("ln1a"), 1)

            def attn_in(i):
                for u, n in seqs(i):
                    act.wait_ge(sem("nmr2"), n + 1)
                    freed(act, sem("p_xT"), 2 * i)
                    normalize(xn[u], h_all[:, bass.ds(n * D, D)], u, RSTD2, NMR2).then_inc(sem("xn"), 1)

            def turn_x(i, u):
                act.wait_ge(sem("p_xT"), 2 * i + u + 1)
                S.copy(xT[u][0:HALF, :], psum_s[u][0:HALF, 2, 0:2 * P]).then_inc(sem("xT"), 1)

            def squared(i):
                for u, n in seqs(i):
                    act.wait_ge(sem("p_qkv"), n + 1)
                    freed(act, sem("ssqk0"), 2 * i)
                    S.activation(squares[u], psum_s[u][:, 0, 0:2 * D], ACT.Square).then_inc(sem("sq"), 1)

            def values(i):
                for u, n in seqs(i):
                    act.wait_ge(sem("p_qkv"), n + 1)
                    freed(act, sem("p_pv"), 2 * i)
                    S.copy(v_aug[u].rearrange("p (h d) -> p h d", d=HD + 1)[:, :, 0:HD],
                           psum_s[u][:, 1, 0:D].rearrange("p (h d) -> p h d", d=HD)).then_inc(sem("v"), 1)

            def turn_qk(i):
                for u, n in seqs(i):
                    act.wait_ge(sem("p_kT"), n + 1)
                    S.copy(kT16[u][0:GW, :], psum_s[u][0:GW, 2, :]).then_inc(sem("kT16"), 1)
                    act.wait_ge(sem("p_qT0"), n + 1)
                    S.activation(qT16[u][0:GW, :], psum_s[u][0:GW, 1, :], ACT.Copy, scale=qk_scale[0:GW, 0:1]).then_inc(sem("qT16"), 1)
                    S.copy(kT[u][0:GW, :], psum_s[u][0:GW, 2, :]).then_inc(sem("kT"), 1)

            def turn_q(i):
                for u, n in seqs(i):
                    act.wait_ge(sem("p_qT1"), n + 1)
                    S.activation(qT[u][0:GW, :], psum_s[u][0:GW, 0, :], ACT.Copy, scale=qk_scale[0:GW, 0:1]).then_inc(sem("qT"), 1)

            def front(i):
                attn_in(i)
                turn_x(i, 0)
                turn_x(i, 1)
                squared(i)
                values(i)
                turn_qk(i)
                turn_q(i)

            def tok(i):
                sines(i)
                ln1(i)

            def route(i):
                for u, n in seqs(i):
                    act.wait_ge(sem("negtop"), n + 1)
                    act.wait_ge(sem("topi"), n + 1)
                    S.activation(cols(small[u], EXPS, NE), psum_m[u][:, LG:LG + NE], ACT.Exp,
                                 bias=cols(small[u], NEGTOP, 1), accum_out=cols(small[u], ZSUM, 1)).then_inc(sem("zsum"), 1)

            def back(i, with_front, with_tok, with_route):
                if with_front:
                    attn_in(i + 1)
                for u, n in seqs(i):
                    if u == 1 and with_route:
                        route(i - 1)
                    act.wait_ge(sem("p_sT"), n + 1)
                    S.activation(probsT[u], psum_s[u].rearrange("p b c -> p (b c)"), ACT.Exp).then_inc(sem("probs"), 1)
                if with_front:
                    turn_x(i + 1, 0)
                    turn_x(i + 1, 1)
                    squared(i + 1)
                for u, n in seqs(i):
                    act.wait_ge(sem("p_oT"), n + 1)
                    S.copy(oT[u][0:HALF, :], psum_m[u][0:HALF, 2 * P:4 * P]).then_inc(sem("oT"), 1)
                if with_front:
                    values(i + 1)
                    turn_qk(i + 1)
                if with_tok:
                    sines(i + 2)
                for u, n in seqs(i):
                    act.wait_ge(sem("nmr3"), n + 1)
                    freed(act, sem("out_plain"), 64 * i)
                    normalize(x2[u], h1[u], u, RSTD3, NMR3).then_inc(sem("x2"), 1)
                for u, n in seqs(i):
                    act.wait_ge(sem("x2"), n + 1)
                    S.activation(o_sb[u], x2[u], ACT.Square, accum_out=cols(small[u], SSQ + 1, 1)).then_inc(sem("ssq"), 1)
                if with_front:
                    turn_q(i + 1)
                for u, n in seqs(i):
                    act.wait_ge(sem("p_nT"), n + 1)
                    S.copy(nT[u][0:HALF, :], psum_m[u][0:HALF, 2 * P:4 * P]).then_inc(sem("nT"), 1)
                if with_tok:
                    ln1(i + 2)

            act.wait_ge(sem("const"), 16 * N_CONST)
            act.wait_ge(sem("qk_part"), 4)
            phase_a(act, tok, front, back, route)

            def turn_rows(q, us, u):
                if u in us:
                    act.wait_ge(sem("b_gT"), 2 * q + u + 1)
                    S.copy(gT[u][0:HALF, :].rearrange("p (k c) -> p k c", k=2),
                           psum[u][0:HALF, 0:2, FF // 2:512]).then_inc(sem("gT"), 1)

            def relu(q, u):
                act.wait_ge(sem("b_hid"), 2 * q + u + 1)
                S.activation(hid[u].rearrange("p (k f) -> p k f", k=2), psum[u][:, 0:2, 0:FF // 2], ACT.Relu).then_inc(sem("hid"), 1)

            def blocks(q, k0, us, ahead):
                after = next_blocks(q)
                for u in us:
                    relu(q, u)
                for u in after:
                    turn_rows(q + 1, after, u)

            turn_rows(0, (0, 1), 0)
            turn_rows(0, (0, 1), 1)
            phase_b(act, blocks)

        @block.vector
        def _(dve):
            V = nc.vector
            logit_turn = dve.alloc_register("turn_logit")
            dve.reg_mov(logit_turn, 1)

            for u in range(2):
                V.memset(qk_pad[u], 0.0).then_inc(sem("pad0"), 1)
                for tile in (xT[u], oT[u]):
                    V.memset(tile[HALF:HALF + 1, :], 1.0).then_inc(sem("ones"), 1)
                V.memset(v_aug[u].rearrange("p (h d) -> p h d", d=HD + 1)[:, :, HD:HD + 1], 1.0).then_inc(sem("ones"), 1)
            V.memset(tokens[:, :], 0.0).then_inc(sem("zeroed"), 1)
            V.memset(total[:, :], 0.0).then_inc(sem("total"), 1)
            V.memset(qk_scale[:, :], -1.0).then_inc(sem("memset"), 1)
            V.memset(wqkv[HALF:HALF + 1, 0, :], 0.0).then_inc(sem("memset"), 1)
            V.memset(wproj[HALF:HALF + 1, 0, :], 0.0).then_inc(sem("memset"), 1)
            dve.wait_ge(sem("pad0"), 2)
            for u in range(2):
                kp = qk_pad[u].rearrange("p (h d) -> p h d", d=HPAD)
                V.memset(kp[:, HEADS:2 * HEADS, HD:HD + 1], 1.0).then_inc(sem("pad1"), 1)
            dve.wait_ge(sem("const"), 16 * N_CONST)
            dve.wait_ge(sem("seg"), 16 * MODAL_V)
            pt = pair_table
            V.tensor_tensor(pt[:, 0:D], pt[:, 0:D], pt[:, D:2 * D], ALU.add).then_inc(sem("pair_sum"), 1)
            for k, rows in enumerate((WORD_V, NPI_V, POS_V, MODAL_V, SEG_V)):
                V.tensor_scalar(wrapped[:, k, :], rawid[:, k, :], 0.0, float(rows), ALU.is_lt, ALU.mult).then_inc(sem("wrap"), 1)
                dve.wait_ge(sem("wrap"), 3 * k + 1)
                V.tensor_tensor(wrapped[:, k, :], wrapped[:, k, :], rawid[:, k, :], ALU.add).then_inc(sem("wrap"), 1)
                dve.wait_ge(sem("wrap"), 3 * k + 2)
                V.tensor_scalar(wrapped[:, k, :], wrapped[:, k, :], 0.0, float(rows - 1), ALU.max, ALU.min).then_inc(sem("wrap"), 1)
            dve.wait_ge(sem("wrap"), 15)
            V.tensor_copy(ids[:, :, 0:3], wrapped[:, 0:3, :].rearrange("p k n -> p n k")).then_inc(sem("ids"), 1)
            V.scalar_tensor_tensor(ids[:, :, 3], wrapped[:, 3, :], float(SEG_V), wrapped[:, 4, :], ALU.mult, ALU.add).then_inc(sem("ids"), 1)
            dve.wait_ge(sem("qkw"), 16 * 8)
            for g in range(P // HPAD):
                a = qk_scale[g * HPAD:g * HPAD + HD, :]
                V.scalar_tensor_tensor(a[:, 0:1], a[:, 0:1], HD ** -0.5, a[:, 1:2], ALU.mult, ALU.mult).then_inc(sem("qk_part"), 1)
            dve.wait_ge(sem("qk_part"), 4)
            dve.wait_ge(sem("ident"), 6)

            def reduce_args(i):
                a = [terms[u][:, 4 * D:6 * D].rearrange("p (k d) -> p k d", k=2) for u in range(2)]
                for u, n in seqs(i):
                    freed(dve, sem("summed"), 2 * i)
                    freed(dve, sem("xn"), 2 * i)
                    for k in range(2):
                        V.scalar_tensor_tensor(a[u][:, k, :], t2v_w[:, k, :], tau[:, k, bass.ds(n, 1)], t2v_b[:, k, :],
                                               ALU.mult, ALU.add).then_inc(sem("arg"), 1)
                r = [turns[u].rearrange("p (k d) -> p k d", k=2) for u in range(2)]
                for u, n in seqs(i):
                    dve.wait_ge(sem("arg"), 2 * n + 2)
                    freed(dve, sem("sin"), 2 * i)
                    V.tensor_scalar(r[u], a[u], 1.0 / TWO_PI, ROUND, ALU.mult, ALU.add).then_inc(sem("turn0"), 1)
                for u, n in seqs(i):
                    dve.wait_ge(sem("turn0"), n + 1)
                    V.tensor_scalar(r[u], r[u], ROUND, None, ALU.subtract).then_inc(sem("turn1"), 1)
                for u, n in seqs(i):
                    x = a[u][:, :, 0:T2V]
                    dve.wait_ge(sem("turn1"), n + 1)
                    V.scalar_tensor_tensor(x, r[u][:, :, 0:T2V], -TWO_PI_HI, x, ALU.mult, ALU.add).then_inc(sem("turn2"), 1)
                for u, n in seqs(i):
                    x, y = a[u][:, :, 0:T2V], r[u][:, :, 0:T2V]
                    dve.wait_ge(sem("turn2"), n + 1)
                    V.scalar_tensor_tensor(y, y, -TWO_PI_LO, x, ALU.mult, ALU.add).then_inc(sem("turn3"), 1)
                for u, n in seqs(i):
                    y = r[u][:, :, 0:T2V]
                    dve.wait_ge(sem("turn3"), n + 1)
                    V.tensor_scalar(y, y, PI_BELOW, -PI_BELOW, ALU.min, ALU.max).then_inc(sem("reduced"), 1)

            def variance(i, src, source, made, stats_at, mv_at, eps, tag):
                for u, n in seqs(i):
                    dve.wait_ge(sem("ident"), 6)
                    dve.wait_ge(sem(source), n + 1)
                    V.bn_stats(cols(small[u], stats_at, 6), src(u, n)).then_inc(sem("stats" + tag), 1)
                for u, n in seqs(i):
                    dve.wait_ge(sem("ident"), 6)
                    dve.wait_ge(sem("stats" + tag), n + 1)
                    V.bn_aggr(cols(small[u], mv_at, 2), cols(small[u], stats_at, 6)).then_inc(sem("mv" + tag), 1)
                for u, n in seqs(i):
                    v = cols(small[u], mv_at + 1, 1)
                    dve.wait_ge(sem("mv" + tag), n + 1)
                    V.tensor_scalar(v, v, eps, None, ALU.add).then_inc(sem(made), 1)

            def shift(i, mv_at, rstd_at, nmr_at, tag):
                for u, n in seqs(i):
                    s = small[u]
                    dve.wait_ge(sem("rstd" + tag), n + 1)
                    V.scalar_tensor_tensor(cols(s, nmr_at, 1), cols(s, mv_at, 1), -1.0, cols(s, rstd_at, 1),
                                           ALU.mult, ALU.mult).then_inc(sem("nmr" + tag), 1)

            def h_of(u, n):
                return h_all[:, bass.ds(n * D, D)]

            def sum_terms(i):
                for u, n in seqs(i):
                    dve.wait_ge(sem("sin"), n + 1)
                    dve.wait_ge(sem(f"gathered{u}"), 64 * (i + 1))
                    V.tensor_reduce(h_of(u, n), terms[u].rearrange("p (k d) -> p d k", k=6), AX, ALU.add).then_inc(sem("summed"), 1)
                variance(i, h_of, "summed", "var1", STATS, MV, LN_EPS, "1")

            def second_norm(i):
                variance(i, h_of, "h", "var2", STATS, MV2, NORM_EPS, "2")
                shift(i, MV2, RSTD2, NMR2, "2")

            def head_norm(i):
                for u, n in seqs(i):
                    dve.wait_ge(sem("sq"), n + 1)
                    V.tensor_reduce(ms_qk[:, u, :], squares[u].rearrange("p (h d) -> p h d", d=HD), AX, ALU.add).then_inc(sem("ssqk0"), 1)
                v, y, w = (x[:, :, :].rearrange("p u h -> p (u h)") for x in (ms_qk, rs_qk, nr_qk))
                dve.wait_ge(sem("ssqk0"), 2 * i + 2)
                V.tensor_scalar(v, v, 1.0 / HD, RMS_EPS, ALU.mult, ALU.add).then_inc(sem("ssqk"), 1)
                dve.wait_ge(sem("ssqk"), i + 1)
                V.tensor_scalar(y.bitcast(I32), v.bitcast(I32), -0.5, RSQRT_BITS, ALU.mult, ALU.add).then_inc(sem("guess"), 1)
                dve.wait_ge(sem("guess"), i + 1)
                for k in range(3):
                    V.scalar_tensor_tensor(w, y, -0.5, y, ALU.mult, ALU.mult).then_inc(sem("newton"), 1)
                    dve.wait_ge(sem("newton"), 9 * i + 3 * k + 1)
                    V.tensor_tensor(w, w, v, ALU.mult).then_inc(sem("newton"), 1)
                    dve.wait_ge(sem("newton"), 9 * i + 3 * k + 2)
                    V.scalar_tensor_tensor(y, w, 1.5, y, ALU.add, ALU.mult).then_inc(sem("newton"), 1)
                    dve.wait_ge(sem("newton"), 9 * i + 3 * k + 3)
                for u, n in seqs(i):
                    V.tensor_tensor(qk_pad[u].rearrange("p (h d) -> p h d", d=HPAD)[:, :, 0:HD],
                                    psum_s[u][:, 0, 0:2 * D].rearrange("p (h d) -> p h d", d=HD),
                                    rs_qk[:, u, :].unsqueeze(2).broadcast_to([P, 2 * HEADS, HD]), ALU.mult).then_inc(sem("qk"), 1)

            def guard(i):
                for u, n in seqs(i):
                    dve.wait_ge(sem("p_guard"), n + 1)
                    V.tensor_reduce(qk_pad[u][:, 0:CHUNKS * GW].rearrange("p (c g d) -> p g c d", c=CHUNKS, d=HPAD)[:, :, :, HD],
                                    psum_s[u].rearrange("p g (c m) -> p g c m", m=P), AX,
                                    ALU.max).then_inc(sem("guard"), 1)

            def attended(i):
                pv = [psum_m[u][:, 0:HEADS * (HD + 1)].rearrange("p (h d) -> p h d", d=HD + 1) for u in range(2)]
                for u, n in seqs(i):
                    dve.wait_ge(sem("p_pv"), n + 1)
                    freed(dve, sem("ssq"), 2 * i)
                    V.reciprocal(cols(small[u], RSUM, HEADS), pv[u][:, :, HD]).then_inc(sem("rsum"), 1)
                    dve.wait_ge(sem("rsum"), n + 1)
                    V.tensor_tensor(o_sb[u].rearrange("p (h d) -> p h d", d=HD), pv[u][:, :, 0:HD],
                                    cols(small[u], RSUM, HEADS).unsqueeze(2).broadcast_to([P, HEADS, HD]),
                                    ALU.mult).then_inc(sem("o"), 1)

            def residual(i):
                for u, n in seqs(i):
                    dve.wait_ge(sem("p_y"), n + 1)
                    freed(dve, sem("base"), 2 * i)
                    V.tensor_tensor(h1[u], psum_m[u][:, 0:D], h_of(u, n), ALU.add).then_inc(sem("h1"), 1)
                variance(i, lambda u, n: h1[u], "h1", "var3", STATS3, MV3, NORM_EPS, "3")
                shift(i, MV3, RSTD3, NMR3, "3")

            def experts_in(i):
                for u, n in seqs(i):
                    s = small[u]
                    dve.wait_ge(sem("ssq"), n + 1)
                    V.tensor_scalar(cols(s, SSQ, 1), cols(s, SSQ + 1, 1), 1.0 / D, RMS_EPS, ALU.mult, ALU.add).then_inc(sem("ssq_e"), 1)
                for u, n in seqs(i):
                    dve.wait_ge(sem("rstdn"), n + 1)
                    freed(dve, sem("out_plain"), 64 * i)
                    V.scalar_tensor_tensor(row[u][:, 0:D], x2[u], cols(small[u], RSTDN, 1), lnw_bc[:, :],
                                           ALU.mult, ALU.mult).then_inc(sem("normed"), 1)

            def choose(i):
                for u, n in seqs(i):
                    if isinstance(i, int):
                        dve.wait_ge(sem("p_logit"), n + 1)
                    else:
                        dve.wait_ge(sem("p_logit"), logit_turn)
                        dve.reg_add(logit_turn, logit_turn, 1)
                    V.max(cols(small[u], TOP, 8), psum_m[u][:, LG:LG + NE]).then_inc(sem("top"), 1)
                for u, n in seqs(i):
                    s = small[u]
                    dve.wait_ge(sem("top"), n + 1)
                    V.tensor_scalar(cols(s, NEGTOP, 1), cols(s, TOP, 1), -1.0, None, ALU.mult).then_inc(sem("negtop"), 1)
                    V.max_index(top_i[u][:, :], cols(s, TOP, 8), psum_m[u][:, LG:LG + NE]).then_inc(sem("topi"), 1)
                for u, n in seqs(i):
                    dve.wait_ge(sem("topi"), n + 1)
                    V.tensor_copy(cols(small[u], TOPF, 1), top_i[u][:, 0:1]).then_inc(sem("topf"), 1)
                for u, n in seqs(i):
                    dve.wait_ge(sem("topf"), n + 1)
                    V.tensor_scalar(cols(small[u], ONEH, NE), expert_iota[:, :], cols(small[u], TOPF, 1), None, ALU.is_equal).then_inc(sem("oneh"), 1)
                for u, n in seqs(i):
                    dve.wait_ge(sem("oneh"), n + 1)
                    V.tensor_copy(onehot16[u][:, :], cols(small[u], ONEH, NE)).then_inc(sem("oneh16"), 1)

            def place(i):
                for u, n in seqs(i):
                    s = small[u]
                    dve.wait_ge(sem("zsum"), n + 1)
                    V.reciprocal(row[u][:, 2 * D:2 * D + 1], cols(s, ZSUM, 1)).then_inc(sem("rp"), 1)
                    freed(dve, sem("listed"), 32 * i)
                    V.tensor_copy(tok_col[u][:, :], token_iota[:, bass.ds(n, 1)]).then_inc(sem("tokcol"), 1)
                    dve.wait_ge(sem("p_prio"), n + 1)
                    V.scalar_tensor_tensor(cols(s, SCR, NE), psum_m[u][:, LG + NE:LG + 2 * NE], 1.0, cols(s, ONEH, NE), ALU.mult, ALU.mult,
                                           accum_out=cols(s, PRIO, 1)).then_inc(sem("prio"), 1)
                    dve.wait_ge(sem("total"), n + 1)
                    V.scalar_tensor_tensor(cols(s, EXPS, NE), total[:, :], 1.0, cols(s, ONEH, NE), ALU.mult, ALU.mult,
                                           accum_out=cols(s, BASE, 1)).then_inc(sem("basep"), 1)
                    V.scalar_tensor_tensor(total[:, :], psum_m[u][:, LG + 2 * NE:LG + 3 * NE], float(CAP), total[:, :],
                                           ALU.min, ALU.add).then_inc(sem("total"), 1)
                for u, n in seqs(i):
                    s = small[u]
                    dve.wait_ge(sem("prio"), n + 1)
                    V.tensor_scalar(cols(s, KEEP, 1), cols(s, PRIO, 1), float(CAP), BIG, ALU.is_gt, ALU.mult).then_inc(sem("keep"), 1)
                    dve.wait_ge(sem("basep"), n + 1)
                    V.tensor_tensor(cols(s, BASE, 1), cols(s, BASE, 1), cols(s, PRIO, 1), ALU.add).then_inc(sem("dest0"), 1)
                for u, n in seqs(i):
                    s = small[u]
                    dve.wait_ge(sem("dest0"), n + 1)
                    V.tensor_scalar(cols(s, SCR, SPLIT), list_edge[:, :], cols(s, BASE, 1), None, ALU.is_lt, ALU.add,
                                    accum_out=cols(s, SPLITNO, 1)).then_inc(sem("dest1"), 1)
                    dve.wait_ge(sem("keep"), n + 1)
                    V.scalar_tensor_tensor(cols(s, DEST, 1), cols(s, BASE, 1), float(NLISTS), cols(s, KEEP, 1), ALU.mult, ALU.add).then_inc(sem("dest2"), 1)
                for u, n in seqs(i):
                    s = small[u]
                    dve.wait_ge(sem("dest2"), n + 1)
                    dve.wait_ge(sem("dest1"), n + 1)
                    V.scalar_tensor_tensor(cols(s, DEST, 1), cols(s, SPLITNO, 1), 1.0 - P * NLISTS, cols(s, DEST, 1), ALU.mult, ALU.add).then_inc(sem("dest3"), 1)
                for u, n in seqs(i):
                    s = small[u]
                    dve.wait_ge(sem("dest3"), n + 1)
                    V.scalar_tensor_tensor(cols(s, DEST, 1), cols(s, TOPF, 1), float(SPLIT), cols(s, DEST, 1), ALU.mult, ALU.add).then_inc(sem("dest4"), 1)
                for u, n in seqs(i):
                    dve.wait_ge(sem("dest4"), n + 1)
                    dve.wait_ge(sem("tokcol"), n + 1)
                    V.tensor_scalar(slot_i[u][:, :], cols(small[u], DEST, 1), float(NLISTS), None, ALU.subtract).then_inc(sem("dest"), 1)

            def tok(i):
                reduce_args(i)
                sum_terms(i)
                shift(i, MV, RSTD1, NMR1, "1")
                second_norm(i)

            def front(i):
                head_norm(i)
                guard(i)

            def route(i):
                choose(i)
                place(i)

            def back(i, with_front, with_tok, with_route):
                if with_route:
                    choose(i - 1)
                if with_tok:
                    reduce_args(i + 2)
                if with_route:
                    place(i - 1)
                if with_front:
                    head_norm(i + 1)
                attended(i)
                residual(i)
                if with_tok:
                    sum_terms(i + 2)
                if with_front:
                    guard(i + 1)
                experts_in(i)
                if with_tok:
                    shift(i + 2, MV, RSTD1, NMR1, "1")
                    second_norm(i + 2)

            phase_a(dve, tok, front, back, route)

            steps = [0]

            def planned(ins):
                steps[0] += 1
                ins.then_inc(sem("plan"), 1)
                dve.wait_ge(sem("plan"), steps[0])

            dve.wait_ge(sem("total"), NSEQ + 1)
            dve.wait_ge(sem("out_plain"), 32 * NSEQ)
            dve.wait_ge(sem("listed"), 16 * NSEQ)
            big = shared[:, 0:NBLK * NE].rearrange("p (j e) -> p j e", e=NE)
            big2 = shared[:, 512:512 + NBLK * NE].rearrange("p (j e) -> p j e", e=NE)
            nb, cum, ones, excl = (cols(plan, a, NE) for a in (16, 32, 48, 64))
            jrow, ej, within, length, q0, q1 = (cols(plan, 112 + 32 * a, NBLK) for a in range(6))
            nblk = cols(plan, 304, 1)
            k8 = shared[:, 0:8 * NE].rearrange("p (e k) -> p e k", k=8)
            planned(V.memset(ones, 1.0))
            for k in range(NSEQ * CAP // P):
                planned(V.tensor_scalar(k8[:, :, k], total[:, :], float(k * P), None, ALU.is_gt))
            planned(V.tensor_reduce(nb, k8, AX, ALU.add))
            planned(V.tensor_tensor_scan(cum, ones, nb, 0.0, ALU.mult, ALU.add))
            planned(V.tensor_tensor(excl, cum, nb, ALU.subtract))
            planned(V.tensor_scalar(nblk, cum[:, NE - 1:NE], 1.0, None, ALU.subtract))
            planned(V.tensor_scalar(jrow, blk_idx[:, :], nblk, None, ALU.min))

            def over(v):
                return v.unsqueeze(1).broadcast_to([P, NBLK, NE])

            planned(V.tensor_tensor(big, over(cum), jrow.unsqueeze(2).broadcast_to([P, NBLK, NE]), ALU.is_le))
            planned(V.tensor_reduce(ej, big, AX, ALU.add))
            planned(V.tensor_scalar(blk_col[:, :], ej, float(WCOL), None, ALU.mult))
            V.tensor_copy(plan[:, 399:400], ones[:, 0:1]).then_inc(sem("blk_col"), 1)
            planned(V.tensor_tensor(big, over(expert_iota[:, :]), ej.unsqueeze(2).broadcast_to([P, NBLK, NE]), ALU.is_equal))
            planned(V.tensor_tensor(big2, big, over(excl), ALU.mult))
            planned(V.tensor_reduce(within, big2, AX, ALU.add))
            planned(V.tensor_tensor(big2, big, over(total[:, :]), ALU.mult))
            planned(V.tensor_reduce(length, big2, AX, ALU.add))
            planned(V.tensor_tensor(within, jrow, within, ALU.subtract))
            planned(V.scalar_tensor_tensor(blk_list[:, :], ej, float(SPLIT), within, ALU.mult, ALU.add))
            planned(V.tensor_scalar(within, within, float(P), token_iota[:, 0:1], ALU.mult, ALU.add))
            planned(V.tensor_tensor(q0, within, length, ALU.is_ge))
            planned(V.tensor_tensor(q1, blk_idx[:, :], jrow, ALU.is_gt))
            planned(V.tensor_tensor(q0, q0, q1, ALU.add))
            planned(V.tensor_scalar(blk_pen[:, :], q0, BIG, None, ALU.mult))
            dve.wait_ge(sem("tokens"), 16)

            def pick_rows(q, k0, us):
                for u in us:
                    j = 2 * q + u
                    at = dve.value_load(blk_list[0:1, bass.ds(j, 1)], min_val=0, max_val=NLISTS - 1)
                    if not isinstance(q, int) or q >= 2:
                        dve.wait_ge(sem(f"rows{k0 + u}"), 8 * (q - k0 // 2))
                    V.tensor_copy(gidx[k0 + u][:, :], tokens[:, bass.ds(at, 1)]).then_inc(sem("gidx"), 1)

            def blocks(q, k0, us, ahead):
                pick_rows(q + 2, k0, ahead)
                for u in us:
                    dve.wait_ge(sem("b_hT"), 2 * q + u + 1)
                    V.tensor_copy(hidT[u], psum[u][:, 2:4, :].rearrange("p b c -> p (b c)")[:, 0:FC * P]).then_inc(sem("hidT"), 1)
                for u in us:
                    j = 2 * q + u
                    at = dve.value_load(blk_list[0:1, bass.ds(j, 1)], min_val=0, max_val=NLISTS - 1)
                    freed(dve, sem(f"scattered{u}"), 16 * q)
                    V.tensor_tensor(oidx[u][:, :], tokens[:, bass.ds(at, 1)], blk_pen[:, bass.ds(j, 1)], ALU.add).then_inc(sem("oidx"), 1)
                    dve.wait_ge(sem("b_y"), j + 1)
                    dve.wait_ge(sem("oidx"), j + 1)
                    g = grow[k0 + u]
                    V.scalar_tensor_tensor(res[u], psum[u][:, 3, Y0:Y0 + D], g[:, 2 * D:2 * D + 1], g[:, D:2 * D],
                                           ALU.mult, ALU.add).then_inc(sem("res"), 1)

            pick_rows(0, 0, (0, 1))
            pick_rows(1, 2, (0, 1))
            phase_b(dve, blocks)

        @block.tensor
        def _(pe):
            T = nc.tensor

            def halves(dst, src, done):
                T.transpose(dst(0), src[:, 0:HALF], ident[:, :])
                T.transpose(dst(1), src[:, HALF:D], ident[:, :]).then_inc(sem(done), 1)

            def over_d(dst, xt, w, start, width, bias):
                k1 = HALF + 1 if bias else HALF
                T.matmul(dst, xt[0:HALF, 0:P], w[0:HALF, 0, start:start + width], start=True, stop=False)
                return T.matmul(dst, xt[0:k1, P:2 * P], w[0:k1, 1, start:start + width], start=False, stop=True)

            def k_pad(u):
                return qk_pad[u][:, HEADS * HPAD:]

            def turn_x(i, u):
                pe.wait_ge(sem("xn"), 2 * i + u + 1)
                freed(pe, sem("probs"), 2 * i + u - 1)
                halves(lambda k: psum_s[u][0:HALF, 2, k * P:(k + 1) * P], xn[u], "p_xT")

            def qkv(i, u):
                pe.wait_ge(sem("xT"), 2 * i + u + 1)
                over_d(psum_s[u][:, 0, 0:2 * D], xT[u], wqkv, 0, 2 * D, True)
                over_d(psum_s[u][:, 1, 0:D], xT[u], wqkv, 2 * D, D, True).then_inc(sem("p_qkv"), 1)

            def turn_qk(i, u):
                n = 2 * i + u
                pe.wait_ge(sem("qk"), n + 1)
                for c in range(CHUNKS):
                    last = T.transpose(psum_s[u][0:GW, 2, c * P:(c + 1) * P], k_pad(u)[:, c * GW:(c + 1) * GW], ident[:, :])
                last.then_inc(sem("p_kT"), 1)
                pe.wait_ge(sem("v"), n + 1)
                for c in range(CHUNKS):
                    last = T.transpose(psum_s[u][0:GW, 1, c * P:(c + 1) * P], qk_pad[u][:, c * GW:(c + 1) * GW], ident[:, :])
                last.then_inc(sem("p_qT0"), 1)

            def scores(i, u, dst, lhs, rhs, rows_used, done):
                for h in range(HEADS):
                    c, g = divmod(h, GROUPS)
                    rows_ = slice(g * HPAD, g * HPAD + rows_used)
                    last = T.matmul(dst[:, g, c * P:(c + 1) * P], lhs[u][rows_, c * P:(c + 1) * P],
                                    rhs[u][rows_, c * P:(c + 1) * P], start=True, stop=True)
                last.then_inc(sem(done), 1)

            def guard_scores(i, u):
                n = 2 * i + u
                pe.wait_ge(sem("qT16"), n + 1)
                pe.wait_ge(sem("kT"), n + 1)
                scores(i, u, psum_s[u], qT16, kT16, HD, "p_guard")

            def turn_q(i, u):
                pe.wait_ge(sem("guard"), 2 * i + u + 1)
                for c in range(CHUNKS):
                    last = T.transpose(psum_s[u][0:GW, 0, c * P:(c + 1) * P], qk_pad[u][:, c * GW:(c + 1) * GW], ident[:, :])
                last.then_inc(sem("p_qT1"), 1)

            def scores_T(i, u):
                pe.wait_ge(sem("qT"), 2 * i + u + 1)
                scores(i, u, psum_s[u], kT, qT, HD + 1, "p_sT")

            def attend(i, u):
                pe.wait_ge(sem("probs"), 2 * i + u + 1)
                freed(pe, sem("total"), 2 * i + 1 if not isinstance(i, int) or i else 0)
                for h in range(HEADS):
                    c, g = divmod(h, GROUPS)
                    at = (g * CHUNKS + c) * P
                    last = T.matmul(psum_m[u][:, h * (HD + 1):(h + 1) * (HD + 1)], probsT[u][:, at:at + P],
                                    v_aug[u][:, h * (HD + 1):(h + 1) * (HD + 1)], start=True, stop=True)
                last.then_inc(sem("p_pv"), 1)

            def turn_o(i, u):
                pe.wait_ge(sem("o"), 2 * i + u + 1)
                halves(lambda k: psum_m[u][0:HALF, (2 + k) * P:(3 + k) * P], o_sb[u], "p_oT")

            def project(i, u):
                pe.wait_ge(sem("oT"), 2 * i + u + 1)
                over_d(psum_m[u][:, 0:D], oT[u], wproj, 0, D, True).then_inc(sem("p_y"), 1)

            def turn_n(i, u):
                pe.wait_ge(sem("normed"), 2 * i + u + 1)
                halves(lambda k: psum_m[u][0:HALF, (2 + k) * P:(3 + k) * P], row[u], "p_nT")

            def logits(i, u):
                pe.wait_ge(sem("nT"), 2 * i + u + 1)
                over_d(psum_m[u][:, LG:LG + NE], nT[u], wrout, 0, NE, False).then_inc(sem("p_logit"), 1)

            def places(i, u):
                n = 2 * i + u
                pe.wait_ge(sem("oneh16"), n + 1)
                pe.wait_ge(sem("zsum"), n + 1)
                T.matmul(psum_m[u][:, LG + NE:LG + 2 * NE], identb[:, 0, :], onehot16[u][:, :], start=True, stop=True)
                T.matmul(psum_m[u][:, LG + 2 * NE:LG + 3 * NE], identb[:, 1, :], onehot16[u][:, :], start=True, stop=True).then_inc(sem("p_prio"), 1)

            def front(i):
                for stage in (turn_x, qkv, turn_qk, guard_scores, turn_q):
                    for u in range(2):
                        stage(i, u)

            def route(i):
                for stage in (logits, places):
                    for u in range(2):
                        stage(i, u)

            def back(i, with_front, with_tok, with_route):
                if with_route:
                    logits(i - 1, 0)
                    logits(i - 1, 1)
                scores_T(i, 0)
                scores_T(i, 1)
                if with_route:
                    places(i - 1, 0)
                    places(i - 1, 1)
                if with_front:
                    turn_x(i + 1, 0)
                    turn_x(i + 1, 1)
                    qkv(i + 1, 0)
                    qkv(i + 1, 1)
                attend(i, 0)
                attend(i, 1)
                turn_o(i, 0)
                turn_o(i, 1)
                project(i, 0)
                project(i, 1)
                if with_front:
                    turn_qk(i + 1, 0)
                    turn_qk(i + 1, 1)
                    guard_scores(i + 1, 0)
                    guard_scores(i + 1, 1)
                    turn_q(i + 1, 0)
                    turn_q(i + 1, 1)
                turn_n(i, 0)
                turn_n(i, 1)

            pe.wait_ge(sem("ident"), 6)
            pe.wait_ge(sem("ones"), 6)
            pe.wait_ge(sem("pad1"), 2)
            pe.wait_ge(sem("const"), 16 * N_CONST)
            phase_a(pe, lambda i: None, front, back, route)

            pe.wait_ge(sem("blk_col"), 1)

            def turn_rows(q, k0, us, u):
                if u in us:
                    pe.wait_ge(sem(f"rows{k0 + u}"), 8 * (q - k0 // 2) + 16)
                    if not isinstance(q, int) or q:
                        pe.wait_ge(sem("hid"), 2 * q + u - 1)
                    halves(lambda k: psum[u][0:HALF, k, FF // 2:512], grow[k0 + u], "b_gT")

            def blocks(q, k0, us, ahead):
                at = [pe.value_load(blk_col[0:1, bass.ds(2 * q + u, 1)], min_val=0, max_val=(NE - 1) * WCOL) for u in us]
                after = next_blocks(q)
                for u in us:
                    pe.wait_ge(sem("gT"), 2 * q + u + 1)
                    for half in range(2):
                        for k in range(2):
                            last = T.matmul(psum[u][:, half, 0:FF // 2], gT[u][0:HALF, k * P:(k + 1) * P],
                                            weights[0:HALF, bass.ds(at[u] + k * FF + half * (FF // 2), FF // 2)],
                                            start=k == 0, stop=k == 1)
                    last.then_inc(sem("b_hid"), 1)
                for u in us:
                    turn_rows(q + 1, 2 - k0, after, u)
                    pe.wait_ge(sem("hid"), 2 * q + u + 1)
                    freed(pe, sem("res"), 2 * q)
                    for c in range(FC):
                        last = T.transpose(psum[u][:, 2 + c // 4, (c % 4) * P:(c % 4 + 1) * P], hid[u][:, c * P:(c + 1) * P], ident[:, :])
                    last.then_inc(sem("b_hT"), 1)
                for u in us:
                    pe.wait_ge(sem("hidT"), 2 * q + u + 1)
                    for c in range(FC):
                        last = T.matmul(psum[u][:, 3, Y0:Y0 + D], hidT[u][:, c * P:(c + 1) * P],
                                        weights[:, bass.ds(at[u] + 2 * FF + c * D, D)], start=c == 0, stop=c == FC - 1)
                    last.then_inc(sem("b_y"), 1)

            turn_rows(0, 0, (0, 1), 0)
            turn_rows(0, 0, (0, 1), 1)
            pe.wait_ge(sem("weights"), 32 * NE)
            phase_b(pe, blocks)


def kernel(**inputs):
    import numpy as np
    import concourse.bacc as bacc
    from concourse.bass_utils import run_bass_kernel_spmd

    a = {k: np.asarray(v) for k, v in inputs.items()}
    tok = "L0_tok_"
    ids = [a["x"], a["itok_BS_0_9999"], a["itok_BS_0_2047"], a["itok_BS_0_15"], a["itok_BS_0_3"]]
    arrays = {
        "ids": np.stack([x.T for x in ids]),
        "taus": np.stack([a["fside_BS_age_tau"].T, a["fside_BS_delays_tau"].T]),
        "word_table": a[tok + "word_table"],
        "npi_table": a[tok + "npi_table"],
        "posi_table": a[tok + "posi_table"],
        "modal_table": a[tok + "modalities_table"],
        "seg_table": a[tok + "seg_table"],
        "ln_gamma": a[tok + "ln_gamma"],
        "ln_beta": a[tok + "ln_beta"],
        "qkv_wT": a["L0_attn_qkv_w"].T,
        "qkv_b": a["L0_attn_qkv_b"],
        "proj_wT": a["L0_attn_proj_w"].T,
        "proj_b": a["L0_attn_proj_b"],
        "q_norm_w": a["L0_attn_q_norm_w"],
        "k_norm_w": a["L0_attn_k_norm_w"],
        "ln_w": a["L0_ffn_ln_w"],
        "w_router": a["L0_ffn_w_router"],
        "wi": a["L0_ffn_wi"],
        "wo": a["L0_ffn_wo"],
    }
    for k in ("age", "delay"):
        arrays |= {k + x: a[tok + k + x].reshape(-1) for x in ("_w", "_b", "_w0", "_b0")}
    arrays = {"in_" + k: np.ascontiguousarray(v) for k, v in arrays.items()}

    nc = bacc.Bacc("TRN2", target_bir_lowering=False, num_devices=1)
    t = {k[3:]: nc.dram_tensor(k, v.shape, mybir.dt.from_np(v.dtype), kind="ExternalInput").ap()
         for k, v in arrays.items()}
    out = nc.dram_tensor("tower_out", [NSEQ * P, D], F32, kind="ExternalOutput").ap()
    tower_kernel(nc, t, out)
    r = run_bass_kernel_spmd(nc, [arrays], core_ids=[0])
    return r.results[0]["tower_out"].reshape(NSEQ, P, D)
```

```python
from contextlib import ExitStack

import concourse.bass as bass
from concourse import mybir

F32 = mybir.dt.float32
BF16 = mybir.dt.bfloat16
I32 = mybir.dt.int32
U32 = mybir.dt.uint32
ALU = mybir.AluOpType
ACT = mybir.ActivationFunctionType
AX = mybir.AxisListType.X

P = 128
NSEQ = 16
D = 192
HALF = D // 2
HEADS = 12
HD = D // HEADS
GROUPS = 3
CHUNKS = HEADS // GROUPS
HPAD = 32
NE = 16
CAP = 64
FF = 768
FC = FF // P
SLOTS = NSEQ * CAP
SPLIT = SLOTS // P
NLISTS = NE * SPLIT
WCOL = 2 * FF + FC * D
GW = GROUPS * HPAD
MODAL_V, SEG_V, WORD_V, NPI_V, POS_V = 16, 4, 8000, 2500, 512
T2V = D - 1
NPAIR = NSEQ // 2
NBLK = (NSEQ * P - NE) // P + NE
ROW = 2 * D + 1
BIG = float(1 << 20)
RSQRT_BITS = 1597463007.0
ROUND = 12582912.0
TWO_PI = 6.283185307179586
TWO_PI_HI = 6.28125
TWO_PI_LO = TWO_PI - TWO_PI_HI
PI_BELOW = 3.1415925
LN_EPS, NORM_EPS, RMS_EPS = 1e-12, 1e-5, 1e-6
SHARED = 7048
ARENA_FIRST = 10


def tower_kernel(nc, t, out):
    assert NBLK == 31
    ctx = ExitStack()
    with ctx:
        def sb(name, shape, dt=F32):
            return ctx.enter_context(nc.sbuf_tensor(name, shape, dt))

        sems = {}

        def sem(name):
            if name not in sems:
                sems[name] = ctx.enter_context(nc.semaphore("s_" + name))
            return sems[name]

        weights = sb("weights", [P, NE * WCOL])
        w_by_expert = weights[:, :].rearrange("p (e c) -> p e c", e=NE)
        shared = sb("shared", [P, SHARED])

        def carver(ap, start, end):
            at = [start]

            def carve(cols):
                a = at[0]
                at[0] += cols
                assert at[0] <= end, (at[0], end)
                return ap[:, a:a + cols]

            return carve

        arena = carver(weights, ARENA_FIRST * WCOL, NE * WCOL)
        share_a = carver(shared, 0, SHARED)
        share_b = carver(shared, 0, SHARED)

        terms = [arena(6 * D) for _ in range(2)]
        turns = [arena(2 * D) for _ in range(2)]
        xn = [arena(D) for _ in range(2)]
        xT = [arena(2 * P) for _ in range(2)]
        squares = [arena(2 * D) for _ in range(2)]
        qk_pad = [arena(2 * HEADS * HPAD) for _ in range(2)]
        kT16 = [arena(CHUNKS * P // 2).bitcast(BF16) for _ in range(2)]
        qT16 = [arena(CHUNKS * P // 2).bitcast(BF16) for _ in range(2)]
        kT = [arena(CHUNKS * P) for _ in range(2)]
        qT = [arena(HEADS * P) for _ in range(2)]
        v_aug = [arena(HEADS * HPAD) for _ in range(2)]
        h_all = arena(NSEQ * D)
        oT = [arena(2 * P) for _ in range(2)]
        pvT = [arena(HEADS * HPAD), share_a(HEADS * HPAD)]
        nT = oT
        probsT = [share_a(HEADS * P) for _ in range(2)]
        row = [share_a(ROW) for _ in range(2)]
        h1 = [share_a(D) for _ in range(2)]
        x2 = [share_a(D) for _ in range(2)]
        o_sb = [share_a(D) for _ in range(2)]
        wqkv = share_a(2 * 3 * D)[0:HALF + 1, :].rearrange("p (k f) -> p k f", k=2)
        wproj = share_a(2 * D)[0:HALF + 1, :].rearrange("p (k f) -> p k f", k=2)

        hidT = [share_b(FC * P) for _ in range(2)]
        res = [share_b(D) for _ in range(2)]
        grow = [share_b(ROW) for _ in range(4)]
        gT = [share_b(2 * P) for _ in range(2)]
        wi_now = [share_b(2 * FF) for _ in range(2)]

        ident = sb("ident", [P, P])
        identb = sb("identb", [P, 3, P], BF16)
        guard16 = [sb(f"guard16{u}", [P, HEADS], BF16) for u in range(2)]
        guardT = [sb(f"guardT{u}", [HEADS, P], BF16) for u in range(2)]
        wrout = sb("wrout", [HALF, 2, NE])
        vectors = sb("vectors", [P, 7, D])
        t2v_w, t2v_b = vectors[:, 0:2, :], vectors[:, 2:4, :]
        gamma_bc, beta_bc, lnw_bc = (vectors[:, k, :] for k in (4, 5, 6))
        tau = sb("tau", [P, 2, NSEQ])
        ids = sb("ids", [P, NSEQ, 4], I32)
        pair_table = shared[0:MODAL_V * SEG_V, 0:2 * D]
        rawid = shared[:, 2 * D:2 * D + 5 * NSEQ].bitcast(I32).rearrange("p (k n) -> p k n", k=5)
        wrapped = shared[:, 2 * D + 5 * NSEQ:2 * D + 10 * NSEQ].rearrange("p (k n) -> p k n", k=5)
        qk_norm = sb("qk_norm", [GW, 2])
        qk_scale = sb("qk_scale", [GW, 1])
        mhalf = sb("mhalf", [P, 1])
        expert_iota = sb("expert_iota", [P, NE])
        token_iota = sb("token_iota", [P, NSEQ])
        small = [sb(f"small{u}", [P, 160]) for u in range(2)]
        ms_qk = sb("ms_qk", [P, 2, 2 * HEADS])
        rs_qk = sb("rs_qk", [P, 2, 2 * HEADS])
        nr_qk = sb("nr_qk", [P, 2, 2 * HEADS])
        idx4 = [sb(f"idx4{u}", [P, 4], I32) for u in range(2)]
        slot_i = [sb(f"slot_i{u}", [P, 1], I32) for u in range(2)]
        top_i = [sb(f"top_i{u}", [P, 8], U32) for u in range(2)]
        onehot16 = [sb(f"onehot16{u}", [P, NE], BF16) for u in range(2)]
        total = sb("total", [P, NE])
        tokens = sb("tokens", [P, NLISTS])
        tok_col = [sb(f"tok_col{u}", [P, 1]) for u in range(2)]
        list_edge = sb("list_edge", [P, SPLIT])
        plan = shared[:, 1152:1552]
        blk_idx = sb("blk_idx", [P, NBLK])
        blk_pen = sb("blk_pen", [P, NBLK])
        blk_col = sb("blk_col", [P, NBLK], I32)
        blk_list = sb("blk_list", [P, NBLK], I32)
        gidx = [sb(f"gidx{k}", [P, 1], I32) for k in range(4)]
        oidx = [sb(f"oidx{u}", [P, 1], I32) for u in range(2)]

        psum = [ctx.enter_context(nc.psum_tensor(f"psum{u}", [P, 4, 512], F32)) for u in range(2)]
        psum_s = [psum[u][:, 0:3, :] for u in range(2)]
        psum_m = [psum[u][:, 3, :] for u in range(2)]

        def cols(tile, start, n):
            return tile[:, start:start + n]

        STATS, MV, RSTD1, MV2, RSTD2, MV3, RSTD3, SSQ, RSTDN = 0, 8, 10, 12, 14, 16, 18, 20, 22
        NMR1, NMR2, NMR3, STATS3, RSUM, TOP, NEGTOP, EXPS, ZSUM, ONEH, SCR = 24, 25, 26, 28, 72, 84, 92, 93, 109, 110, 126
        TOPF, PRIO, BASE, KEEP, DEST, SPLITNO = 144, 145, 146, 147, 148, 149

        pair_dram = nc.dram_tensor("pair_rows", [MODAL_V * SEG_V, D], F32).ap()
        rows = nc.dram_tensor("token_rows", [NSEQ * P, ROW], F32).ap()
        lists = nc.dram_tensor("expert_lists", [P * NLISTS, 1], F32).ap()

        def freed(eng, semaphore, value):
            if not isinstance(value, int) or value > 0:
                eng.wait_ge(semaphore, value)

        def seqs(i):
            return [(u, 2 * i + u) for u in range(2)]

        def phase_b(eng, blocks):
            both = (0, 1)
            blocks(0, 0, both, both)
            blocks(1, 2, both, both)
            with eng.Fori(1, NBLK // 4 - 1) as d:
                blocks(2 * d, 0, both, both)
                blocks(2 * d + 1, 2, both, both)
            blocks(NBLK // 2 - 3, 0, both, both)
            blocks(NBLK // 2 - 2, 2, both, (0,))
            blocks(NBLK // 2 - 1, 0, both, ())
            blocks(NBLK // 2, 2, (0,), ())

        def next_blocks(q):
            if isinstance(q, int) and q >= NBLK // 2 - 1:
                return (0,) if q == NBLK // 2 - 1 else ()
            return (0, 1)

        def further(i):
            return not isinstance(i, int) or i + 3 < NPAIR

        def phase_a(start, eng, back, route):
            start()
            back(0, True, True, False)
            with eng.Fori(1, NPAIR - 3) as i:
                back(i, True, True, True)
            back(NPAIR - 3, True, True, True)
            back(NPAIR - 2, True, False, True)
            back(NPAIR - 1, False, False, True)
            route(NPAIR - 1)

        EARLY = 4
        assert ARENA_FIRST - EARLY == NPAIR - 2
        N_CONST = 6
        LG = 0

        block = ctx.enter_context(nc.Block())

        @block.sync
        def _(sp):
            def load(name, dst, src):
                sp.dma_start(dst, src).then_inc(sem(name), 16)

            load("raw_ids", rawid[:, :, :], t["ids"].rearrange("k p n -> p k n"))
            load("pair_parts", pair_table[:, 0:D], t["modal_table"].unsqueeze(1).broadcast_to([MODAL_V, SEG_V, D]))
            load("pair_parts", pair_table[:, D:2 * D], t["seg_table"].unsqueeze(0).broadcast_to([MODAL_V, SEG_V, D]))
            load("vectors", tau[:, :, :], t["taus"].rearrange("k p n -> p k n"))
            load("vectors", vectors[:, :, :], t["vectors"].partition_broadcast(P))
            sp.wait_ge(sem("pair_sum"), 1)
            load("pair_stored", pair_dram, pair_table[:, 0:D])
            load("const", wqkv[0:HALF, 0, :], t["qkv_wT"][0:HALF, :])
            load("const", wqkv[0:HALF + 1, 1, :], t["qkv_wT"][HALF:D + 1, :])
            load("const", wproj[0:HALF, 0, :], t["proj_wT"][0:HALF, :])
            load("const", wproj[0:HALF + 1, 1, :], t["proj_wT"][HALF:D + 1, :])
            load("const", wrout[:, :, :], t["w_router"].rearrange("(k p) f -> p k f", p=HALF))
            load("const", qk_norm[:, :], t["qk_norm"])
            sp.wait_ge(sem("zeroed"), 1)
            load("lists0", lists.rearrange("(p q) o -> p (q o)", p=P), tokens[:, :])

            def load_expert(e):
                sp.dma_start(w_by_expert[0:HALF, e, 0:2 * FF].rearrange("p (k f) -> p k f", k=2),
                             t["wi"][e].rearrange("(k p) f -> p k f", p=HALF)).then_inc(sem("weights"), 16)
                sp.dma_start(w_by_expert[:, e, 2 * FF:WCOL].rearrange("p (k f) -> p k f", k=FC),
                             t["wo"][e].rearrange("(k p) f -> p k f", p=P)).then_inc(sem("weights"), 16)

            def load_expert_at(e):
                at = e * WCOL
                sp.dma_start(weights[0:HALF, bass.ds(at, 2 * FF)].rearrange("p (k f) -> p k f", k=2),
                             t["wi"][bass.ds(e, 1), :, :].rearrange("o (k p) f -> p (o k) f", p=HALF)).then_inc(sem("weights"), 16)
                sp.dma_start(weights[:, bass.ds(at + 2 * FF, FC * D)].rearrange("p (k f) -> p k f", k=FC),
                             t["wo"][bass.ds(e, 1), :, :].rearrange("o (k p) f -> p (o k) f", p=P)).then_inc(sem("weights"), 16)

            def store_and_load(i, experts):
                for u, n in seqs(i):
                    sp.wait_ge(sem("out0"), n + 1)
                    sp.dma_start(out[bass.ds(n * P, P), :], x2[u]).then_inc(sem("out_plain"), 16)
                    sp.dma_start(rows[bass.ds(n * P, P), :], row[u]).then_inc(sem("out_plain"), 16)
                for e in experts:
                    load_expert_at(e)

            sp.wait_ge(sem("xn"), 2)
            for e in range(EARLY):
                load_expert_at(e)
            with sp.Fori(0, ARENA_FIRST - EARLY) as i:
                store_and_load(i, [i + EARLY])
            sp.wait_ge(sem("summed"), NSEQ)
            load_expert(ARENA_FIRST)
            store_and_load(NPAIR - 2, [])
            sp.wait_ge(sem("p_sT"), NSEQ)
            for e in range(ARENA_FIRST + 1, NE - 2):
                load_expert(e)
            sp.wait_ge(sem("p_logit"), NSEQ)
            load_expert(NE - 2)
            load_expert(NE - 1)
            store_and_load(NPAIR - 1, [])
            sp.wait_ge(sem("listed"), 16 * NSEQ)
            sp.dma_start(tokens[:, :], lists.rearrange("(p q) o -> p (q o)", p=P)).then_inc(sem("tokens"), 16)
            sp.wait_ge(sem("out_plain"), 32 * NSEQ)
            sp.wait_ge(sem("scattered0"), 16 * ((NBLK + 1) // 2))
            sp.wait_ge(sem("scattered1"), 16 * (NBLK // 2))

        @block.gpsimd
        def _(pool):
            turn = {name: pool.alloc_register("turn_" + name) for name in ("idx4", "rp", "dest", "gidx", "res")}
            for name, first in (("idx4", 9), ("rp", 1), ("dest", 1), ("gidx", 9), ("res", 5)):
                pool.reg_mov(turn[name], first)

            def arrived(name, value):
                if isinstance(value, int):
                    pool.wait_ge(sem(name), value)
                else:
                    pool.wait_ge(sem(name), turn[name])
                    pool.reg_add(turn[name], turn[name], 1)

            nc.gpsimd.memset(ident[:, :], 0.0).then_inc(sem("g"), 1)
            nc.gpsimd.memset(identb[:, :, :], 1.0).then_inc(sem("g"), 1)
            pool.wait_ge(sem("g"), 2)
            nc.gpsimd.affine_select(out=ident[:, :], in_=ident[:, :], compare_op=ALU.not_equal, fill=1.0,
                                    base=0, pattern=[[-1, P]], channel_multiplier=1).then_inc(sem("ident"), 1)
            nc.gpsimd.affine_select(out=identb[:, 2, :], in_=identb[:, 2, :], compare_op=ALU.is_equal, fill=0.0,
                                    base=0, pattern=[[-1, P]], channel_multiplier=1).then_inc(sem("ident"), 1)
            nc.gpsimd.affine_select(out=identb[:, 0, :], in_=identb[:, 0, :], compare_op=ALU.is_ge, fill=0.0,
                                    base=0, pattern=[[1, P]], channel_multiplier=-1).then_inc(sem("ident"), 1)
            nc.gpsimd.memset(mhalf[:, :], -0.5).then_inc(sem("g"), 1)
            nc.gpsimd.iota(expert_iota[:, :], [[1, NE]], base=0, channel_multiplier=0,
                           allow_small_or_imprecise_dtypes=True).then_inc(sem("ident"), 1)
            nc.gpsimd.iota(token_iota[:, :], [[P, NSEQ]], base=0, channel_multiplier=1,
                           allow_small_or_imprecise_dtypes=True).then_inc(sem("ident"), 1)
            nc.gpsimd.iota(list_edge[:, :], [[P, SPLIT]], base=P, channel_multiplier=0,
                           allow_small_or_imprecise_dtypes=True).then_inc(sem("ident"), 1)
            nc.gpsimd.iota(blk_idx[:, :], [[1, NBLK]], base=0, channel_multiplier=0,
                           allow_small_or_imprecise_dtypes=True).then_inc(sem("ident"), 1)
            for u in range(2):
                nc.gpsimd.memset(qT[u][0:GW, :], 0.0).then_inc(sem("zeros"), 1)

            G = nc.gpsimd

            def gather_tables(i, u):
                n = 2 * i + u
                freed(pool, sem("summed"), 2 * i)
                G.tensor_copy(idx4[u][:, :], ids[:, bass.ds(n, 1), :].rearrange("p a k -> p (a k)")).then_inc(sem("idx4"), 1)
                arrived("idx4", n + 1)
                for k, table in enumerate((t["word_table"], t["npi_table"], t["posi_table"], pair_dram)):
                    if k == 3 and isinstance(i, int) and n == 0:
                        pool.wait_ge(sem("pair_stored"), 16)
                    G.indirect_dma_start(
                        out=terms[u][:, k * D:(k + 1) * D], out_offset=None, in_=table,
                        in_offset=bass.IndirectOffsetOnAxis(ap=idx4[u][:, k:k + 1], axis=0),
                    ).then_inc(sem(f"gathered{u}"), 16)

            def power(i, src, made, done):
                for u, n in seqs(i):
                    pool.wait_ge(sem(made), n + 1)
                    G.tensor_tensor(cols(small[u], src[1], 1), cols(small[u], src[0], 1), mhalf[:, :], ALU.pow).then_inc(sem(done), 1)

            def embed(i):
                power(i, (MV + 1, RSTD1), "var1", "rstd1")

            def scale_shift(i):
                for u, n in seqs(i):
                    h = h_all[:, bass.ds(n * D, D)]
                    pool.wait_ge(sem("ident"), 7)
                    pool.wait_ge(sem("ln1a"), n + 1)
                    G.tensor_tensor(h, h, gamma_bc, ALU.mult).then_inc(sem("ln1b"), 1)
                for u, n in seqs(i):
                    h = h_all[:, bass.ds(n * D, D)]
                    pool.wait_ge(sem("ident"), 7)
                    pool.wait_ge(sem("ln1b"), n + 1)
                    G.tensor_tensor(h, h, beta_bc, ALU.add).then_inc(sem("h"), 1)

            def unrouted(i, u):
                n = 2 * i + u
                arrived("rp", n + 1)
                G.tensor_scalar(x2[u], row[u][:, 0:D], row[u][:, 2 * D:2 * D + 1], None, ALU.mult).then_inc(sem("rp_n"), 1)
                pool.wait_ge(sem("rp_n"), n + 1)
                G.tensor_tensor(x2[u], x2[u], row[u][:, D:2 * D], ALU.add).then_inc(sem("out0"), 1)

            def enlist(i, u):
                arrived("dest", 2 * i + u + 1)
                G.indirect_dma_start(
                    out=lists, out_offset=bass.IndirectOffsetOnAxis(ap=slot_i[u][:, :], axis=0),
                    in_=tok_col[u][:, :], in_offset=None, bounds_check=P * NLISTS - 1, oob_is_err=False,
                ).then_inc(sem("listed"), 16)

            def start():
                for i in range(2):
                    for u in range(2):
                        gather_tables(i, u)
                    embed(i)
                    if i == 0:
                        pool.wait_ge(sem("vectors"), 32)
                    scale_shift(i)
                    power(i, (MV2 + 1, RSTD2), "var2", "rstd2")
                for u in range(2):
                    gather_tables(2, u)
                pool.wait_ge(sem("lists0"), 16)

            def route(i):
                unrouted(i, 0)
                enlist(i, 0)
                enlist(i, 1)
                unrouted(i, 1)

            def back(i, with_front, with_tok, with_route):
                if with_tok:
                    embed(i + 2)
                if further(i):
                    gather_tables(i + 3, 0)
                    gather_tables(i + 3, 1)
                if with_tok:
                    scale_shift(i + 2)
                if with_route:
                    unrouted(i - 1, 0)
                    unrouted(i - 1, 1)
                if with_tok:
                    power(i + 2, (MV2 + 1, RSTD2), "var2", "rstd2")
                if with_route:
                    enlist(i - 1, 0)
                    enlist(i - 1, 1)
                power(i, (MV3 + 1, RSTD3), "var3", "rstd3")
                for u, n in seqs(i):
                    pool.wait_ge(sem("x2"), n + 1)
                    G.tensor_tensor(row[u][:, D:2 * D], x2[u], h1[u], ALU.add).then_inc(sem("base"), 1)
                power(i, (SSQ, RSTDN), "ssq_e", "rstdn")

            pool.wait_ge(sem("g"), 3)
            pool.wait_ge(sem("ids"), 2)
            phase_a(start, pool, back, route)

            pool.wait_ge(sem("listed"), 16 * NSEQ)
            pool.wait_ge(sem("out_plain"), 32 * NSEQ)

            def gather_rows(q, k0, us):
                for u in us:
                    arrived("gidx", 2 * q + u + 1)
                    G.indirect_dma_start(
                        out=grow[k0 + u], out_offset=None, in_=rows,
                        in_offset=bass.IndirectOffsetOnAxis(ap=gidx[k0 + u][:, :], axis=0),
                    ).then_inc(sem(f"rows{k0 + u}"), 16)

            def blocks(q, k0, us, ahead):
                for u in us:
                    arrived("res", 2 * q + u + 1)
                    G.indirect_dma_start(
                        out=out, out_offset=bass.IndirectOffsetOnAxis(ap=oidx[u][:, :], axis=0),
                        in_=res[u], in_offset=None, bounds_check=NSEQ * P - 1, oob_is_err=False,
                    ).then_inc(sem(f"scattered{u}"), 16)
                gather_rows(q + 2, k0, ahead)

            gather_rows(0, 0, (0, 1))
            gather_rows(1, 2, (0, 1))
            phase_b(pool, blocks)

        @block.scalar
        def _(act):
            S = nc.scalar

            def normalize(dst, src, u, rstd, nmr):
                return S.activation(dst, src, ACT.Identity, scale=cols(small[u], rstd, 1), bias=cols(small[u], nmr, 1))

            def sines(i):
                for u, n in seqs(i):
                    r = turns[u].rearrange("p (k d) -> p k d", k=2)
                    a = terms[u][:, 4 * D:6 * D].rearrange("p (k d) -> p k d", k=2)
                    act.wait_ge(sem("reduced"), n + 1)
                    S.activation(a[:, :, 0:T2V], r[:, :, 0:T2V], ACT.Sin).then_inc(sem("sin"), 1)

            def ln1(i):
                for u, n in seqs(i):
                    h = h_all[:, bass.ds(n * D, D)]
                    act.wait_ge(sem("nmr1"), n + 1)
                    normalize(h, h, u, RSTD1, NMR1).then_inc(sem("ln1a"), 1)

            def attn_in(i):
                for u, n in seqs(i):
                    act.wait_ge(sem("nmr2"), n + 1)
                    freed(act, sem("p_xT"), 2 * i)
                    normalize(xn[u], h_all[:, bass.ds(n * D, D)], u, RSTD2, NMR2).then_inc(sem("xn"), 1)

            def turn_x(i, u):
                act.wait_ge(sem("p_xT"), 2 * i + u + 1)
                S.copy(xT[u][0:HALF, :], psum_s[u][0:HALF, 2, 0:2 * P]).then_inc(sem("xT"), 1)

            def squared(i):
                for u, n in seqs(i):
                    act.wait_ge(sem("p_qkv"), n + 1)
                    freed(act, sem("ssqk0"), 2 * i)
                    S.activation(squares[u], psum_s[u][:, 0, 0:2 * D], ACT.Square).then_inc(sem("sq"), 1)

            def values(i, u):
                n = 2 * i + u
                act.wait_ge(sem("p_qkv"), n + 1)
                freed(act, sem("p_pv"), n - 1 if not isinstance(i, int) or i else 0)
                S.copy(v_aug[u].rearrange("p (h d) -> p h d", d=HPAD)[:, :, 0:HD],
                       psum_s[u][:, 1, 0:D].rearrange("p (h d) -> p h d", d=HD)).then_inc(sem("v"), 1)

            def copy_pv(i, u):
                act.wait_ge(sem("p_pv"), 2 * i + u + 1)
                S.copy(pvT[u], psum_m[u][:, 0:HEADS * HPAD]).then_inc(sem("pvT"), 1)

            def turn_16(i, u):
                n = 2 * i + u
                act.wait_ge(sem("p_kT"), n + 1)
                S.copy(kT16[u][0:GW, :], psum_s[u][0:GW, 2, :]).then_inc(sem("kT16"), 1)
                act.wait_ge(sem("p_qT0"), n + 1)
                S.activation(qT16[u][0:GW, :], psum_s[u][0:GW, 1, :], ACT.Copy, scale=qk_scale[0:GW, 0:1]).then_inc(sem("qT16"), 1)

            def turn_qk(i, u):
                S.copy(kT[u][0:GW, :], psum_s[u][0:GW, 2, :])
                for g in range(GROUPS):
                    r = slice(g * HPAD, (g + 1) * HPAD)
                    last = S.activation(qT[u][r, :].rearrange("p (c g t) -> p c g t", c=CHUNKS, g=GROUPS)[:, :, g, :],
                                        psum_s[u][r, 1, :].rearrange("p (c t) -> p c t", c=CHUNKS), ACT.Copy, scale=qk_scale[r, 0:1])
                last.then_inc(sem("qT"), 1)

            def turn_guard(i, u):
                act.wait_ge(sem("p_guardT"), 2 * i + u + 1)
                S.activation(guardT[u][:, :], psum_m[u][0:HEADS, 2 * P:3 * P], ACT.Copy, scale=-1.0).then_inc(sem("guardT"), 1)

            def turn_n(i, u):
                act.wait_ge(sem("p_nT"), 2 * i + u + 1)
                S.copy(nT[u][0:HALF, :], psum_m[u][0:HALF, 2 * P:4 * P]).then_inc(sem("nT"), 1)

            def exp_logits(i):
                for u, n in seqs(i):
                    act.wait_ge(sem("negtop"), n + 1)
                    act.wait_ge(sem("topi"), n + 1)
                    S.activation(cols(small[u], EXPS, NE), psum_m[u][:, LG:LG + NE], ACT.Exp,
                                 bias=cols(small[u], NEGTOP, 1), accum_out=cols(small[u], ZSUM, 1)).then_inc(sem("zsum"), 1)

            def exp_scores(i, u):
                act.wait_ge(sem("p_sT"), 2 * i + u + 1)
                S.activation(probsT[u], psum_s[u].rearrange("p b c -> p (b c)"), ACT.Exp).then_inc(sem("probs"), 1)

            def start():
                sines(0)
                ln1(0)
                attn_in(0)
                turn_x(0, 0)
                turn_x(0, 1)
                sines(1)
                squared(0)
                values(0, 0)
                values(0, 1)
                act.wait_ge(sem("qk_scale"), 1)
                act.wait_ge(sem("zeros"), 4)
                for u in range(2):
                    turn_16(0, u)
                    turn_qk(0, u)
                ln1(1)
                turn_guard(0, 0)
                sines(2)

            def route(i):
                turn_n(i, 0)
                turn_n(i, 1)
                exp_logits(i)

            def back(i, with_front, with_tok, with_route):
                turn_guard(i, 1)
                exp_scores(i, 0)
                if with_route:
                    turn_n(i - 1, 0)
                if with_front:
                    attn_in(i + 1)
                    turn_x(i + 1, 0)
                exp_scores(i, 1)
                if with_route:
                    turn_n(i - 1, 1)
                if with_front:
                    turn_x(i + 1, 1)
                if with_route:
                    exp_logits(i - 1)
                if with_tok:
                    ln1(i + 2)
                if with_front:
                    squared(i + 1)
                copy_pv(i, 0)
                if with_front:
                    values(i + 1, 0)
                copy_pv(i, 1)
                if with_front:
                    values(i + 1, 1)
                    turn_16(i + 1, 0)
                    turn_qk(i + 1, 0)
                for u, n in seqs(i):
                    act.wait_ge(sem("p_oT"), n + 1)
                    S.copy(oT[u][0:HALF, :], psum_m[u][0:HALF, 2 * P:4 * P]).then_inc(sem("oT"), 1)
                if with_front:
                    turn_16(i + 1, 1)
                    turn_qk(i + 1, 1)
                    turn_guard(i + 1, 0)
                for u, n in seqs(i):
                    act.wait_ge(sem("nmr3"), n + 1)
                    freed(act, sem("out_plain"), 64 * i)
                    normalize(x2[u], h1[u], u, RSTD3, NMR3).then_inc(sem("x2"), 1)
                for u, n in seqs(i):
                    act.wait_ge(sem("x2"), n + 1)
                    S.activation(o_sb[u], x2[u], ACT.Square, accum_out=cols(small[u], SSQ + 1, 1)).then_inc(sem("ssq"), 1)
                if further(i):
                    sines(i + 3)

            phase_a(start, act, back, route)

            def turn_rows(q, us, u):
                if u in us:
                    act.wait_ge(sem("b_gT"), 2 * q + u + 1)
                    S.copy(gT[u][0:HALF, :], psum[u][0:HALF, 2, 0:2 * P]).then_inc(sem("gT"), 1)

            def relu(q, u):
                act.wait_ge(sem("b_hid"), 2 * q + u + 1)
                freed(act, sem("b_y"), 2 * q + u - 1 if not isinstance(q, int) or q else 0)
                S.activation(hidT[u], psum[u][:, 0:2, :].rearrange("p b c -> p (b c)")[:, 0:FC * P], ACT.Relu).then_inc(sem("hidT"), 1)

            def blocks(q, k0, us, ahead):
                after = next_blocks(q)
                for u in us:
                    relu(q, u)
                for u in after:
                    turn_rows(q + 1, after, u)

            turn_rows(0, (0, 1), 0)
            turn_rows(0, (0, 1), 1)
            act.wait_ge(sem("planned"), 1)
            phase_b(act, blocks)

        @block.vector
        def _(dve):
            V = nc.vector
            logit_turn = dve.alloc_register("turn_logit")
            dve.reg_mov(logit_turn, 1)

            for u in range(2):
                for tile in (xT[u], oT[u]):
                    V.memset(tile[HALF:HALF + 1, :], 1.0).then_inc(sem("ones"), 1)
                V.memset(v_aug[u].rearrange("p (h d) -> p h d", d=HPAD)[:, :, HD:HD + 1], 1.0).then_inc(sem("ones"), 1)
                V.memset(v_aug[u].rearrange("p (h d) -> p h d", d=HPAD)[:, :, HD + 1:HPAD], 0.0).then_inc(sem("ones"), 1)
            V.memset(tokens[:, :], 0.0).then_inc(sem("zeroed"), 1)
            V.memset(total[:, :], 0.0).then_inc(sem("total"), 1)
            dve.wait_ge(sem("raw_ids"), 16)
            tables = list(enumerate((WORD_V, NPI_V, POS_V, MODAL_V, SEG_V)))
            for k, rows in tables:
                V.tensor_scalar(wrapped[:, k, :], rawid[:, k, :], 0.0, float(rows), ALU.is_lt, ALU.mult).then_inc(sem("wrap"), 1)
            for k, rows in tables:
                dve.wait_ge(sem("wrap"), k + 1)
                V.tensor_tensor(wrapped[:, k, :], wrapped[:, k, :], rawid[:, k, :], ALU.add).then_inc(sem("wrap"), 1)
            for k, rows in tables:
                dve.wait_ge(sem("wrap"), len(tables) + k + 1)
                V.tensor_scalar(wrapped[:, k, :], wrapped[:, k, :], 0.0, float(rows - 1), ALU.max, ALU.min).then_inc(sem("wrap"), 1)
            dve.wait_ge(sem("wrap"), 3 * len(tables))
            V.tensor_copy(ids[:, :, 0:3], wrapped[:, 0:3, :].rearrange("p k n -> p n k")).then_inc(sem("ids"), 1)
            V.scalar_tensor_tensor(ids[:, :, 3], wrapped[:, 3, :], float(SEG_V), wrapped[:, 4, :], ALU.mult, ALU.add).then_inc(sem("ids"), 1)
            dve.wait_ge(sem("pair_parts"), 32)
            V.tensor_tensor(pair_table[:, 0:D], pair_table[:, 0:D], pair_table[:, D:2 * D], ALU.add).then_inc(sem("pair_sum"), 1)
            for u in range(2):
                V.memset(qk_pad[u], 0.0).then_inc(sem("zeros"), 1)
            dve.wait_ge(sem("vectors"), 32)
            dve.wait_ge(sem("ident"), 7)

            def reduce_args(i):
                a = [terms[u][:, 4 * D:6 * D].rearrange("p (k d) -> p k d", k=2) for u in range(2)]
                for u, n in seqs(i):
                    freed(dve, sem("summed"), 2 * i)
                    for k in range(2):
                        V.scalar_tensor_tensor(a[u][:, k, :], t2v_w[:, k, :], tau[:, k, bass.ds(n, 1)], t2v_b[:, k, :],
                                               ALU.mult, ALU.add).then_inc(sem("arg"), 1)
                r = [turns[u].rearrange("p (k d) -> p k d", k=2) for u in range(2)]
                for u, n in seqs(i):
                    dve.wait_ge(sem("arg"), 2 * n + 2)
                    freed(dve, sem("sin"), 2 * i)
                    V.tensor_scalar(r[u], a[u], 1.0 / TWO_PI, ROUND, ALU.mult, ALU.add).then_inc(sem("turn0"), 1)
                for u, n in seqs(i):
                    dve.wait_ge(sem("turn0"), n + 1)
                    V.tensor_scalar(r[u], r[u], ROUND, None, ALU.subtract).then_inc(sem("turn1"), 1)

            def reduce_args_on(i):
                a = [terms[u][:, 4 * D:6 * D].rearrange("p (k d) -> p k d", k=2) for u in range(2)]
                r = [turns[u].rearrange("p (k d) -> p k d", k=2) for u in range(2)]
                for u, n in seqs(i):
                    x = a[u][:, :, 0:T2V]
                    dve.wait_ge(sem("turn1"), n + 1)
                    V.scalar_tensor_tensor(x, r[u][:, :, 0:T2V], -TWO_PI_HI, x, ALU.mult, ALU.add).then_inc(sem("turn2"), 1)
                for u, n in seqs(i):
                    x, y = a[u][:, :, 0:T2V], r[u][:, :, 0:T2V]
                    dve.wait_ge(sem("turn2"), n + 1)
                    V.scalar_tensor_tensor(y, y, -TWO_PI_LO, x, ALU.mult, ALU.add).then_inc(sem("turn3"), 1)
                for u, n in seqs(i):
                    y = r[u][:, :, 0:T2V]
                    dve.wait_ge(sem("turn3"), n + 1)
                    V.tensor_scalar(y, y, PI_BELOW, -PI_BELOW, ALU.min, ALU.max).then_inc(sem("reduced"), 1)

            def variance(i, src, source, made, stats_at, mv_at, eps, tag):
                for u, n in seqs(i):
                    dve.wait_ge(sem("ident"), 7)
                    dve.wait_ge(sem(source), n + 1)
                    V.bn_stats(cols(small[u], stats_at, 6), src(u, n)).then_inc(sem("stats" + tag), 1)
                for u, n in seqs(i):
                    dve.wait_ge(sem("ident"), 7)
                    dve.wait_ge(sem("stats" + tag), n + 1)
                    V.bn_aggr(cols(small[u], mv_at, 2), cols(small[u], stats_at, 6)).then_inc(sem("mv" + tag), 1)
                for u, n in seqs(i):
                    v = cols(small[u], mv_at + 1, 1)
                    dve.wait_ge(sem("mv" + tag), n + 1)
                    V.tensor_scalar(v, v, eps, None, ALU.add).then_inc(sem(made), 1)

            def shift(i, mv_at, rstd_at, nmr_at, tag):
                for u, n in seqs(i):
                    s = small[u]
                    dve.wait_ge(sem("rstd" + tag), n + 1)
                    V.scalar_tensor_tensor(cols(s, nmr_at, 1), cols(s, mv_at, 1), -1.0, cols(s, rstd_at, 1),
                                           ALU.mult, ALU.mult).then_inc(sem("nmr" + tag), 1)

            def h_of(u, n):
                return h_all[:, bass.ds(n * D, D)]

            def sum_terms(i):
                for u, n in seqs(i):
                    dve.wait_ge(sem("sin"), n + 1)
                    dve.wait_ge(sem(f"gathered{u}"), 64 * (i + 1))
                    V.tensor_reduce(h_of(u, n), terms[u].rearrange("p (k d) -> p d k", k=6), AX, ALU.add).then_inc(sem("summed"), 1)
                variance(i, h_of, "summed", "var1", STATS, MV, LN_EPS, "1")

            def second_norm(i):
                variance(i, h_of, "h", "var2", STATS, MV2, NORM_EPS, "2")
                shift(i, MV2, RSTD2, NMR2, "2")

            def head_norm(i):
                for u, n in seqs(i):
                    dve.wait_ge(sem("sq"), n + 1)
                    V.tensor_reduce(ms_qk[:, u, :], squares[u].rearrange("p (h d) -> p h d", d=HD), AX, ALU.add).then_inc(sem("ssqk0"), 1)
                v, y, w = (x[:, :, :].rearrange("p u h -> p (u h)") for x in (ms_qk, rs_qk, nr_qk))
                dve.wait_ge(sem("ssqk0"), 2 * i + 2)
                V.tensor_scalar(v, v, 1.0 / HD, RMS_EPS, ALU.mult, ALU.add).then_inc(sem("ssqk"), 1)
                dve.wait_ge(sem("ssqk"), i + 1)
                V.tensor_scalar(y.bitcast(I32), v.bitcast(I32), -0.5, RSQRT_BITS, ALU.mult, ALU.add).then_inc(sem("guess"), 1)
                dve.wait_ge(sem("guess"), i + 1)
                for k in range(3):
                    V.scalar_tensor_tensor(w, y, -0.5, y, ALU.mult, ALU.mult).then_inc(sem("newton"), 1)
                    dve.wait_ge(sem("newton"), 9 * i + 3 * k + 1)
                    V.tensor_tensor(w, w, v, ALU.mult).then_inc(sem("newton"), 1)
                    dve.wait_ge(sem("newton"), 9 * i + 3 * k + 2)
                    V.scalar_tensor_tensor(y, w, 1.5, y, ALU.add, ALU.mult).then_inc(sem("newton"), 1)
                    dve.wait_ge(sem("newton"), 9 * i + 3 * k + 3)
                for u, n in seqs(i):
                    V.tensor_tensor(qk_pad[u].rearrange("p (h d) -> p h d", d=HPAD)[:, :, 0:HD],
                                    psum_s[u][:, 0, 0:2 * D].rearrange("p (h d) -> p h d", d=HD),
                                    rs_qk[:, u, :].unsqueeze(2).broadcast_to([P, 2 * HEADS, HD]), ALU.mult).then_inc(sem("qk"), 1)

            def guard(i, u):
                dve.wait_ge(sem("p_guard"), 2 * i + u + 1)
                V.tensor_reduce(guard16[u][:, :].rearrange("p (c g) -> p g c", c=CHUNKS),
                                psum_s[u].rearrange("p g (c m) -> p g c m", m=P), AX,
                                ALU.max).then_inc(sem("guard"), 1)

            def attended(i, u):
                n = 2 * i + u
                pv = psum_m[u][:, 0:HEADS * HPAD].rearrange("p (h d) -> p h d", d=HPAD)
                dve.wait_ge(sem("p_pvback"), n + 1)
                freed(dve, sem("ssq"), 2 * i)
                V.reciprocal(cols(small[u], RSUM, HEADS), pv[:, :, HD]).then_inc(sem("rsum"), 1)
                dve.wait_ge(sem("rsum"), n + 1)
                V.tensor_tensor(o_sb[u].rearrange("p (h d) -> p h d", d=HD), pv[:, :, 0:HD],
                                cols(small[u], RSUM, HEADS).unsqueeze(2).broadcast_to([P, HEADS, HD]),
                                ALU.mult).then_inc(sem("o"), 1)

            def residual(i):
                for u, n in seqs(i):
                    dve.wait_ge(sem("p_y"), n + 1)
                    freed(dve, sem("base"), 2 * i)
                    V.tensor_tensor(h1[u], psum_m[u][:, 0:D], h_of(u, n), ALU.add).then_inc(sem("h1"), 1)
                variance(i, lambda u, n: h1[u], "h1", "var3", STATS3, MV3, NORM_EPS, "3")

            def experts_in(i):
                for u, n in seqs(i):
                    s = small[u]
                    dve.wait_ge(sem("ssq"), n + 1)
                    V.tensor_scalar(cols(s, SSQ, 1), cols(s, SSQ + 1, 1), 1.0 / D, RMS_EPS, ALU.mult, ALU.add).then_inc(sem("ssq_e"), 1)
                for u, n in seqs(i):
                    dve.wait_ge(sem("rstdn"), n + 1)
                    freed(dve, sem("out_plain"), 64 * i)
                    V.scalar_tensor_tensor(row[u][:, 0:D], x2[u], cols(small[u], RSTDN, 1), lnw_bc,
                                           ALU.mult, ALU.mult).then_inc(sem("normed"), 1)

            def choose(i):
                for u, n in seqs(i):
                    if isinstance(i, int):
                        dve.wait_ge(sem("p_logit"), n + 1)
                    else:
                        dve.wait_ge(sem("p_logit"), logit_turn)
                        dve.reg_add(logit_turn, logit_turn, 1)
                    V.max(cols(small[u], TOP, 8), psum_m[u][:, LG:LG + NE]).then_inc(sem("top"), 1)
                for u, n in seqs(i):
                    s = small[u]
                    dve.wait_ge(sem("top"), n + 1)
                    V.tensor_scalar(cols(s, NEGTOP, 1), cols(s, TOP, 1), -1.0, None, ALU.mult).then_inc(sem("negtop"), 1)
                    V.max_index(top_i[u][:, :], cols(s, TOP, 8), psum_m[u][:, LG:LG + NE]).then_inc(sem("topi"), 1)
                for u, n in seqs(i):
                    dve.wait_ge(sem("topi"), n + 1)
                    V.tensor_copy(cols(small[u], TOPF, 1), top_i[u][:, 0:1]).then_inc(sem("topf"), 1)
                for u, n in seqs(i):
                    dve.wait_ge(sem("topf"), n + 1)
                    V.tensor_scalar(cols(small[u], ONEH, NE), expert_iota[:, :], cols(small[u], TOPF, 1), None, ALU.is_equal).then_inc(sem("oneh"), 1)
                for u, n in seqs(i):
                    dve.wait_ge(sem("oneh"), n + 1)
                    V.tensor_copy(onehot16[u][:, :], cols(small[u], ONEH, NE)).then_inc(sem("oneh16"), 1)

            def place(i):
                for u, n in seqs(i):
                    s = small[u]
                    dve.wait_ge(sem("zsum"), n + 1)
                    V.reciprocal(row[u][:, 2 * D:2 * D + 1], cols(s, ZSUM, 1)).then_inc(sem("rp"), 1)
                    freed(dve, sem("listed"), 32 * i)
                    V.tensor_copy(tok_col[u][:, :], token_iota[:, bass.ds(n, 1)]).then_inc(sem("tokcol"), 1)
                    dve.wait_ge(sem("p_prio"), n + 1)
                    V.scalar_tensor_tensor(cols(s, SCR, NE), psum_m[u][:, LG + NE:LG + 2 * NE], 1.0, cols(s, ONEH, NE), ALU.mult, ALU.mult,
                                           accum_out=cols(s, PRIO, 1)).then_inc(sem("prio"), 1)
                    dve.wait_ge(sem("total"), n + 1)
                    V.scalar_tensor_tensor(cols(s, EXPS, NE), total[:, :], 1.0, cols(s, ONEH, NE), ALU.mult, ALU.mult,
                                           accum_out=cols(s, BASE, 1)).then_inc(sem("basep"), 1)
                    V.scalar_tensor_tensor(total[:, :], psum_m[u][:, LG + 2 * NE:LG + 3 * NE], float(CAP), total[:, :],
                                           ALU.min, ALU.add).then_inc(sem("total"), 1)
                for u, n in seqs(i):
                    s = small[u]
                    dve.wait_ge(sem("prio"), n + 1)
                    V.tensor_scalar(cols(s, KEEP, 1), cols(s, PRIO, 1), float(CAP), BIG, ALU.is_gt, ALU.mult).then_inc(sem("keep"), 1)
                    dve.wait_ge(sem("basep"), n + 1)
                    V.tensor_tensor(cols(s, BASE, 1), cols(s, BASE, 1), cols(s, PRIO, 1), ALU.add).then_inc(sem("dest0"), 1)
                for u, n in seqs(i):
                    s = small[u]
                    dve.wait_ge(sem("dest0"), n + 1)
                    V.tensor_scalar(cols(s, SCR, SPLIT), list_edge[:, :], cols(s, BASE, 1), None, ALU.is_lt, ALU.add,
                                    accum_out=cols(s, SPLITNO, 1)).then_inc(sem("dest1"), 1)
                    dve.wait_ge(sem("keep"), n + 1)
                    V.scalar_tensor_tensor(cols(s, DEST, 1), cols(s, BASE, 1), float(NLISTS), cols(s, KEEP, 1), ALU.mult, ALU.add).then_inc(sem("dest2"), 1)
                for u, n in seqs(i):
                    s = small[u]
                    dve.wait_ge(sem("dest2"), n + 1)
                    dve.wait_ge(sem("dest1"), n + 1)
                    V.scalar_tensor_tensor(cols(s, DEST, 1), cols(s, SPLITNO, 1), 1.0 - P * NLISTS, cols(s, DEST, 1), ALU.mult, ALU.add).then_inc(sem("dest3"), 1)
                for u, n in seqs(i):
                    s = small[u]
                    dve.wait_ge(sem("dest3"), n + 1)
                    V.scalar_tensor_tensor(cols(s, DEST, 1), cols(s, TOPF, 1), float(SPLIT), cols(s, DEST, 1), ALU.mult, ALU.add).then_inc(sem("dest4"), 1)
                for u, n in seqs(i):
                    dve.wait_ge(sem("dest4"), n + 1)
                    dve.wait_ge(sem("tokcol"), n + 1)
                    V.tensor_scalar(slot_i[u][:, :], cols(small[u], DEST, 1), float(NLISTS), None, ALU.subtract).then_inc(sem("dest"), 1)

            def start():
                reduce_args(0)
                reduce_args_on(0)
                sum_terms(0)
                shift(0, MV, RSTD1, NMR1, "1")
                second_norm(0)
                reduce_args(1)
                reduce_args_on(1)
                dve.wait_ge(sem("const"), 16 * N_CONST)
                V.scalar_tensor_tensor(qk_scale[:, :], qk_norm[:, 0:1], HD ** -0.5, qk_norm[:, 1:2], ALU.mult, ALU.mult).then_inc(sem("qk_scale"), 1)
                dve.wait_ge(sem("zeros"), 4)
                head_norm(0)
                sum_terms(1)
                shift(1, MV, RSTD1, NMR1, "1")
                guard(0, 0)
                guard(0, 1)
                second_norm(1)
                reduce_args(2)
                reduce_args_on(2)

            def route(i):
                choose(i)
                place(i)

            def back(i, with_front, with_tok, with_route):
                if with_tok:
                    sum_terms(i + 2)
                if with_route:
                    choose(i - 1)
                if with_tok:
                    shift(i + 2, MV, RSTD1, NMR1, "1")
                if with_route:
                    place(i - 1)
                if with_front:
                    head_norm(i + 1)
                attended(i, 0)
                attended(i, 1)
                if further(i):
                    reduce_args(i + 3)
                if with_tok:
                    second_norm(i + 2)
                if with_front:
                    guard(i + 1, 0)
                residual(i)
                shift(i, MV3, RSTD3, NMR3, "3")
                if with_front:
                    guard(i + 1, 1)
                if further(i):
                    reduce_args_on(i + 3)
                experts_in(i)

            phase_a(start, dve, back, route)

            steps = [0]

            def planned(ins):
                steps[0] += 1
                ins.then_inc(sem("plan"), 1)
                dve.wait_ge(sem("plan"), steps[0])

            dve.wait_ge(sem("total"), NSEQ + 1)
            big, big2 = (shared[:, 512 * k:512 * k + NBLK * NE].rearrange("p (j e) -> p j e", e=NE) for k in range(2))
            nb, cum, ones = (cols(plan, a, NE) for a in (16, 32, 48))
            nth, ej, before, within, length, late = (cols(plan, 112 + 32 * a, NBLK) for a in range(6))
            over_k = shared[:, 1024:1024 + NE * SPLIT].rearrange("p (e k) -> p e k", k=SPLIT)

            def over(v):
                return v.unsqueeze(1).broadcast_to([P, NBLK, NE])

            planned(V.memset(ones, 1.0))
            planned(V.scalar_tensor_tensor(over_k, total[:, :].unsqueeze(2).broadcast_to([P, NE, SPLIT]), float(P),
                                           list_edge[:, :].unsqueeze(1).broadcast_to([P, NE, SPLIT]), ALU.add, ALU.is_gt))
            planned(V.tensor_reduce(nb, over_k, AX, ALU.add))
            planned(V.tensor_tensor_scan(cum, ones, nb, 0.0, ALU.mult, ALU.add))
            planned(V.tensor_scalar(nth, blk_idx[:, :], 1.0, cum[:, NE - 1:NE], ALU.add, ALU.min))
            planned(V.tensor_tensor(big, over(cum), nth.unsqueeze(2).broadcast_to([P, NBLK, NE]), ALU.is_lt))
            planned(V.tensor_reduce(ej, big, AX, ALU.add))
            planned(V.tensor_scalar(blk_col[:, :], ej, float(WCOL), None, ALU.mult))
            V.tensor_copy(cols(plan, 399, 1), ones[:, 0:1]).then_inc(sem("blk_col"), 1)
            planned(V.tensor_tensor(big2, big, over(nb), ALU.mult))
            planned(V.tensor_reduce(before, big2, AX, ALU.add))
            planned(V.scalar_tensor_tensor(within, nth, 1.0, before, ALU.subtract, ALU.subtract))
            planned(V.scalar_tensor_tensor(blk_list[:, :], ej, float(SPLIT), within, ALU.mult, ALU.add))
            dve.wait_ge(sem("tokens"), 16)

            def pick_rows(q, k0, us):
                for u in us:
                    j = 2 * q + u
                    at = dve.value_load(blk_list[0:1, bass.ds(j, 1)], min_val=0, max_val=NLISTS - 1)
                    if not isinstance(q, int) or q >= 2:
                        dve.wait_ge(sem(f"rows{k0 + u}"), 8 * (q - k0 // 2))
                    V.tensor_copy(gidx[k0 + u][:, :], tokens[:, bass.ds(at, 1)]).then_inc(sem("gidx"), 1)

            def take_wi(q, us):
                for u in us:
                    at = dve.value_load(blk_col[0:1, bass.ds(2 * q + u, 1)], min_val=0, max_val=(NE - 1) * WCOL)
                    freed(dve, sem("b_hid"), 2 * q + u - 1 if not isinstance(q, int) or q else 0)
                    V.tensor_copy(wi_now[u][0:HALF, :], weights[0:HALF, bass.ds(at, 2 * FF)]).then_inc(sem("wi_now"), 1)

            def blocks(q, k0, us, ahead):
                pick_rows(q + 2, k0, ahead)
                take_wi(q + 1, next_blocks(q))
                for u in us:
                    j = 2 * q + u
                    at = dve.value_load(blk_list[0:1, bass.ds(j, 1)], min_val=0, max_val=NLISTS - 1)
                    freed(dve, sem(f"scattered{u}"), 16 * q)
                    V.tensor_tensor(oidx[u][:, :], tokens[:, bass.ds(at, 1)], blk_pen[:, bass.ds(j, 1)], ALU.add).then_inc(sem("oidx"), 1)
                    dve.wait_ge(sem("b_y"), j + 1)
                    dve.wait_ge(sem("oidx"), j + 1)
                    g = grow[k0 + u]
                    V.scalar_tensor_tensor(res[u], psum[u][:, 3, 0:D], g[:, 2 * D:2 * D + 1], g[:, D:2 * D],
                                           ALU.mult, ALU.add).then_inc(sem("res"), 1)

            pick_rows(0, 0, (0, 1))
            pick_rows(1, 2, (0, 1))
            dve.wait_ge(sem("weights"), 32 * NE)
            dve.wait_ge(sem("out_plain"), 32 * NSEQ)
            take_wi(0, (0, 1))
            planned(V.tensor_tensor(big, over(expert_iota[:, :]), ej.unsqueeze(2).broadcast_to([P, NBLK, NE]), ALU.is_equal))
            planned(V.tensor_tensor(big2, big, over(total[:, :]), ALU.mult))
            planned(V.tensor_reduce(length, big2, AX, ALU.add))
            planned(V.tensor_scalar(within, within, float(P), token_iota[:, 0:1], ALU.mult, ALU.add))
            planned(V.tensor_tensor(within, within, length, ALU.is_ge))
            planned(V.tensor_tensor(late, blk_idx[:, :], nth, ALU.is_ge))
            planned(V.tensor_tensor(within, within, late, ALU.add))
            planned(V.tensor_scalar(blk_pen[:, :], within, BIG, None, ALU.mult))
            V.tensor_copy(cols(plan, 398, 1), ones[:, 0:1]).then_inc(sem("planned"), 1)
            phase_b(dve, blocks)

        @block.tensor
        def _(pe):
            T = nc.tensor

            def halves(dst, src, done):
                T.transpose(dst(0), src[:, 0:HALF], ident[:, :])
                T.transpose(dst(1), src[:, HALF:D], ident[:, :]).then_inc(sem(done), 1)

            def over_d(dst, xt, w, start, width, bias):
                k1 = HALF + 1 if bias else HALF
                T.matmul(dst, xt[0:HALF, 0:P], w[0:HALF, 0, start:start + width], start=True, stop=False)
                return T.matmul(dst, xt[0:k1, P:2 * P], w[0:k1, 1, start:start + width], start=False, stop=True)

            def k_pad(u):
                return qk_pad[u][:, HEADS * HPAD:]

            def turn_x(i, u):
                pe.wait_ge(sem("xn"), 2 * i + u + 1)
                freed(pe, sem("probs"), 2 * i + u - 1)
                halves(lambda k: psum_s[u][0:HALF, 2, k * P:(k + 1) * P], xn[u], "p_xT")

            def qkv(i, u):
                pe.wait_ge(sem("xT"), 2 * i + u + 1)
                over_d(psum_s[u][:, 0, 0:2 * D], xT[u], wqkv, 0, 2 * D, True)
                over_d(psum_s[u][:, 1, 0:D], xT[u], wqkv, 2 * D, D, True).then_inc(sem("p_qkv"), 1)

            def turn_qk(i, u):
                n = 2 * i + u
                pe.wait_ge(sem("qk"), n + 1)
                for c in range(CHUNKS):
                    last = T.transpose(psum_s[u][0:GW, 2, c * P:(c + 1) * P], k_pad(u)[:, c * GW:(c + 1) * GW], ident[:, :])
                last.then_inc(sem("p_kT"), 1)
                pe.wait_ge(sem("v"), n + 1)
                for c in range(CHUNKS):
                    last = T.transpose(psum_s[u][0:GW, 1, c * P:(c + 1) * P], qk_pad[u][:, c * GW:(c + 1) * GW], ident[:, :])
                last.then_inc(sem("p_qT0"), 1)

            def guard_scores(i, u):
                n = 2 * i + u
                pe.wait_ge(sem("qT16"), n + 1)
                pe.wait_ge(sem("kT16"), n + 1)
                pe.wait_ge(sem("qT"), n + 1)
                for h in range(HEADS):
                    c, g = divmod(h, GROUPS)
                    rows_ = slice(g * HPAD, g * HPAD + HD)
                    last = T.matmul(psum_s[u][:, g, c * P:(c + 1) * P], qT16[u][rows_, c * P:(c + 1) * P],
                                    kT16[u][rows_, c * P:(c + 1) * P], start=True, stop=True)
                last.then_inc(sem("p_guard"), 1)

            def turn_guard(i, u):
                pe.wait_ge(sem("guard"), 2 * i + u + 1)
                freed(pe, sem("h1"), 2 * i + u - 1 if not isinstance(i, int) or i else 0)
                T.matmul(psum_m[u][0:HEADS, 2 * P:3 * P], guard16[u][:, :], identb[:, 2, :], start=True, stop=True).then_inc(sem("p_guardT"), 1)

            def scores_T(i, u):
                pe.wait_ge(sem("guard"), 2 * i + u + 1)
                flat = psum_s[u].rearrange("p b c -> p (b c)")
                for c in range(CHUNKS):
                    at, end = c * GROUPS * P, (c + 1) * GROUPS * P
                    while at < end:
                        to = min(end, (at // 512 + 1) * 512)
                        T.matmul(flat[:, at:to], kT[u][0:GW, c * P:(c + 1) * P], qT[u][0:GW, at:to], start=at % 512 == 0, stop=False)
                        at = to

            def subtract_guard(i, u):
                pe.wait_ge(sem("guardT"), 2 * i + u + 1)
                flat = psum_s[u].rearrange("p b c -> p (b c)")
                for h in range(HEADS):
                    last = T.matmul(flat[:, h * P:(h + 1) * P], identb[0:HEADS, 2, h:h + 1].broadcast_to([HEADS, P]),
                                    guardT[u][:, :], start=False, stop=h % 4 == 3)
                last.then_inc(sem("p_sT"), 1)

            def attend(i, u):
                pe.wait_ge(sem("probs"), 2 * i + u + 1)
                freed(pe, sem("total"), 2 * i + 1 if not isinstance(i, int) or i else 0)
                for h in range(HEADS):
                    c, g = divmod(h, P // HPAD)
                    last = T.matmul(psum_m[u][g * HPAD:(g + 1) * HPAD, c * P:(c + 1) * P], v_aug[u][:, h * HPAD:(h + 1) * HPAD],
                                    probsT[u][:, h * P:(h + 1) * P], start=True, stop=True)
                last.then_inc(sem("p_pv"), 1)

            def turn_pv(i, u):
                pe.wait_ge(sem("pvT"), 2 * i + u + 1)
                for c in range(HEADS * HPAD // P):
                    last = T.transpose(psum_m[u][:, c * P:(c + 1) * P], pvT[u][:, c * P:(c + 1) * P], ident[:, :])
                last.then_inc(sem("p_pvback"), 1)

            def turn_o(i, u):
                pe.wait_ge(sem("o"), 2 * i + u + 1)
                halves(lambda k: psum_m[u][0:HALF, (2 + k) * P:(3 + k) * P], o_sb[u], "p_oT")

            def project(i, u):
                pe.wait_ge(sem("oT"), 2 * i + u + 1)
                over_d(psum_m[u][:, 0:D], oT[u], wproj, 0, D, True).then_inc(sem("p_y"), 1)

            def turn_n(i, u):
                pe.wait_ge(sem("normed"), 2 * i + u + 1)
                halves(lambda k: psum_m[u][0:HALF, (2 + k) * P:(3 + k) * P], row[u], "p_nT")

            def logits(i, u):
                pe.wait_ge(sem("nT"), 2 * i + u + 1)
                over_d(psum_m[u][:, LG:LG + NE], nT[u], wrout, 0, NE, False).then_inc(sem("p_logit"), 1)

            def places(i, u):
                n = 2 * i + u
                pe.wait_ge(sem("oneh16"), n + 1)
                pe.wait_ge(sem("zsum"), n + 1)
                T.matmul(psum_m[u][:, LG + NE:LG + 2 * NE], identb[:, 0, :], onehot16[u][:, :], start=True, stop=True)
                T.matmul(psum_m[u][:, LG + 2 * NE:LG + 3 * NE], identb[:, 1, :], onehot16[u][:, :], start=True, stop=True).then_inc(sem("p_prio"), 1)

            def start():
                for stage in (turn_x, qkv, turn_qk, guard_scores):
                    for u in range(2):
                        stage(0, u)
                turn_guard(0, 0)

            def route(i):
                for stage in (turn_n, logits, places):
                    for u in range(2):
                        stage(i, u)

            def back(i, with_front, with_tok, with_route):
                scores_T(i, 0)
                subtract_guard(i, 0)
                turn_guard(i, 1)
                if with_route:
                    turn_n(i - 1, 0)
                scores_T(i, 1)
                if with_front:
                    turn_x(i + 1, 0)
                subtract_guard(i, 1)
                if with_route:
                    turn_n(i - 1, 1)
                if with_front:
                    qkv(i + 1, 0)
                    turn_x(i + 1, 1)
                if with_route:
                    logits(i - 1, 0)
                    logits(i - 1, 1)
                if with_front:
                    qkv(i + 1, 1)
                if with_route:
                    places(i - 1, 0)
                    places(i - 1, 1)
                attend(i, 0)
                attend(i, 1)
                turn_pv(i, 0)
                turn_pv(i, 1)
                if with_front:
                    turn_qk(i + 1, 0)
                    turn_qk(i + 1, 1)
                turn_o(i, 0)
                turn_o(i, 1)
                if with_front:
                    guard_scores(i + 1, 0)
                project(i, 0)
                project(i, 1)
                if with_front:
                    guard_scores(i + 1, 1)
                    turn_guard(i + 1, 0)

            pe.wait_ge(sem("ident"), 7)
            pe.wait_ge(sem("ones"), 8)
            pe.wait_ge(sem("const"), 16 * N_CONST)
            phase_a(start, pe, back, route)

            pe.wait_ge(sem("blk_col"), 1)

            def turn_rows(q, k0, us, u):
                if u in us:
                    pe.wait_ge(sem(f"rows{k0 + u}"), 8 * (q - k0 // 2) + 16)
                    halves(lambda k: psum[u][0:HALF, 2, k * P:(k + 1) * P], grow[k0 + u], "b_gT")

            def blocks(q, k0, us, ahead):
                at = [pe.value_load(blk_col[0:1, bass.ds(2 * q + u, 1)], min_val=0, max_val=(NE - 1) * WCOL) for u in us]
                after = next_blocks(q)
                for u in us:
                    pe.wait_ge(sem("gT"), 2 * q + u + 1)
                    pe.wait_ge(sem("wi_now"), 2 * q + u + 1)
                    freed(pe, sem("hidT"), 2 * q + u - 1 if not isinstance(q, int) or q else 0)
                    for c in range(FC):
                        for k in range(2):
                            w0 = k * FF + c * P
                            last = T.matmul(psum[u][:, c // 4, (c % 4) * P:(c % 4 + 1) * P], wi_now[u][0:HALF, w0:w0 + P],
                                            gT[u][0:HALF, k * P:(k + 1) * P], start=k == 0, stop=k == 1)
                    last.then_inc(sem("b_hid"), 1)
                for u in range(2):
                    turn_rows(q + 1, 2 - k0, after, u)
                for u in us:
                    pe.wait_ge(sem("hidT"), 2 * q + u + 1)
                    freed(pe, sem("res"), 2 * q)
                    for c in range(FC):
                        last = T.matmul(psum[u][:, 3, 0:D], hidT[u][:, c * P:(c + 1) * P],
                                        weights[:, bass.ds(at[u] + 2 * FF + c * D, D)], start=c == 0, stop=c == FC - 1)
                    last.then_inc(sem("b_y"), 1)

            turn_rows(0, 0, (0, 1), 0)
            turn_rows(0, 0, (0, 1), 1)
            pe.wait_ge(sem("weights"), 32 * NE)
            phase_b(pe, blocks)


def kernel(**inputs):
    import numpy as np
    import concourse.bacc as bacc
    from concourse.bass_utils import run_bass_kernel_spmd

    a = {k: np.asarray(v) for k, v in inputs.items()}
    tok = "L0_tok_"
    ids = [a["x"], a["itok_BS_0_9999"], a["itok_BS_0_2047"], a["itok_BS_0_15"], a["itok_BS_0_3"]]
    qk_norm = np.zeros((GROUPS, HPAD, 2), a["L0_attn_q_norm_w"].dtype)
    qk_norm[:, :HD, 0] = a["L0_attn_q_norm_w"]
    qk_norm[:, :HD, 1] = a["L0_attn_k_norm_w"]
    arrays = {
        "ids": np.stack([x.T for x in ids]),
        "taus": np.stack([a["fside_BS_age_tau"].T, a["fside_BS_delays_tau"].T]),
        "word_table": a[tok + "word_table"],
        "npi_table": a[tok + "npi_table"],
        "posi_table": a[tok + "posi_table"],
        "modal_table": a[tok + "modalities_table"],
        "seg_table": a[tok + "seg_table"],
        "vectors": np.concatenate([a[tok + x].reshape(-1) for x in (
            "age_w", "age_w0", "delay_w", "delay_w0", "age_b", "age_b0", "delay_b", "delay_b0", "ln_gamma", "ln_beta",
        )] + [a["L0_ffn_ln_w"]]).reshape(7, D),
        "qkv_wT": np.concatenate([a["L0_attn_qkv_w"].T, a["L0_attn_qkv_b"][None]]),
        "proj_wT": np.concatenate([a["L0_attn_proj_w"].T, a["L0_attn_proj_b"][None]]),
        "qk_norm": qk_norm.reshape(GW, 2),
        "w_router": a["L0_ffn_w_router"],
        "wi": a["L0_ffn_wi"],
        "wo": a["L0_ffn_wo"],
    }
    arrays = {"in_" + k: np.ascontiguousarray(v) for k, v in arrays.items()}

    nc = bacc.Bacc("TRN2", target_bir_lowering=False, num_devices=1)
    t = {k[3:]: nc.dram_tensor(k, v.shape, mybir.dt.from_np(v.dtype), kind="ExternalInput").ap()
         for k, v in arrays.items()}
    out = nc.dram_tensor("tower_out", [NSEQ * P, D], F32, kind="ExternalOutput").ap()
    tower_kernel(nc, t, out)
    r = run_bass_kernel_spmd(nc, [arrays], core_ids=[0])
    return r.results[0]["tower_out"].reshape(NSEQ, P, D)
```
